# Optimizing a Trainium2 kernel written in Bass

```python
import numpy as np
import jax
import jax.numpy as jnp

def _softmax(x, axis=-1):
    return jax.nn.softmax(x, axis=axis)
def _gelu(x):
    return jax.nn.gelu(x, approximate=True)
def _silu(x):
    return jax.nn.silu(x)
def _sigmoid(x):
    return jax.nn.sigmoid(x)
def _layernorm(x, axis=-1, eps=1e-5):
    m = jnp.mean(x, axis=axis, keepdims=True)
    v = jnp.var(x, axis=axis, keepdims=True)
    return (x - m) / jnp.sqrt(v + eps)
def _scatter_add(tgt, idx, src, axis=0):
    return tgt.at[idx].add(src)
def _segment_sum(src, seg, n):
    return jax.ops.segment_sum(src, seg, n)

kernel_name = 'mk_conv_preact_d4_conv_nhwc128_3249d6'

def setup_inputs(seed: int = 0):
    np.random.seed(seed)
    _w = jnp.asarray
    def _rec_inputs():
        import jax
        import jax.numpy as jnp
        _gk = jax.random.key(seed)
        x = 7.22e-05 + 1 * jax.random.normal(jax.random.fold_in(_gk, 1), (4, 128, 128, 128), jnp.float32)
        return x
    x = _rec_inputs()
    def _L0_conv_setup():
        import jax, jax.numpy as jnp
        import numpy as np
        EPS = 1e-06

        def kernel_to_freq_2d(kernel, H, W):
            C, kh, kw = kernel.shape
            th = (jnp.arange(kh) - kh // 2) % H
            tw = (jnp.arange(kw) - kw // 2) % W
            TH, TW = jnp.meshgrid(th, tw, indexing='ij')
            padded = jnp.zeros((C, H, W), dtype=kernel.dtype).at[:, TH, TW].set(kernel)
            return jnp.fft.fft2(padded, axes=(1, 2))

        def heinsen_scan_log(log_coeffs, log_values):

            def op(left, right):
                la, lb = left
                ra, rb = right
                return (la + ra, jnp.logaddexp(ra + lb, rb))
            _, log_h = jax.lax.associative_scan(op, (log_coeffs, log_values), axis=0)
            return log_h
        key = jax.random.key(seed)
        ks = jax.random.split(key, 7)
        B, H, W, C, k = (4, 128, 128, 128, 7)
        fan_in = k * k
        x = jax.random.normal(ks[0], (B, H, W, C), dtype=jnp.float32)
        A_kernel = jax.random.normal(ks[1], (C, k, k), dtype=jnp.float32) / np.sqrt(fan_in)
        B_kernel = jax.random.normal(ks[2], (C, k, k), dtype=jnp.float32) / np.sqrt(fan_in)
        gate_A_kernel = jax.random.normal(ks[3], (C, k, k), dtype=jnp.float32) * 0.02
        gate_B_kernel = jax.random.normal(ks[4], (C, k, k), dtype=jnp.float32) * 0.02
        W_out = jax.random.normal(ks[5], (C, C), dtype=jnp.float32) / np.sqrt(C)
        b_out = jnp.zeros((C,), dtype=jnp.float32)
        return dict(x=x, A_kernel=A_kernel, B_kernel=B_kernel, gate_A_kernel=gate_A_kernel, gate_B_kernel=gate_B_kernel, W_out=W_out, b_out=b_out, T=8)
    _L0_conv_all = _L0_conv_setup()
    _L0_conv_in = {k: v for k, v in _L0_conv_all.items() if k in ('A_kernel', 'B_kernel', 'gate_A_kernel', 'gate_B_kernel', 'W_out', 'b_out', )}
    del _L0_conv_all

    def _L1_conv_setup():
        import jax, jax.numpy as jnp
        import numpy as np
        EPS = 1e-05

        def _ln(x, g, b):
            m = jnp.mean(x, axis=-1, keepdims=True)
            v = jnp.var(x, axis=-1, keepdims=True)
            return (x - m) / jnp.sqrt(v + EPS) * g + b
        key = jax.random.key(seed)
        ks = jax.random.split(key, 16)
        B, N, CZ, C = (1, 512, 128, 16)
        s_cz = 1.0 / np.sqrt(CZ)
        s_c = 1.0 / np.sqrt(C)

        def lin(k, fan_in, shape):
            return jax.random.uniform(k, shape, jnp.float32, -1.0, 1.0) / np.sqrt(fan_in)
        return {'x': jax.random.normal(ks[0], (B, N, N, CZ), jnp.float32), 'Wa1': lin(ks[1], CZ, (CZ, C)), 'ba1': lin(ks[2], CZ, (C,)), 'Wa2': lin(ks[3], CZ, (CZ, C)), 'ba2': lin(ks[4], CZ, (C,)), 'Wb1': lin(ks[5], CZ, (CZ, C)), 'bb1': lin(ks[6], CZ, (C,)), 'Wb2': lin(ks[7], CZ, (CZ, C)), 'bb2': lin(ks[8], CZ, (C,)), 'ln2_g': jnp.ones((C,), jnp.float32), 'ln2_b': jnp.zeros((C,), jnp.float32), 'Wg': lin(ks[9], CZ, (CZ, CZ)), 'bg': lin(ks[10], CZ, (CZ,)), 'Wz': lin(ks[11], C, (C, CZ)), 'bz': lin(ks[12], C, (CZ,))}
    _L1_conv_all = _L1_conv_setup()
    _L1_conv_in = {k: v for k, v in _L1_conv_all.items() if k in ('Wa1', 'ba1', 'Wa2', 'ba2', 'Wb1', 'bb1', 'Wb2', 'bb2', 'ln2_g', 'ln2_b', 'Wg', 'bg', 'Wz', 'bz', )}
    del _L1_conv_all

    def _L2_conv_setup():
        import jax, jax.numpy as jnp
        import numpy as np
        B, T, N, F, H = (16, 128, 256, 128, 128)

        def _gclstm(x, Wix, Wim, Wfx, Wfm, Wcx, Wcm, Wox, Wom, bi, bf, bc, bo):
            b_, t_, n_, f_ = x.shape
            h_ = Wix.shape[1]
            Wx = jnp.concatenate([Wix, Wfx, Wox, Wcx], axis=1)
            Wm = jnp.concatenate([Wim, Wfm, Wom, Wcm], axis=1)
            bias = jnp.concatenate([bi, bf, bo, bc], axis=1)
            xw = jnp.einsum('btnf,fg->tbng', x, Wx) + bias

            def step(carry, xw_t):
                h, c = carry
                z = xw_t + h @ Wm
                zi, zf, zo, zg = jnp.split(z, 4, axis=-1)
                i = jax.nn.sigmoid(zi)
                f = jax.nn.sigmoid(zf)
                o = jax.nn.sigmoid(zo)
                g = jnp.tanh(zg)
                c_new = f * c + i * g
                h_new = o * jnp.tanh(c_new)
                return ((h_new, c_new), h_new)
            init = (jnp.zeros((b_, n_, h_), x.dtype), jnp.zeros((b_, n_, h_), x.dtype))
            _, states = jax.lax.scan(step, init, xw)
            return states.reshape(b_, t_, n_, h_)
        key = jax.random.key(seed)
        ks = jax.random.split(key, 9)
        s_x = (2.0 / (F + H)) ** 0.5
        s_m = (2.0 / (H + H)) ** 0.5
        return {'x': jax.random.normal(ks[0], (B, T, N, F), dtype=jnp.float32), 'Wix': jax.random.normal(ks[1], (F, H), dtype=jnp.float32) * s_x, 'Wim': jax.random.normal(ks[2], (H, H), dtype=jnp.float32) * s_m, 'Wfx': jax.random.normal(ks[3], (F, H), dtype=jnp.float32) * s_x, 'Wfm': jax.random.normal(ks[4], (H, H), dtype=jnp.float32) * s_m, 'Wcx': jax.random.normal(ks[5], (F, H), dtype=jnp.float32) * s_x, 'Wcm': jax.random.normal(ks[6], (H, H), dtype=jnp.float32) * s_m, 'Wox': jax.random.normal(ks[7], (F, H), dtype=jnp.float32) * s_x, 'Wom': jax.random.normal(ks[8], (H, H), dtype=jnp.float32) * s_m, 'bi': jnp.zeros((1, H), dtype=jnp.float32), 'bf': jnp.zeros((1, H), dtype=jnp.float32), 'bc': jnp.zeros((1, H), dtype=jnp.float32), 'bo': jnp.zeros((1, H), dtype=jnp.float32)}
    _L2_conv_all = _L2_conv_setup()
    _L2_conv_in = {k: v for k, v in _L2_conv_all.items() if k in ('Wix', 'Wim', 'Wfx', 'Wfm', 'Wcx', 'Wcm', 'Wox', 'Wom', 'bi', 'bf', 'bc', 'bo', )}
    del _L2_conv_all

    def _L3_conv_setup():
        import jax, jax.numpy as jnp
        import numpy as np
        B, H, W_DIM, C = (8, 128, 256, 128)
        K = 9

        def conv1d_same(y, W):
            return jax.lax.conv_general_dilated(y, W, window_strides=(1,), padding='SAME', dimension_numbers=('NWC', 'WIO', 'NWC'))
        key = jax.random.key(seed)
        kx, kw = jax.random.split(key)
        x = jax.random.normal(kx, (B, H, W_DIM, C), dtype=jnp.float32)
        W = jax.random.normal(kw, (K, C, C), dtype=jnp.float32) * 0.02
        return {'x': x, 'W': W}
    _L3_conv_all = _L3_conv_setup()
    _L3_conv_in = {k: v for k, v in _L3_conv_all.items() if k in ('W', )}
    del _L3_conv_all

    return {
        "x": x,
        "L0_conv_A_kernel": _L0_conv_in["A_kernel"],
        "L0_conv_B_kernel": _L0_conv_in["B_kernel"],
        "L0_conv_gate_A_kernel": _L0_conv_in["gate_A_kernel"],
        "L0_conv_gate_B_kernel": _L0_conv_in["gate_B_kernel"],
        "L0_conv_W_out": _L0_conv_in["W_out"],
        "L0_conv_b_out": _L0_conv_in["b_out"],
        "L1_conv_Wa1": _L1_conv_in["Wa1"],
        "L1_conv_ba1": _L1_conv_in["ba1"],
        "L1_conv_Wa2": _L1_conv_in["Wa2"],
        "L1_conv_ba2": _L1_conv_in["ba2"],
        "L1_conv_Wb1": _L1_conv_in["Wb1"],
        "L1_conv_bb1": _L1_conv_in["bb1"],
        "L1_conv_Wb2": _L1_conv_in["Wb2"],
        "L1_conv_bb2": _L1_conv_in["bb2"],
        "L1_conv_ln2_g": _L1_conv_in["ln2_g"],
        "L1_conv_ln2_b": _L1_conv_in["ln2_b"],
        "L1_conv_Wg": _L1_conv_in["Wg"],
        "L1_conv_bg": _L1_conv_in["bg"],
        "L1_conv_Wz": _L1_conv_in["Wz"],
        "L1_conv_bz": _L1_conv_in["bz"],
        "L2_conv_Wix": _L2_conv_in["Wix"],
        "L2_conv_Wim": _L2_conv_in["Wim"],
        "L2_conv_Wfx": _L2_conv_in["Wfx"],
        "L2_conv_Wfm": _L2_conv_in["Wfm"],
        "L2_conv_Wcx": _L2_conv_in["Wcx"],
        "L2_conv_Wcm": _L2_conv_in["Wcm"],
        "L2_conv_Wox": _L2_conv_in["Wox"],
        "L2_conv_Wom": _L2_conv_in["Wom"],
        "L2_conv_bi": _L2_conv_in["bi"],
        "L2_conv_bf": _L2_conv_in["bf"],
        "L2_conv_bc": _L2_conv_in["bc"],
        "L2_conv_bo": _L2_conv_in["bo"],
        "L3_conv_W": _L3_conv_in["W"],
    }

def reference(x, L0_conv_A_kernel, L0_conv_B_kernel, L0_conv_gate_A_kernel, L0_conv_gate_B_kernel, L0_conv_W_out, L0_conv_b_out, L1_conv_Wa1, L1_conv_ba1, L1_conv_Wa2, L1_conv_ba2, L1_conv_Wb1, L1_conv_bb1, L1_conv_Wb2, L1_conv_bb2, L1_conv_ln2_g, L1_conv_ln2_b, L1_conv_Wg, L1_conv_bg, L1_conv_Wz, L1_conv_bz, L2_conv_Wix, L2_conv_Wim, L2_conv_Wfx, L2_conv_Wfm, L2_conv_Wcx, L2_conv_Wcm, L2_conv_Wox, L2_conv_Wom, L2_conv_bi, L2_conv_bf, L2_conv_bc, L2_conv_bo, L3_conv_W):
    import jax
    import jax.numpy as jnp
    def _L0_conv_ref(x, A_kernel, B_kernel, gate_A_kernel, gate_B_kernel, W_out, b_out, T):
        import jax, jax.numpy as jnp
        import numpy as np
        EPS = 1e-06

        def kernel_to_freq_2d(kernel, H, W):
            C, kh, kw = kernel.shape
            th = (jnp.arange(kh) - kh // 2) % H
            tw = (jnp.arange(kw) - kw // 2) % W
            TH, TW = jnp.meshgrid(th, tw, indexing='ij')
            padded = jnp.zeros((C, H, W), dtype=kernel.dtype).at[:, TH, TW].set(kernel)
            return jnp.fft.fft2(padded, axes=(1, 2))

        def heinsen_scan_log(log_coeffs, log_values):

            def op(left, right):
                la, lb = left
                ra, rb = right
                return (la + ra, jnp.logaddexp(ra + lb, rb))
            _, log_h = jax.lax.associative_scan(op, (log_coeffs, log_values), axis=0)
            return log_h
        B, H, W, C = x.shape

        def ifft_real(z_bhwc):
            return jnp.fft.ifft2(z_bhwc.transpose(0, 3, 1, 2), axes=(2, 3)).real.transpose(0, 2, 3, 1)
        A_f = kernel_to_freq_2d(A_kernel, H, W).transpose(1, 2, 0)
        B_f = kernel_to_freq_2d(B_kernel, H, W).transpose(1, 2, 0)
        gA_f = kernel_to_freq_2d(gate_A_kernel, H, W).transpose(1, 2, 0)
        gB_f = kernel_to_freq_2d(gate_B_kernel, H, W).transpose(1, 2, 0)
        x_f = jnp.fft.fft2(x.transpose(0, 3, 1, 2), axes=(2, 3)).transpose(0, 2, 3, 1)
        gate_A = jax.nn.sigmoid(ifft_real(gA_f[None] * x_f))
        gate_B = jax.nn.sigmoid(ifft_real(gB_f[None] * x_f))
        a_spatial = ifft_real(jnp.broadcast_to(A_f[None], (B, H, W, C)))
        b_spatial = ifft_real(B_f[None] * x_f)
        a_t = a_spatial * gate_A
        b_t = b_spatial * gate_B
        gate_seq = jnp.tile(a_t[None], (T, 1, 1, 1, 1))
        h_tilde_seq = jnp.tile(b_t[None], (T, 1, 1, 1, 1))
        log_z = -jax.nn.softplus(-gate_seq)
        log_coeffs = -jax.nn.softplus(gate_seq)
        log_values = log_z + jnp.log(jax.nn.softplus(h_tilde_seq) + EPS)
        log_h = heinsen_scan_log(log_coeffs, log_values)
        h_final = jnp.exp(log_h[-1])
        return h_final @ W_out + b_out

    def _L1_conv_ref(x, Wa1, ba1, Wa2, ba2, Wb1, bb1, Wb2, bb2, ln2_g, ln2_b, Wg, bg, Wz, bz):
        import jax, jax.numpy as jnp
        import numpy as np
        EPS = 1e-05

        def _ln(x, g, b):
            m = jnp.mean(x, axis=-1, keepdims=True)
            v = jnp.var(x, axis=-1, keepdims=True)
            return (x - m) / jnp.sqrt(v + EPS) * g + b
        direction = 'outgoing'
        a = jax.nn.sigmoid((x @ Wa1 + ba1) * (x @ Wa2 + ba2))
        b = jax.nn.sigmoid((x @ Wb1 + bb1) * (x @ Wb2 + bb2))
        if direction == 'incoming':
            a = jnp.swapaxes(a, 1, 2)
            b = jnp.swapaxes(b, 1, 2)
        g = jax.nn.sigmoid(x @ Wg + bg)
        z = jnp.einsum('bikc,bkjc->bijc', a, b)
        return g * (_ln(z, ln2_g, ln2_b) @ Wz + bz)

    def _L2_conv_ref(x, Wix, Wim, Wfx, Wfm, Wcx, Wcm, Wox, Wom, bi, bf, bc, bo):
        import jax, jax.numpy as jnp
        import numpy as np
        B, T, N, F, H = (16, 128, 256, 128, 128)

        def _gclstm(x, Wix, Wim, Wfx, Wfm, Wcx, Wcm, Wox, Wom, bi, bf, bc, bo):
            b_, t_, n_, f_ = x.shape
            h_ = Wix.shape[1]
            Wx = jnp.concatenate([Wix, Wfx, Wox, Wcx], axis=1)
            Wm = jnp.concatenate([Wim, Wfm, Wom, Wcm], axis=1)
            bias = jnp.concatenate([bi, bf, bo, bc], axis=1)
            xw = jnp.einsum('btnf,fg->tbng', x, Wx) + bias

            def step(carry, xw_t):
                h, c = carry
                z = xw_t + h @ Wm
                zi, zf, zo, zg = jnp.split(z, 4, axis=-1)
                i = jax.nn.sigmoid(zi)
                f = jax.nn.sigmoid(zf)
                o = jax.nn.sigmoid(zo)
                g = jnp.tanh(zg)
                c_new = f * c + i * g
                h_new = o * jnp.tanh(c_new)
                return ((h_new, c_new), h_new)
            init = (jnp.zeros((b_, n_, h_), x.dtype), jnp.zeros((b_, n_, h_), x.dtype))
            _, states = jax.lax.scan(step, init, xw)
            return states.reshape(b_, t_, n_, h_)
        return _gclstm(x, Wix, Wim, Wfx, Wfm, Wcx, Wcm, Wox, Wom, bi, bf, bc, bo)

    def _L3_conv_ref(x, W):
        import jax, jax.numpy as jnp
        import numpy as np
        B, H, W_DIM, C = (8, 128, 256, 128)
        K = 9

        def conv1d_same(y, W):
            return jax.lax.conv_general_dilated(y, W, window_strides=(1,), padding='SAME', dimension_numbers=('NWC', 'WIO', 'NWC'))
        rows = jnp.moveaxis(x, 1, 0)
        row0 = rows[0]

        def step(carry, row):
            new = row + jax.nn.relu(conv1d_same(carry, W))
            return (new, new)
        _, outs = jax.lax.scan(step, row0, rows[1:])
        out = jnp.concatenate([row0[None], outs], axis=0)
        return jnp.moveaxis(out, 0, 1)

    def _gn(v, G=32, eps=1e-5):
        B_, H_, W_, C_ = v.shape
        g = v.reshape(B_, H_, W_, G, C_ // G)
        m = jnp.mean(g, axis=(1, 2, 4), keepdims=True)
        s = jnp.var(g, axis=(1, 2, 4), keepdims=True)
        return ((g - m) / jnp.sqrt(s + eps)).reshape(v.shape)

    def _ln_c(v, eps=1e-6):
        m = jnp.mean(v, axis=-1, keepdims=True)
        s = jnp.var(v, axis=-1, keepdims=True)
        return (v - m) / jnp.sqrt(s + eps)

    def _ln_t(v, eps=1e-5):
        m = jnp.mean(v, axis=-1, keepdims=True)
        s = jnp.var(v, axis=-1, keepdims=True)
        return (v - m) / jnp.sqrt(s + eps)

    def _to_tokens(v):
        B_, H_, W_, C_ = v.shape
        return v.reshape(B_, H_ * W_, C_)
    def _from_tokens(t, like):
        return t.reshape(like.shape)

    x = x + _L0_conv_ref(_gn(x), L0_conv_A_kernel, L0_conv_B_kernel, L0_conv_gate_A_kernel, L0_conv_gate_B_kernel, L0_conv_W_out, L0_conv_b_out, 8)
    x = x + _L1_conv_ref(_gn(x), L1_conv_Wa1, L1_conv_ba1, L1_conv_Wa2, L1_conv_ba2, L1_conv_Wb1, L1_conv_bb1, L1_conv_Wb2, L1_conv_bb2, L1_conv_ln2_g, L1_conv_ln2_b, L1_conv_Wg, L1_conv_bg, L1_conv_Wz, L1_conv_bz)
    x = x + _L2_conv_ref(_gn(x), L2_conv_Wix, L2_conv_Wim, L2_conv_Wfx, L2_conv_Wfm, L2_conv_Wcx, L2_conv_Wcm, L2_conv_Wox, L2_conv_Wom, L2_conv_bi, L2_conv_bf, L2_conv_bc, L2_conv_bo)
    x = x + _L3_conv_ref(_gn(x), L3_conv_W)
    return x


_drawn_inputs = setup_inputs


def setup_inputs(seed=0):
    import zlib

    import numpy as np

    out = dict(_drawn_inputs(seed))
    spreads = {'L0_conv_b_out': (0.0, 0.1),
     'L1_conv_ln2_g': (1.0, 0.2),
     'L1_conv_ln2_b': (0.0, 0.376),
     'L2_conv_bi': (0.0, 0.8),
     'L2_conv_bf': (0.0, 0.8),
     'L2_conv_bc': (0.0, 0.295),
     'L2_conv_bo': (0.0, 0.8)}
    factors = {'L0_conv_A_kernel': 8.0,
     'L0_conv_gate_A_kernel': 8.0,
     'L0_conv_gate_B_kernel': 3.585,
     'L1_conv_ba1': 3.945,
     'L1_conv_bb2': 3.634,
     'L1_conv_bg': 8.0,
     'L2_conv_Wim': 4.071,
     'L2_conv_Wfm': 4.523,
     'L2_conv_Wom': 3.603}
    for name, (base, spread) in spreads.items():
        noise = np.random.default_rng([zlib.crc32(name.encode()), seed]).standard_normal(out[name].shape)
        drawn = base * np.exp(spread * noise) if base else spread * noise
        out[name] = jnp.asarray(drawn.astype(out[name].dtype))
    for name, factor in factors.items():
        out[name] = (out[name] * factor).astype(out[name].dtype)
    return out
```

```python
import concourse.bass as bass
import concourse.mybir as mybir
from contextlib import ExitStack

F32 = mybir.dt.float32
F16 = mybir.dt.float16
ALU = mybir.AluOpType
ACT = mybir.ActivationFunctionType
AX = mybir.AxisListType

B, H, W, C = 4, 128, 128, 128
P = 128
PLANE = H * W
TILE = 512
ROWS = TILE // W
TILES = PLANE // TILE
GROUP = 4
GN_EPS = 1e-5

SA = 64.0
SW = 64.0
DESCALE = 1.0 / (SA * SW)


class Names:

    def __init__(self, nc, stage):
        self.nc, self.stage, self.stack, self.sems = nc, stage, ExitStack(), []
        self.stack.callback(self.clear)

    def sb(self, name, shape, dt=F32):
        return self.stack.enter_context(self.nc.sbuf_tensor(f"{self.stage}_{name}", shape, dt))

    def ps(self, name, shape, dt=F32):
        return self.stack.enter_context(self.nc.psum_tensor(f"{self.stage}_{name}", shape, dt))

    def sem(self, name):
        self.sems.append(self.nc.alloc_semaphore(f"{self.stage}_{name}"))
        return self.sems[-1]

    def clear(self):
        if self.sems:
            self.nc.clear_and_free_semaphores(self.sems)
            self.nc.all_engine_barrier()


def group_matrix(nc, pool, zeros_done, g):
    nc.gpsimd.memset(g[:, :], 1.0 / GROUP).then_inc(zeros_done, 1)
    pool.wait_ge(zeros_done, 1)
    v = g[:, :].rearrange("c (q r) -> c q r", r=GROUP)
    nc.gpsimd.affine_select(out=v, in_=v, compare_op=ALU.is_ge, fill=0.0, base=0,
                            pattern=[[-GROUP, P // GROUP], [0, GROUP]], channel_multiplier=1).then_inc(zeros_done, 1)
    pool.wait_ge(zeros_done, 2)
    nc.gpsimd.affine_select(out=v, in_=v, compare_op=ALU.is_ge, fill=0.0, base=GROUP - 1,
                            pattern=[[GROUP, P // GROUP], [0, GROUP]], channel_multiplier=-1).then_inc(zeros_done, 1)


def group_norm_coefficients(nc, n, stats, coef, gain):
    own = Names(nc, n.stage)
    with own.stack:
        st = own.sb("gn_st", [C, B, TILES * 6])
        mv = own.sb("gn_mv", [C, B, 2])
        mom = own.sb("gn_mom", [C, 2, B])
        mg = own.sb("gn_mg", [C, 2, B])
        t = own.sb("gn_t", [C, 6, B])
        g = own.sb("gn_group", [C, C])
        pm = own.ps("gn_pm", [C, 512])
        loaded, group_ready, moments, averaged, var_ready, root_ready, step = (
            n.sem(f"gn_{x}") for x in ("loaded", "group_ready", "moments", "averaged", "var_ready", "root_ready", "step"))

        with nc.Block() as block:
            @block.sync
            def _(sp):
                sp.dma_start(st[:, :, :], stats).then_inc(loaded, 16)

            @block.gpsimd
            def _(pool):
                group_matrix(nc, pool, group_ready, g)

            @block.tensor
            def _(pe):
                pe.wait_ge(group_ready, 3)
                pe.wait_ge(moments, 1)
                nc.tensor.matmul(pm[:, 0:2 * B], g[:, :], mom[:, :, :].rearrange("c a b -> c (a b)"),
                                 start=True, stop=True).then_inc(averaged, 1)

            @block.scalar
            def _(act):
                act.wait_ge(var_ready, 1)
                nc.scalar.activation(t[:, 2, :], t[:, 1, :], ACT.Sqrt).then_inc(root_ready, 1)

            @block.vector
            def _(dve):
                done = [0]

                def link(ins):
                    done[0] += 1
                    ins.then_inc(step, 1)
                    dve.wait_ge(step, done[0])

                dve.wait_ge(loaded, 16)
                for b in range(B):
                    last = nc.vector.bn_aggr(mv[:, b, :], st[:, b, :])
                link(last)
                nc.vector.tensor_copy(mom[:, 0, :], mv[:, :, 0])
                link(nc.vector.tensor_tensor(t[:, 0, :], mv[:, :, 0], mv[:, :, 0], ALU.mult))
                nc.vector.tensor_tensor(mom[:, 1, :], t[:, 0, :], mv[:, :, 1], ALU.add).then_inc(moments, 1)
                dve.wait_ge(averaged, 1)
                rsqrt_and_shift(nc, link, lambda ins: ins.then_inc(var_ready, 1), lambda: dve.wait_ge(root_ready, 1),
                                pm[:, 0:B], pm[:, B:2 * B], mg, t,
                                coef[:, :, 0], coef[:, :, 1], gain, GN_EPS)


def rsqrt_and_shift(nc, link, to_root, from_root, mean_ps, second_ps, mg, t, scale_out, shift_out, gain, eps):
    link(nc.vector.tensor_copy(mg[:, 0, :], mean_ps))
    link(nc.vector.tensor_tensor(t[:, 0, :], mg[:, 0, :], mg[:, 0, :], ALU.mult))
    link(nc.vector.scalar_tensor_tensor(t[:, 1, :], second_ps, eps, t[:, 0, :], ALU.add, ALU.subtract))
    to_root(nc.vector.tensor_copy(t[:, 0, :], t[:, 1, :]))
    from_root()
    link(nc.vector.reciprocal(t[:, 3, :], t[:, 2, :]))
    link(nc.vector.tensor_tensor(t[:, 4, :], t[:, 3, :], t[:, 3, :], ALU.mult))
    link(nc.vector.tensor_tensor(t[:, 5, :], t[:, 4, :], t[:, 1, :], ALU.mult))
    link(nc.vector.tensor_scalar(t[:, 4, :], t[:, 5, :], -0.5 * gain, 1.5 * gain, ALU.mult, ALU.add))
    link(nc.vector.tensor_tensor(scale_out, t[:, 4, :], t[:, 3, :], ALU.mult))
    link(nc.vector.scalar_tensor_tensor(shift_out, mg[:, 0, :], -1.0, scale_out, ALU.mult, ALU.mult))


def split_weights(nc, dve, hi_ready, count, w32, wh, wl):
    nc.vector.tensor_scalar(wh, w32, SW, None, ALU.mult).then_inc(hi_ready, 1)
    dve.wait_ge(hi_ready, count)
    return nc.vector.scalar_tensor_tensor(wl, w32, SW, wh, ALU.mult, ALU.subtract)


KS = 7
R = KS // 2
STEPS = 8
EPS0 = 1e-6
S0 = 1.0 - 0.5 ** STEPS


def stage_origin(nc, x, ka, kga, coef0, hf):
    n = Names(nc, "org")
    SIDE = 2 * KS - 1
    with n.stack:
        xp = n.sb("xp", [B * SIDE, SIDE, C])
        ident = n.sb("ident", [P, P])
        a32 = n.sb("a32", [C, KS, KS])
        ga = n.sb("ga", [C, KS * KS])
        gsum = n.sb("gsum", [C, 1])
        co = n.sb("co", [C, B, 2])
        pat = n.sb("pat", [C, SIDE * B, SIDE])
        acc = n.sb("acc", [C, 2, KS * B, KS])
        v = n.sb("v", [C, 6, B, KS, KS])
        sp_ = n.sb("sp", [C, 2, B, KS, KS])
        SPLIT = TILE // (B * SIDE)
        pt = n.ps("pt", [C, 2 * TILE])
        (in_x, in_w, in_h, ident_ready, turned, done, sig_go, sig_done, ready, stored) = (
            n.sem(s) for s in ("in_x", "in_w", "in_h", "ident_ready", "turned", "done", "sig_go", "sig_done",
                               "ready", "stored"))
        hf_t = hf.rearrange("c (b h w) -> c b h w", b=B, h=H)
        far = [(H - (SIDE // 2), 0, SIDE // 2), (0, SIDE // 2, SIDE // 2 + 1)]
        near = [(H - R, 0, R), (0, R, R + 1)]
        with nc.Block() as block:
            @block.sync
            def _(sp):
                for b in range(B):
                    for h0, r0, hn in far:
                        for w0, c0, wn in far:
                            sp.dma_start(xp[b * SIDE + r0:b * SIDE + r0 + hn, c0:c0 + wn, :],
                                         x[b, h0:h0 + hn, w0:w0 + wn, :]).then_inc(in_x, 16)
                sp.dma_start(a32[:, :, :], ka).then_inc(in_w, 16)
                sp.dma_start(ga[:, :], kga.rearrange("c i j -> c (i j)")).then_inc(in_w, 16)
                for r in range(GROUP):
                    sp.dma_start(co[r:C:GROUP, :, :], coef0).then_inc(in_w, 16)
                for h0, r0, hn in near:
                    for w0, c0, wn in near:
                        for b in range(B):
                            sp.dma_start(sp_[:, 0, b, r0:r0 + hn, c0:c0 + wn], hf_t[:, b, h0:h0 + hn, w0:w0 + wn]
                                         ).then_inc(in_h, 16)
                sp.wait_ge(ready, 1)
                for h0, r0, hn in near:
                    for w0, c0, wn in near:
                        for b in range(B):
                            sp.dma_start(hf_t[:, b, h0:h0 + hn, w0:w0 + wn], sp_[:, 1, b, r0:r0 + hn, c0:c0 + wn]
                                         ).then_inc(stored, 16)
                sp.wait_ge(stored, 16 * 4 * B)

            @block.gpsimd
            def _(pool):
                nc.gpsimd.memset(ident[:, :], 0.0).then_inc(ident_ready, 1)
                pool.wait_ge(ident_ready, 1)
                nc.gpsimd.affine_select(out=ident[:, :], in_=ident[:, :], compare_op=ALU.not_equal, fill=1.0,
                                        base=0, pattern=[[-1, P]], channel_multiplier=1).then_inc(ident_ready, 1)

            @block.tensor
            def _(pe):
                pe.wait_ge(ident_ready, 2)
                pe.wait_ge(in_x, 16 * 4 * B)
                M = B * SIDE
                for k in range(SIDE):
                    at = k * M if k < SPLIT else TILE + (k - SPLIT) * M
                    last = nc.tensor.transpose(pt[:, at:at + M], xp[:, k, :], ident[0:M, 0:M])
                last.then_inc(turned, 1)

            @block.scalar
            def _(act):
                f = lambda k: v[:, k, :, :, :].rearrange("c b i j -> c (b i j)")
                act.wait_ge(sig_go, 1)
                nc.scalar.activation(f(1), f(0), ACT.Sigmoid).then_inc(sig_done, 1)
                act.wait_ge(sig_go, 2)
                nc.scalar.activation(f(3), f(2), ACT.Sigmoid).then_inc(sig_done, 1)
                nc.scalar.activation(f(4), f(2), ACT.Sigmoid, scale=-1.0).then_inc(sig_done, 1)

            @block.vector
            def _(dve):
                count = [0]

                def link(ins):
                    count[0] += 1
                    ins.then_inc(done, 1)
                    dve.wait_ge(done, count[0])

                dve.wait_ge(turned, 1)
                M = B * SIDE
                pf = pat[:, :, :].rearrange("c m s -> c (m s)")
                nc.vector.tensor_copy(pf[:, 0:SPLIT * M], pt[:, 0:SPLIT * M])
                link(nc.vector.tensor_copy(pf[:, SPLIT * M:SIDE * M], pt[:, TILE:TILE + (SIDE - SPLIT) * M]))
                dve.wait_ge(in_w, 16 * (2 + GROUP))
                link(nc.vector.reduce_sum(gsum[:, :], ga[:, :], AX.X))
                for i in range(KS):
                    for j in range(KS):
                        k = i * KS + j
                        win = pat[:, (KS - 1 - j) * B:(SIDE - j) * B, KS - 1 - i:SIDE - i]
                        if k == 0:
                            link(nc.vector.tensor_scalar(acc[:, 0, :, :], win, ga[:, 0:1], None, ALU.mult))
                        else:
                            link(nc.vector.scalar_tensor_tensor(acc[:, k % 2, :, :], win, ga[:, k:k + 1],
                                                                acc[:, 1 - k % 2, :, :], ALU.mult, ALU.add))
                full = acc[:, (KS * KS - 1) % 2, :, :].rearrange("c (j b) i -> c b i j", b=B)
                link(nc.vector.tensor_scalar(v[:, 5, 0, 0, 0:B], co[:, :, 1], gsum[:, :], 1.0 / SA, ALU.mult, ALU.mult))
                link(nc.vector.tensor_scalar(v[:, 5, 0, 1, 0:B], co[:, :, 0], 1.0 / SA, None, ALU.mult))
                for b in range(B):
                    last = nc.vector.tensor_scalar(v[:, 0, b, :, :], full[:, b, :, :], v[:, 5, 0, 1, b:b + 1],
                                                   v[:, 5, 0, 0, b:b + 1], ALU.mult, ALU.add)
                link(last)
                dve.sem_inc(sig_go, 1)
                dve.wait_ge(sig_done, 1)
                for b in range(B):
                    last = nc.vector.tensor_tensor(v[:, 2, b, :, :], v[:, 1, b, :, :], a32[:, :, :], ALU.mult)
                link(last)
                dve.sem_inc(sig_go, 1)
                dve.wait_ge(sig_done, 3)
                f = lambda k: v[:, k, :, :, :].rearrange("c b i j -> c (b i j)")
                s, c, t, u = f(3), f(4), f(5), f(0)
                link(nc.vector.scalar_tensor_tensor(t, c, 1.0, s, ALU.add, ALU.mult))
                link(nc.vector.tensor_tensor(u, c, c, ALU.mult))
                link(nc.vector.scalar_tensor_tensor(s, u, 1.0, t, ALU.add, ALU.mult))
                link(nc.vector.tensor_tensor(c, u, u, ALU.mult))
                link(nc.vector.scalar_tensor_tensor(t, c, 1.0, s, ALU.add, ALU.mult))
                link(nc.vector.tensor_scalar(u, t, 1.0 / S0, None, ALU.mult))
                dve.wait_ge(in_h, 16 * 4 * B)
                g = lambda k: sp_[:, k, :, :, :].rearrange("c b i j -> c (b i j)")
                link(nc.vector.scalar_tensor_tensor(t, g(0), EPS0, u, ALU.add, ALU.mult))
                nc.vector.tensor_scalar(g(1), t, -EPS0, None, ALU.add).then_inc(ready, 1)


def stage_mix(nc, x, hf, w_out, b_out, x1, stats1):
    n = Names(nc, "mix")
    PAIR = 2 * TILE
    NP = B * PLANE // PAIR
    SUB = PAIR // P
    with n.stack:
        w32 = n.sb("w32", [C, C])
        wh = n.sb("wh", [C, C], F16)
        wl = n.sb("wl", [C, C], F16)
        ident = n.sb("ident", [P, P])
        eps = n.sb("eps", [C, 1])
        bo = n.sb("bo", [C, 1])
        bias = n.sb("bias", [C, 1])
        ws = n.sb("ws", [C, C])
        w_in, ws_ready, w_hi, ident_ready, summed = (n.sem(s) for s in ("w_in", "ws_ready", "w_hi", "ident_ready", "summed"))
        own = Names(nc, "mixw")
        with own.stack:
            pb = own.ps("pb", [C, TILE])
            with nc.Block() as block:
                @block.sync
                def _(sp):
                    sp.dma_start(w32[:, :], w_out).then_inc(w_in, 16)
                    sp.dma_start(bo[:, :], b_out.rearrange("(c a) -> c a", a=1)).then_inc(w_in, 16)

                @block.gpsimd
                def _(pool):
                    nc.gpsimd.memset(ident[:, :], 0.0).then_inc(ident_ready, 1)
                    pool.wait_ge(ident_ready, 1)
                    nc.gpsimd.affine_select(out=ident[:, :], in_=ident[:, :], compare_op=ALU.not_equal, fill=SA * SW,
                                            base=0, pattern=[[-1, P]], channel_multiplier=1).then_inc(ident_ready, 1)

                @block.tensor
                def _(pe):
                    pe.wait_ge(ws_ready, 2)
                    nc.tensor.matmul(pb[:, 0:1], ws[:, :], eps[:, :], start=True, stop=True).then_inc(summed, 1)

                @block.vector
                def _(dve):
                    nc.vector.memset(eps[:, :], EPS0).then_inc(ws_ready, 1)
                    dve.wait_ge(w_in, 32)
                    nc.vector.tensor_scalar(ws[:, :], w32[:, :], S0, None, ALU.mult).then_inc(ws_ready, 1)
                    dve.wait_ge(ws_ready, 2)
                    split_weights(nc, dve, w_hi, 1, ws[:, :], wh[:, :], wl[:, :])
                    dve.wait_ge(summed, 1)
                    nc.vector.tensor_tensor(bias[:, :], pb[:, 0:1], bo[:, :], ALU.add)

        xin = n.sb("xin", [P, 2, SUB, C])
        hin = n.sb("hin", [C, 2, PAIR])
        hh = n.sb("hh", [C, 2, PAIR], F16)
        hl = n.sb("hl", [C, 2, PAIR], F16)
        xo = n.sb("xo", [C, 2, PAIR])
        st = n.sb("st", [C, B * TILES, 6])
        acc = [n.ps(f"acc{k}", [C, TILE]) for k in range(4)]
        x_in = [n.sem(f"x_in{k}") for k in range(2)]
        h_in = [n.sem(f"h_in{k}") for k in range(2)]
        stored = [n.sem(f"stored{k}") for k in range(2)]
        hi_done, lo_done, acc_done, out_done, st_done, st_stored = (
            n.sem(s) for s in ("hi_done", "lo_done", "acc_done", "out_done", "st_done", "st_stored"))
        x_t = x.rearrange("b h w c -> (b h w) c").rearrange("(t s p) c -> p t s c", p=P, s=SUB)
        with nc.Block() as block:
            @block.sync
            def _(sp):
                def load(i, k):
                    sp.dma_start(xin[:, k, :, :], x_t[:, bass.ds(i * 2 + k, 1), :, :].rearrange("p a s c -> p (a s) c")
                                 ).then_inc(x_in[k], 16)
                    sp.dma_start(hin[:, k, :], hf[:, bass.ds(i * (2 * PAIR) + k * PAIR, PAIR)]).then_inc(h_in[k], 16)

                load(0, 0)
                load(0, 1)
                with sp.Fori(1, NP // 2) as i:
                    for k in range(2):
                        sp.wait_ge(acc_done, i * 4 + (2 * k - 2))
                        sp.wait_ge(lo_done, i * 4 + (2 * k - 2))
                        load(i, k)

            @block.scalar
            def _(act):
                def split(i, k):
                    act.wait_ge(h_in[k], i * 16 + 16)
                    for u in range(2):
                        nc.scalar.activation(hh[:, k, u * TILE:(u + 1) * TILE], hin[:, k, u * TILE:(u + 1) * TILE],
                                             ACT.Copy, scale=SA).then_inc(hi_done, 1)

                def leave(i, k, first):
                    if not first:
                        act.wait_ge(stored[k], i * 16)
                        act.wait_ge(st_done, i * 4 + (2 * k - 2))
                    for u in range(2):
                        act.wait_ge(acc_done, i * 4 + (2 * k + u + 1))
                        nc.scalar.activation(xo[:, k, u * TILE:(u + 1) * TILE], acc[2 * k + u][:, :], ACT.Identity,
                                             bias=bias[:, 0:1], scale=DESCALE).then_inc(out_done, 1)
                    act.wait_ge(out_done, i * 4 + (2 * k + 2))
                    act.dma_start(x1[:, bass.ds(i * (2 * PAIR) + k * PAIR, PAIR)], xo[:, k, :]).then_inc(stored[k], 16)

                split(0, 0)
                split(0, 1)
                leave(0, 0, True)
                act.wait_ge(acc_done, 2)
                split(1, 0)
                leave(0, 1, True)
                with act.Fori(1, NP // 2 - 1) as i:
                    act.wait_ge(acc_done, i * 4)
                    split(i, 1)
                    leave(i, 0, False)
                    act.wait_ge(acc_done, i * 4 + 2)
                    split(i + 1, 0)
                    leave(i, 1, False)
                i = NP // 2 - 1
                act.wait_ge(acc_done, i * 4)
                split(i, 1)
                leave(i, 0, False)
                leave(i, 1, False)
                act.wait_ge(st_done, B * TILES)
                act.dma_start(stats1, st[:, :, :].rearrange("c (b t) s -> c b (t s)", b=B)).then_inc(st_stored, 16)
                act.wait_ge(st_stored, 16)
                act.wait_ge(stored[0], 16 * NP // 2)
                act.wait_ge(stored[1], 16 * NP // 2)

            @block.vector
            def _(dve):
                def rest(i, k):
                    for u in range(2):
                        cols = slice(u * TILE, (u + 1) * TILE)
                        dve.wait_ge(hi_done, i * 4 + (2 * k + u + 1))
                        nc.vector.scalar_tensor_tensor(hl[:, k, cols], hin[:, k, cols], SA, hh[:, k, cols],
                                                       ALU.mult, ALU.subtract).then_inc(lo_done, 1)

                def stat(i, k):
                    for u in range(2):
                        dve.wait_ge(out_done, i * 4 + (2 * k + u + 1))
                        nc.vector.bn_stats(st[:, bass.ds(i * 4 + 2 * k + u, 1), :].rearrange("c a s -> c (a s)"),
                                           xo[:, k, u * TILE:(u + 1) * TILE]).then_inc(st_done, 1)

                rest(0, 0)
                with dve.Fori(0, NP // 2 - 1) as i:
                    rest(i, 1)
                    stat(i, 0)
                    rest(i + 1, 0)
                    stat(i, 1)
                rest(NP // 2 - 1, 1)
                stat(NP // 2 - 1, 0)
                stat(NP // 2 - 1, 1)

            @block.tensor
            def _(pe):
                def pair(i, k, first):
                    pe.wait_ge(x_in[k], i * 16 + 16)
                    for u in range(2):
                        cols = slice(u * TILE, (u + 1) * TILE)
                        if not first:
                            pe.wait_ge(out_done, i * 4 + (2 * k + u - 3))
                        for s in range(TILE // P):
                            nc.tensor.matmul(acc[2 * k + u][:, s * P:(s + 1) * P], xin[:, k, u * (TILE // P) + s, :],
                                             ident[:, :], start=(s == 0), stop=False, skip_group_check=True)
                        pe.wait_ge(lo_done, i * 4 + (2 * k + u + 1))
                        for a, b in ((wh, hh), (wh, hl), (wl, hh)):
                            last = nc.tensor.matmul(acc[2 * k + u][:, :], a[:, :], b[:, k, cols], start=False,
                                                    stop=(a is wl), skip_group_check=True)
                        last.then_inc(acc_done, 1)

                pair(0, 0, True)
                pair(0, 1, True)
                with pe.Fori(1, NP // 2) as i:
                    pair(i, 0, False)
                    pair(i, 1, False)


QUADS = C // GROUP
CG = 32
QG = CG // GROUP
NCG = C // CG
PER = 8
SUMS = 2 * KS
WP = W + 2 * R


def stage_taps(nc, kb, kg, taps):
    n = Names(nc, "tap")
    with n.stack:
        k32 = n.sb("k32", [C, 2, KS, KS])
        dbl = n.sb("dbl", [C, 2, 2, KS, 2 * PER], F16)
        rot = n.sb("rot", [C, PER, 2 * SUMS, PER], F16)
        k_in, cleared, hi_done, lo_done, turned, stored = (
            n.sem(s) for s in ("k_in", "cleared", "hi_done", "lo_done", "turned", "stored"))
        with nc.Block() as block:
            @block.sync
            def _(sp):
                sp.dma_start(k32[:, 0, :, :], kg).then_inc(k_in, 16)
                sp.dma_start(k32[:, 1, :, :], kb).then_inc(k_in, 16)
                sp.wait_ge(turned, 1)
                sp.dma_start(taps.rearrange("p c n -> c p n"), rot[:, :, :, :].rearrange("c p n m -> c p (n m)")
                             ).then_inc(stored, 16)
                sp.wait_ge(stored, 16)

            @block.vector
            def _(dve):
                nc.vector.memset(dbl[:, :, :, :, :], 0.0).then_inc(cleared, 1)
                dve.wait_ge(cleared, 1)
                dve.wait_ge(k_in, 32)
                for k in range(2):
                    src = k32[:, k, :, :].rearrange("c i j -> c j i")
                    last = nc.vector.tensor_scalar(dbl[:, 0, k, :, 0:KS], src, SW, None, ALU.mult)
                last.then_inc(hi_done, 1)
                dve.wait_ge(hi_done, 1)
                for k in range(2):
                    src = k32[:, k, :, :].rearrange("c i j -> c j i")
                    last = nc.vector.scalar_tensor_tensor(dbl[:, 1, k, :, 0:KS], src, SW, dbl[:, 0, k, :, 0:KS],
                                                          ALU.mult, ALU.subtract)
                last.then_inc(lo_done, 1)
                dve.wait_ge(lo_done, 1)
                d = dbl[:, :, :, :, :].rearrange("c a k j m -> c (a k j) m")
                nc.vector.tensor_copy(d[:, :, PER:2 * PER], d[:, :, 0:PER]).then_inc(lo_done, 1)
                dve.wait_ge(lo_done, 2)
                for p in range(PER):
                    s = (R - p) % PER
                    last = nc.vector.tensor_copy(rot[:, p, :, :], d[:, :, s:s + PER])
                last.then_inc(turned, 1)


def stage_depthwise(nc, x, taps, coef0, hf):
    n = Names(nc, "dw")
    with n.stack:
        xg = n.sb("xg", [H, 2 * B, W, CG])
        xn = n.sb("xn", [H, GROUP, B, W])
        xh = n.sb("xh", [H, 2, GROUP, B, WP], F16)
        xl = n.sb("xl", [H, 2, GROUP, B, WP], F16)
        vt = n.sb("v", [H, 2, GROUP, 2 * SUMS, PER], F16)
        circ = n.sb("circ", [H, 2, 2 * SUMS, H], F16)
        mask = n.sb("mask", [H, H], F16)
        mk = n.sb("mk", [H, 3, H])
        ones = n.sb("ones", [H, H])
        e = n.sb("e", [H, 2, B * W])
        bt = n.sb("bt", [H, 2, B * W])
        ln = n.sb("ln", [H, 2, B * W])
        so = n.sb("so", [H, 2, B * W])
        NG = QG * B
        bs = n.sb("bs", [H, NG, 6])
        mom = n.sb("mom", [H, 2, NG])
        sq = n.sb("sq", [H, 3, NG])
        mg = n.sb("mg", [H, 2, NG])
        t = n.sb("t", [H, 6, NG])
        coef = n.sb("coef", [H, NG, 2])
        gate_ps = [n.ps(f"gate{k}", [H, B * W]) for k in range(2)]
        val_ps = [n.ps(f"val{k}", [H, B * W]) for k in range(2)]
        pm = n.ps("pm", [H, TILE])
        x_in = [n.sem(f"x_in{b}") for b in range(B)]
        v_in = [n.sem(f"v_in{k}") for k in range(2)]
        stored = [n.sem(f"stored{k}") for k in range(2)]
        (mask_parts, mask_ready, xn_done, hi_done, lo_done, xh_wrapped, xl_wrapped, circ_ready, gate_done, val_done, e_ready,
         cap_done, sig_done, bt_done, abs_done, lge_done, exp_done, ln_done, so_ready, stats_step, moments, averaged,
         var_ready, root_ready, coef_ready, coef_stored) = (
            n.sem(s) for s in (
                "mask_parts", "mask_ready", "xn_done", "hi_done", "lo_done", "xh_wrapped", "xl_wrapped", "circ_ready", "gate_done",
                "val_done", "e_ready", "cap_done", "sig_done", "bt_done", "abs_done", "lge_done", "exp_done", "ln_done",
                "so_ready", "stats_step", "moments", "averaged", "var_ready", "root_ready", "coef_ready",
                "coef_stored"))
        x_t = x.rearrange("b h w c -> h b w c")
        hf_t = hf.rearrange("c (b h w) -> h c b w", b=B, h=H)
        PERQ = GROUP
        LINKS = 5 + 9

        with nc.Block() as block:
            @block.sync
            def _(sp):
                def load_x(cg, piece):
                    b, half = divmod(piece, 2)
                    cols = slice(half * (W // 2), (half + 1) * (W // 2))
                    sp.dma_start(xg[:, bass.ds((cg % 2) * B + b, 1), cols, :].rearrange("h a w c -> h (a w) c"),
                                 x_t[:, b, cols, bass.ds(cg * CG, CG)]).then_inc(x_in[b], 16)

                def load_v(q, s):
                    src = taps[:, bass.ds(q * GROUP, GROUP), :].rearrange("p c n -> p (c n)")
                    sp.dma_start(vt[:, s, :, :, :].rearrange("p c n m -> p (c n m)"),
                                 src.partition_broadcast(H // PER)).then_inc(v_in[s], 16)

                def store_coef(cg):
                    sp.wait_ge(coef_ready, cg + 1)
                    sp.dma_start(coef0[bass.ds(cg, 1), :], coef[0:1, :, :].rearrange("p g s -> p (g s)")
                                 ).then_inc(coef_stored, 16)

                def body(cg, first=False, ahead=True, last=False):
                    for g in range(QG):
                        if not (last and g == QG - 1):
                            if not (first and g == 0):
                                sp.wait_ge(circ_ready, cg * CG + g * PERQ)
                            load_v(cg * QG + (g + 1), (g + 1) % 2)
                        if g == QG - 1 and ahead:
                            sp.wait_ge(xn_done, (cg + 1) * (QG * B))
                            sp.wait_ge(hi_done, (cg + 1) * (QG * B))
                        for r in range(PERQ):
                            c = cg * CG + (g * PERQ + r)
                            sp.wait_ge(so_ready, c + 1)
                            sp.dma_start(hf_t[:, bass.ds(c, 1), :, :].rearrange("h a b w -> h (a b) w"),
                                         so[:, r % 2, :].rearrange("h (b w) -> h b w", b=B)).then_inc(stored[r % 2], 16)
                            if g == QG - 1 and ahead:
                                load_x(cg + 2, r)
                            if g == 0 and not first and not last:
                                load_x(cg + 1, PERQ + r)
                        if g == QG - 1 and not last:
                            store_coef(cg + 1)

                for piece in range(2 * B):
                    load_x(0, piece)
                load_v(0, 0)
                for b in range(B):
                    sp.wait_ge(x_in[b], 32)
                for piece in range(2 * B):
                    load_x(1, piece)
                store_coef(0)
                body(0, first=True)
                with sp.Fori(1, NCG - 2) as cg:
                    body(cg)
                body(NCG - 2, ahead=False)
                body(NCG - 1, ahead=False, last=True)
                for k in range(2):
                    sp.wait_ge(stored[k], 16 * C // 2)
                sp.wait_ge(coef_stored, 16 * NCG)

            @block.gpsimd
            def _(pool):
                nc.gpsimd.memset(mk[:, :, :], 1.0).then_inc(mask_parts, 1)
                pool.wait_ge(mask_parts, 1)
                nc.gpsimd.affine_select(out=mk[:, 0, :], in_=mk[:, 0, :], compare_op=ALU.is_ge, fill=0.0, base=R,
                                        pattern=[[1, H]], channel_multiplier=-1).then_inc(mask_parts, 1)
                nc.gpsimd.affine_select(out=mk[:, 1, :], in_=mk[:, 1, :], compare_op=ALU.is_ge, fill=0.0,
                                        base=-(H - R), pattern=[[-1, H]], channel_multiplier=1).then_inc(mask_parts, 1)
                nc.gpsimd.affine_select(out=mk[:, 2, :], in_=mk[:, 2, :], compare_op=ALU.is_ge, fill=0.0,
                                        base=-(H - R), pattern=[[1, H]], channel_multiplier=-1).then_inc(mask_parts, 1)
                pool.wait_ge(mask_parts, 4)
                nc.gpsimd.affine_select(out=mk[:, 0, :], in_=mk[:, 0, :], compare_op=ALU.is_ge, fill=0.0, base=R,
                                        pattern=[[-1, H]], channel_multiplier=1).then_inc(mask_parts, 1)

                def split(q, s):
                    for b in range(B):
                        pool.wait_ge(hi_done, q * B + (b + 1))
                        pool.wait_ge(xn_done, q * B + (b + 1))
                        nc.gpsimd.tensor_tensor(xl[:, s, :, b, R:R + W], xn[:, :, b, :], xh[:, s, :, b, R:R + W],
                                                ALU.subtract).then_inc(lo_done, 1)
                    rest = lambda at, src: nc.gpsimd.tensor_tensor(
                        xl[:, s, :, :, at:at + R], xn[:, :, :, src:src + R], xh[:, s, :, :, R + src:2 * R + src],
                        ALU.subtract)
                    rest(0, W - R)
                    rest(R + W, 0).then_inc(xl_wrapped, 1)

                with pool.Fori(0, QUADS // 2) as i:
                    split(i * 2, 0)
                    split(i * 2 + 1, 1)

            @block.tensor
            def _(pe):
                def channel(c, s, u, k, reused):
                    pe.wait_ge(circ_ready, c + 1)
                    if reused:
                        pe.wait_ge(bt_done, c - 1)
                    for kern, ps, done in ((0, gate_ps, gate_done), (1, val_ps, val_done)):
                        for j in range(KS):
                            hi = circ[:, k, kern * KS + j, :]
                            lo = circ[:, k, SUMS + kern * KS + j, :]
                            cols = slice(KS - 1 - j, KS - 1 - j + W)
                            for p, (a, b) in enumerate(((hi, xh), (hi, xl), (lo, xh))):
                                last = nc.tensor.matmul(ps[k][:, :], a, b[:, s, u, :, cols],
                                                        start=(j == 0 and p == 0), stop=(j == KS - 1 and p == 2))
                        last.then_inc(done, 1)

                def average(cg):
                    pe.wait_ge(moments, cg + 1)
                    nc.tensor.matmul(pm[:, 0:2 * NG], ones[:, :], mom[:, :, :].rearrange("h a g -> h (a g)"),
                                     start=True, stop=True).then_inc(averaged, 1)

                def quad(q, s, first=False, avg=None):
                    pe.wait_ge(xh_wrapped, q + 1)
                    pe.wait_ge(xl_wrapped, q + 1)
                    for u in range(PERQ):
                        channel(q * PERQ + u, s, u, u % 2, not (first and u < 2))
                        if avg is not None and u == 2:
                            average(avg)

                average(0)
                def load(cg, first=False, last=False):
                    for g in range(QG):
                        quad(cg * QG + g, g % 2, first and g == 0, cg + 1 if g == QG - 2 and not last else None)
                load(0, first=True)
                with pe.Fori(1, NCG - 1) as cg:
                    load(cg)
                load(NCG - 1, last=True)

            @block.scalar
            def _(act):
                def norm(q, slot, g, s):
                    for b in range(B):
                        k = g * B + b
                        nc.scalar.activation(xh[:, s, :, b, R:R + W],
                                             xg[:, bass.ds(slot * B + b, 1), :, g * GROUP:(g + 1) * GROUP
                                                ].rearrange("h a w c -> h c (a w)"),
                                             ACT.Identity, bias=coef[:, k, 1:2], scale=coef[:, k, 0:1]
                                             ).then_inc(hi_done, 1)
                    act.wait_ge(hi_done, (q + 1) * B)
                    rows = xh[:, s, :, :, :].rearrange("h c b w -> h (c b) w")
                    nc.scalar.activation(rows[:, :, 0:R], rows[:, :, W:W + R], ACT.Copy)
                    nc.scalar.activation(rows[:, :, W + R:WP], rows[:, :, R:2 * R], ACT.Copy).then_inc(xh_wrapped, 1)

                def gate(c, k):
                    act.wait_ge(gate_done, c + 1)
                    nc.scalar.activation(e[:, k, :], gate_ps[k][:, :], ACT.Exp, scale=-DESCALE).then_inc(e_ready, 1)

                def sigmoid(c, k):
                    act.wait_ge(cap_done, c + 1)
                    nc.scalar.activation(e[:, k, :], e[:, k, :], ACT.Ln, bias=1.0).then_inc(lge_done, 1)
                    act.wait_ge(lge_done, c + 1)
                    nc.scalar.activation(e[:, k, :], e[:, k, :], ACT.Exp, scale=-1.0).then_inc(sig_done, 1)

                def log1p(c, k):
                    act.wait_ge(bt_done, c + 1)
                    nc.scalar.activation(ln[:, k, :], bt[:, k, :], ACT.Abs).then_inc(abs_done, 1)
                    act.wait_ge(abs_done, c + 1)
                    nc.scalar.activation(ln[:, k, :], ln[:, k, :], ACT.Exp, scale=-1.0).then_inc(exp_done, 1)
                    act.wait_ge(exp_done, c + 1)
                    nc.scalar.activation(ln[:, k, :], ln[:, k, :], ACT.Ln, bias=1.0).then_inc(ln_done, 1)

                def root(cg):
                    act.wait_ge(var_ready, cg + 1)
                    nc.scalar.activation(t[:, 2, :], t[:, 1, :], ACT.Sqrt).then_inc(root_ready, 1)
                    act.preload_act_table_set("natural_log_exp_and_others")

                def body(cg, first=False, last=False):
                    for g in range(QG):
                        for r in range(PERQ):
                            c = cg * CG + (g * PERQ + r)
                            if r == 1 and not (last and g == QG - 1):
                                q = cg * QG + (g + 1)
                                if not (first and g == 0):
                                    act.wait_ge(val_done, (q - 1) * PERQ)
                                if g == QG - 1:
                                    act.wait_ge(coef_ready, cg + 2)
                                norm(q, (cg + (g == QG - 1)) % 2, (g + 1) % QG, (g + 1) % 2)
                            gate(c, r % 2)
                            if g == QG - 2 and r == 2 and not last:
                                root(cg + 1)
                            sigmoid(c, r % 2)
                            log1p(c, r % 2)

                root(0)
                act.wait_ge(coef_ready, 1)
                norm(0, 0, 0, 0)
                body(0, first=True)
                with act.Fori(1, NCG - 1) as cg:
                    body(cg)
                body(NCG - 1, last=True)

            @block.vector
            def _(dve):
                def stat(cg, slot, k):
                    b, g = divmod(k, QG)
                    if g == 0:
                        dve.wait_ge(x_in[b], cg * 32 + 32)
                    k = g * B + b
                    nc.vector.bn_stats(bs[:, k, :], xg[:, bass.ds(slot * B + b, 1), :, g * GROUP:(g + 1) * GROUP
                                                       ].rearrange("h a w c -> h (a w) c")).then_inc(stats_step, 1)

                def coefficients(cg):
                    base = cg * (NG + LINKS) + NG
                    count = [0]

                    def link(ins):
                        count[0] += 1
                        ins.then_inc(stats_step, 1)
                        dve.wait_ge(stats_step, base + count[0])

                    dve.wait_ge(stats_step, base)
                    me, mo, ve, vo = bs[:, :, 1], bs[:, :, 4], bs[:, :, 2], bs[:, :, 5]
                    link(nc.vector.tensor_tensor(mom[:, 0, :], me, mo, ALU.add))
                    nc.vector.tensor_tensor(sq[:, 0, :], me, me, ALU.mult)
                    nc.vector.tensor_tensor(sq[:, 1, :], mo, mo, ALU.mult)
                    link(nc.vector.tensor_tensor(sq[:, 2, :], ve, vo, ALU.add))
                    link(nc.vector.tensor_tensor(sq[:, 0, :], sq[:, 0, :], sq[:, 1, :], ALU.add))
                    link(nc.vector.scalar_tensor_tensor(mom[:, 1, :], sq[:, 2, :], 1.0 / (W * GROUP // 2), sq[:, 0, :],
                                                        ALU.mult, ALU.add))
                    nc.vector.tensor_copy(mg[:, 1, 0:1], mom[:, 1, 0:1]).then_inc(moments, 1)
                    dve.wait_ge(averaged, cg + 1)
                    rsqrt_and_shift(nc, link, lambda ins: ins.then_inc(var_ready, 1),
                                    lambda: dve.wait_ge(root_ready, cg + 1), pm[:, 0:NG], pm[:, NG:2 * NG], mg, t,
                                    coef[:, :, 0], coef[:, :, 1], SA, GN_EPS)
                    link(nc.vector.tensor_copy(mg[:, 1, 0:1], mom[:, 1, 0:1]))
                    assert count[0] == LINKS, count[0]
                    dve.sem_inc(coef_ready, 1)

                def norm(q, slot, g, b):
                    nc.vector.tensor_scalar(xn[:, :, b, :],
                                            xg[:, bass.ds(slot * B + b, 1), :, g * GROUP:(g + 1) * GROUP
                                               ].rearrange("h a w c -> h c (a w)"),
                                            coef[:, g * B + b, 0:1], coef[:, g * B + b, 1:2],
                                            ALU.mult, ALU.add).then_inc(xn_done, 1)

                def circulants(s, u, k):
                    taps_ = vt[:, s, u, :, :].unsqueeze(2).broadcast_to([H, 2 * SUMS, H // PER, PER])
                    m = mask[:, :].rearrange("h (a m) -> h a m", m=PER).unsqueeze(1).broadcast_to(
                        [H, 2 * SUMS, H // PER, PER])
                    nc.vector.tensor_tensor(circ[:, k, :, :].rearrange("h n (a m) -> h n a m", m=PER), taps_, m,
                                            ALU.mult).then_inc(circ_ready, 1)

                def cap(c, k):
                    dve.wait_ge(e_ready, c + 1)
                    nc.vector.tensor_scalar(e[:, k, :], e[:, k, :], 2.0 ** 60, None, ALU.min).then_inc(cap_done, 1)

                def value(c, k):
                    dve.wait_ge(val_done, c + 1)
                    dve.wait_ge(sig_done, c + 1)
                    nc.vector.scalar_tensor_tensor(bt[:, k, :], val_ps[k][:, :], DESCALE, e[:, k, :],
                                                   ALU.mult, ALU.mult).then_inc(bt_done, 1)

                def softplus(c, k, reused):
                    dve.wait_ge(ln_done, c + 1)
                    if reused is not None:
                        dve.wait_ge(stored[k], reused)
                    nc.vector.scalar_tensor_tensor(so[:, k, :], bt[:, k, :], 0.0, ln[:, k, :], ALU.max, ALU.add
                                                   ).then_inc(so_ready, 1)

                def body(cg, first=False, last=False):
                    nslot = (cg + 1) % 2
                    for g in range(QG):
                        for r in range(PERQ):
                            start, end = first and g == 0 and r == 0, last and g == QG - 1 and r == PERQ - 1
                            c = cg * CG + (g * PERQ + r)
                            if not start:
                                value(c - 1, (r + 1) % 2)
                            if not end:
                                if r == PERQ - 1:
                                    s = (g + 1) % 2
                                    dve.wait_ge(v_in[s], (cg * (QG // 2) + (g + 1) // 2) * 16 + 16)
                                if not start:
                                    dve.wait_ge(val_done, c)
                                circulants((g + (r == PERQ - 1)) % 2, (r + 1) % PERQ, (r + 1) % 2)
                            if not start:
                                early = first and g == 0 and r < 3
                                softplus(c - 1, (r + 1) % 2,
                                         None if early else (cg * (CG // 2) + (g * PERQ + r - 1) // 2) * 16)
                            if r == 3:
                                cap(c, 1)
                            if r < 2 and not (last and g == QG - 1):
                                q = cg * QG + (g + 1)
                                for b in (2 * r, 2 * r + 1):
                                    dve.wait_ge(xl_wrapped, q)
                                    norm(q, (cg + (g == QG - 1)) % 2, (g + 1) % QG, b)
                            if r < 3:
                                cap(c, r % 2)
                            if not last and 2 <= g < 6:
                                for k in range(2):
                                    stat(cg + 1, nslot, ((g - 2) * PERQ + r) * 2 + k)
                            if not last and g == 6 and r == 2:
                                dve.wait_ge(hi_done, (cg + 1) * (QG * B))
                                dve.wait_ge(coef_stored, cg * 16 + 16)
                                coefficients(cg + 1)

                nc.vector.memset(ones[:, :], 1.0 / (2 * H))
                dve.wait_ge(mask_parts, 5)
                nc.vector.tensor_tensor(mk[:, 1, :], mk[:, 1, :], mk[:, 2, :], ALU.add).then_inc(mask_ready, 1)
                dve.wait_ge(mask_ready, 1)
                nc.vector.tensor_tensor(mask[:, :], mk[:, 0, :], mk[:, 1, :], ALU.add).then_inc(mask_ready, 1)
                dve.wait_ge(mask_ready, 2)
                dve.wait_ge(v_in[0], 16)
                circulants(0, 0, 0)
                for k in range(NG):
                    stat(0, 0, k)
                coefficients(0)
                for b in range(B):
                    norm(0, 0, 0, b)
                body(0, first=True)
                with dve.Fori(1, NCG - 1) as cg:
                    body(cg)
                body(NCG - 1, last=True)
                value(C - 1, 1)
                softplus(C - 1, 1, 16 * (C // 2 - 1))


CI = 16
LN_EPS = 1e-5
JB = P // CI


def stage_triangle(nc, x1, stats1, wa, ba, wb, bb, ln_g, ln_b, wg, bg, wz, bz, x2, stats2):
    n = Names(nc, "tri")
    PT = 2
    NL = TILES // PT
    GR = 16
    NGR = H // GR
    ZN = CI * W
    with n.stack:
        coef = n.sb("coef", [C, B, 2])
        ident = n.sb("ident", [P, P])
        gh = n.sb("gh", [C, C], F16)
        gl = n.sb("gl", [C, C], F16)
        ph = n.sb("ph", [C, 2, 2 * CI], F16)
        pl = n.sb("pl", [C, 2, 2 * CI], F16)
        pbias = n.sb("pbias", [P, 2, TILE], F16)
        prow = n.sb("prow", [P, P], F16)
        zh = n.sb("zh", [P, JB, C], F16)
        zl = n.sb("zl", [P, JB, C], F16)
        bgc = n.sb("bg", [C, 1])
        bzc = n.sb("bz", [C, 1])
        group_norm_coefficients(nc, n, stats1, coef, SA)

        own = Names(nc, "triw")
        with own.stack:
            g32 = own.sb("g32", [C, C])
            p32 = own.sb("p32", [C, 2, 2 * CI])
            b32 = own.sb("b32", [1, 2, 2 * CI])
            bh = own.sb("bh", [1, 2, 2 * CI], F16)
            bl = own.sb("bl", [1, 2, 2 * CI], F16)
            rep = own.sb("rep", [P, C])
            lng = own.sb("lng", [P, 1])
            wz32 = own.sb("wz32", [CI, C])
            lnb = own.sb("lnb", [CI, 1])
            bzi = own.sb("bzi", [C, 1])
            mask = own.sb("mask", [P, JB])
            blk = own.sb("blk", [P, JB, C])
            lh = own.sb("lh", [1, 2, TILE], F16)
            ll = own.sb("ll", [1, 2, TILE], F16)
            pz = own.ps("pz", [C, TILE])
            w_in, made, step, summed, moved = (own.sem(s) for s in ("w_in", "made", "step", "summed", "moved"))
            LOADS = 5 + 8 + 2 * JB
            STEPS = 12
            with nc.Block() as block:
                @block.sync
                def _(sp):
                    loads = [(g32[:, :], wg), (bgc[:, :], bg.rearrange("(c a) -> c a", a=1)), (wz32[:, :], wz),
                             (lnb[:, :], ln_b.rearrange("(c a) -> c a", a=1)),
                             (bzi[:, :], bz.rearrange("(c a) -> c a", a=1))]
                    for k, (ws, bs) in enumerate(((wa, ba), (wb, bb))):
                        for u in range(2):
                            loads.append((p32[:, k, u * CI:(u + 1) * CI], ws[u]))
                            loads.append((b32[:, k, u * CI:(u + 1) * CI], bs[u].rearrange("(a c) -> a c", a=1)))
                    for j in range(JB):
                        loads.append((rep[j * CI:(j + 1) * CI, :], wz))
                        loads.append((lng[j * CI:(j + 1) * CI, :], ln_g.rearrange("(c a) -> c a", a=1)))
                    assert len(loads) == LOADS
                    for dst, src in loads:
                        sp.dma_start(dst, src).then_inc(w_in, 16)
                    sp.wait_ge(step, STEPS)
                    sp.dma_start(pbias[0:1, :, :], lh[:, :, :]).then_inc(moved, 16)
                    sp.dma_start(pbias[1:2, :, :], ll[:, :, :]).then_inc(moved, 16)
                    sp.wait_ge(moved, 32)

                @block.gpsimd
                def _(pool):
                    nc.gpsimd.memset(ident[:, :], 0.0)
                    nc.gpsimd.memset(prow[:, :], SA)
                    nc.gpsimd.memset(mask[:, :], 1.0).then_inc(made, 1)
                    pool.wait_ge(made, 1)
                    nc.gpsimd.affine_select(out=ident[:, :], in_=ident[:, :], compare_op=ALU.not_equal, fill=1.0,
                                            base=0, pattern=[[-1, P]], channel_multiplier=1)
                    nc.gpsimd.affine_select(out=prow[:, :], in_=prow[:, :], compare_op=ALU.is_ge, fill=0.0,
                                            base=1, pattern=[[0, P]], channel_multiplier=-1)
                    nc.gpsimd.affine_select(out=mask[:, :], in_=mask[:, :], compare_op=ALU.is_ge, fill=0.0,
                                            base=0, pattern=[[-CI, JB]], channel_multiplier=1).then_inc(made, 1)
                    pool.wait_ge(made, 2)
                    nc.gpsimd.affine_select(out=mask[:, :], in_=mask[:, :], compare_op=ALU.is_ge, fill=0.0,
                                            base=CI - 1, pattern=[[CI, JB]], channel_multiplier=-1).then_inc(made, 1)

                @block.tensor
                def _(pe):
                    pe.wait_ge(w_in, 16 * LOADS)
                    nc.tensor.matmul(pz[:, 0:1], wz32[:, :], lnb[:, :], start=True, stop=True).then_inc(summed, 1)

                @block.vector
                def _(dve):
                    count = [0]

                    def link(ins):
                        count[0] += 1
                        ins.then_inc(step, 1)
                        dve.wait_ge(step, count[0])

                    link(nc.vector.memset(pbias[:, :, :], 0.0))
                    dve.wait_ge(w_in, 16 * LOADS)
                    link(nc.vector.tensor_scalar(bh[:, :, :], b32[:, :, :], SW, None, ALU.mult))
                    link(nc.vector.scalar_tensor_tensor(bl[:, :, :], b32[:, :, :], SW, bh[:, :, :],
                                                        ALU.mult, ALU.subtract))
                    for k in range(2):
                        for dst, src in ((lh, bh), (ll, bl)):
                            v = src[:, k, :].unsqueeze(1).broadcast_to([1, GR, 2 * CI])
                            last = nc.vector.tensor_copy(dst[:, k, :].rearrange("a (r c) -> a r c", r=GR), v)
                    link(last)
                    link(nc.vector.tensor_scalar(gh[:, :], g32[:, :], SW, None, ALU.mult))
                    link(nc.vector.scalar_tensor_tensor(gl[:, :], g32[:, :], SW, gh[:, :], ALU.mult, ALU.subtract))
                    link(nc.vector.tensor_scalar(ph[:, :, :], p32[:, :, :], SW, None, ALU.mult))
                    link(nc.vector.scalar_tensor_tensor(pl[:, :, :], p32[:, :, :], SW, ph[:, :, :],
                                                        ALU.mult, ALU.subtract))
                    dve.wait_ge(made, 3)
                    for j in range(JB):
                        last = nc.vector.tensor_scalar(blk[:, j, :], rep[:, :], lng[:, 0:1], mask[:, j:j + 1],
                                                       ALU.mult, ALU.mult)
                    link(last)
                    link(nc.vector.tensor_scalar(zh[:, :, :], blk[:, :, :], SW, None, ALU.mult))
                    link(nc.vector.scalar_tensor_tensor(zl[:, :, :], blk[:, :, :], SW, zh[:, :, :],
                                                        ALU.mult, ALU.subtract))
                    dve.wait_ge(summed, 1)
                    link(nc.vector.tensor_scalar(bzc[:, :], pz[:, 0:1], bzi[:, 0:1], SA * SW, ALU.add, ALU.mult))
                    assert count[0] == STEPS, count[0]

        xh = n.sb("xh", [C, PLANE], F16)
        xl = n.sb("xl", [C, PLANE], F16)
        gate = n.sb("gate", [C, PLANE])
        xin = n.sb("xin", [C, 2, PT * TILE])
        xr = n.sb("xr", [C, 2, PT * TILE])
        xo = n.sb("xo", [C, 2, PT * TILE])
        xn = n.sb("xn", [C, 2, TILE])
        half = n.sb("half", [P, 2, GR, CI])
        prod = n.sb("prod", [P, 2, GR, CI])
        ab = n.sb("ab", [P, 2, GR, CI])
        abh = n.sb("abh", [P, 2, CI, P], F16)
        abl = n.sb("abl", [P, 2, CI, P], F16)
        zc = n.sb("zc", [P, W, CI])
        zq = n.sb("zq", [P, ZN])
        zparts = zq[:, :].bitcast(F16)
        znh, znl = zparts[:, 0:ZN], zparts[:, ZN:2 * ZN]
        zs = n.sb("zs", [P, 5, W])
        st = n.sb("st", [C, B * TILES, 6])
        gps = [n.ps(f"g{k}", [C, TILE]) for k in range(2)]
        pps = [n.ps(f"p{k}", [P, TILE]) for k in range(2)]
        zps = n.ps("z", [P, ZN])
        ops = [gps[0], gps[1], pps[0], pps[1]]

        x_in = [n.sem(f"x_in{k}") for k in range(2)]
        r_in = [n.sem(f"r_in{k}") for k in range(2)]
        stored = [n.sem(f"stored{k}") for k in range(2)]
        (hi_done, xn_done, lo_done, g_summed, g_done, p_summed, half_done, prod_done, ab_done, abh_done, abl_done,
         z_summed, z_mean, zc_done, sq_done, var_ready, root_ready, zstep, zn_done, z_turned, znh_done, znl_done,
         o_summed, o_done, x2_done, st_done, st_stored) = (
            n.sem(s) for s in (
                "hi_done", "xn_done", "lo_done", "g_summed", "g_done", "p_summed", "half_done", "prod_done",
                "ab_done", "abh_done", "abl_done", "z_summed", "z_mean", "zc_done", "sq_done", "var_ready",
                "root_ready", "zstep", "zn_done", "z_turned", "znh_done", "znl_done", "o_summed", "o_done",
                "x2_done", "st_done", "st_stored"))
        OT = JB * 4
        GPL = GR // ROWS // PT

        NB = NL // 2
        PAIRS = B * NL
        with nc.Block() as block:
            @block.sync
            def _(sp):
                SPAN = PT * TILE

                def load(i, k, reused=True):
                    if reused:
                        sp.wait_ge(hi_done, i * (2 * PT) + (k - 1) * PT)
                        sp.wait_ge(xn_done, i * (2 * PT) + (k - 1) * PT)
                    sp.dma_start(xin[:, k, :], x1[:, bass.ds(i * (2 * SPAN) + k * SPAN, SPAN)]).then_inc(x_in[k], 16)

                def load_r(i, k, reused=True):
                    if reused:
                        sp.wait_ge(x2_done, i * (2 * PT) + (k - 1) * PT)
                    sp.dma_start(xr[:, k, :], x1[:, bass.ds(i * (2 * SPAN) + k * SPAN, SPAN)]).then_inc(r_in[k], 16)

                def store(i, k):
                    sp.wait_ge(x2_done, i * (2 * PT) + (k + 1) * PT)
                    sp.dma_start(x2[:, bass.ds(i * (2 * SPAN) + k * SPAN, SPAN)], xo[:, k, :]).then_inc(stored[k], 16)

                sp.sem_inc(stored[0], 16)
                sp.sem_inc(stored[1], 16)
                load(0, 0, False)
                load(0, 1, False)
                with sp.Fori(1, NB) as i:
                    load(i, 0)
                    load(i, 1)
                load(NB, 0)
                load_r(0, 0, False)
                load(NB, 1)
                load_r(0, 1, False)
                store(0, 0)
                with sp.Fori(NB + 1, PAIRS // 2) as i:
                    load(i, 0)
                    load_r(i - NB, 0)
                    store(i - (NB + 1), 1)
                    load(i, 1)
                    load_r(i - NB, 1)
                    store(i - NB, 0)
                with sp.Fori(PAIRS // 2 - NB, PAIRS // 2) as i:
                    load_r(i, 0)
                    store(i - 1, 1)
                    load_r(i, 1)
                    store(i, 0)
                store(PAIRS // 2 - 1, 1)
                sp.wait_ge(st_done, B * TILES)
                sp.dma_start(stats2, st[:, :, :].rearrange("c (b t) s -> c b (t s)", b=B)).then_inc(st_stored, 16)
                sp.wait_ge(st_stored, 16)
                for k in range(2):
                    sp.wait_ge(stored[k], 16 * PAIRS // 2 + 16)

            @block.gpsimd
            def _(pool):
                with pool.Fori(0, B * TILES // 2) as i:
                    for u in range(2):
                        pool.wait_ge(hi_done, i * 2 + (u + 1))
                        pool.wait_ge(xn_done, i * 2 + (u + 1))
                        cols = bass.ds((i % (TILES // 2)) * (2 * TILE) + u * TILE, TILE)
                        nc.gpsimd.tensor_tensor(xl[:, cols], xn[:, u, :], xh[:, cols], ALU.subtract).then_inc(lo_done, 1)

            @block.tensor
            def _(pe):
                def products(out, parts, first=True, **kw):
                    for p, (a, b) in enumerate(parts):
                        last = nc.tensor.matmul(out, a, b, start=(first and p == 0), stop=(p == 2), **kw)
                    return last

                def project(bank, r, k, xhr, xlr):
                    return products(bank[:, r * 2 * CI:(r + 1) * 2 * CI],
                                    ((xhr, ph[:, k, :]), (xlr, ph[:, k, :]), (xhr, pl[:, k, :])), False,
                                    skip_group_check=True)

                def open_group(bank, k):
                    nc.tensor.matmul(bank[:, :], prow[:, :], pbias[:, k, :], start=True, stop=False,
                                     skip_group_check=True)

                def rows(b, i, first):
                    for tt in range(2 * PT):
                        T = b * TILES + (i * (2 * PT) + tt)
                        pe.wait_ge(lo_done, T + 1)
                        if not (first and tt < 2):
                            pe.wait_ge(g_done, T - 1)
                        at = i * (2 * PT * TILE) + tt * TILE
                        xht, xlt = xh[:, bass.ds(at, TILE)], xl[:, bass.ds(at, TILE)]
                        products(gps[tt % 2][:, :], ((gh[:, :], xht), (gh[:, :], xlt), (gl[:, :], xht))
                                 ).then_inc(g_summed, 1)
                        if tt == 0:
                            if not first:
                                pe.wait_ge(prod_done, b * (2 * NGR) + i)
                            open_group(pps[0], 0)
                        for r in range(ROWS):
                            last = project(pps[0], tt * ROWS + r, 0, xh[:, bass.ds(at + r * W, W)],
                                           xl[:, bass.ds(at + r * W, W)])
                    last.then_inc(p_summed, 1)

                def columns(b, i):
                    for u in range(2):
                        pe.wait_ge(prod_done, b * (2 * NGR) + NGR + i * 2 + (u - 1 if u == 0 else 0))
                        open_group(pps[1 - u], 1)
                        for r in range(GR):
                            w = i * (2 * GR) + (u * GR + r)
                            xhc = xh[:, :].rearrange("c (h w) -> c w h", w=W)[:, bass.ds(w, 1), :].rearrange("c a h -> c (a h)")
                            xlc = xl[:, :].rearrange("c (h w) -> c w h", w=W)[:, bass.ds(w, 1), :].rearrange("c a h -> c (a h)")
                            last = project(pps[1 - u], r, 1, xhc, xlc)
                        last.then_inc(p_summed, 1)

                def triangle(b, first):
                    pe.wait_ge(abl_done, b * (2 * NGR) + 2 * NGR)
                    if not first:
                        pe.wait_ge(znl_done, b * 4)
                    for c in range(CI):
                        last = products(zps[:, c * W:(c + 1) * W],
                                        ((abh[:, 0, c, :], abh[:, 1, c, :]), (abl[:, 0, c, :], abh[:, 1, c, :]),
                                         (abh[:, 0, c, :], abl[:, 1, c, :])))
                    last.then_inc(z_summed, 1)
                    pe.wait_ge(zn_done, b + 1)
                    zf = zc[:, :, :].rearrange("i j c -> i (j c)")
                    for q in range(4):
                        for u in range(4):
                            at = (4 * q + u) * P
                            last = nc.tensor.transpose(zps[:, at:at + P], zf[:, at:at + P], ident[:, :])
                        last.then_inc(z_turned, 1)

                def outer(b, jj, peeled):
                    for q in range(4):
                        if peeled:
                            pe.wait_ge(znl_done, b * 4 + (q + 1))
                            pe.wait_ge(g_done, b * TILES + TILES)
                        else:
                            pe.wait_ge(o_done, b * OT + jj * 4 + (q - 3))
                        w = bass.ds(jj * C, C)
                        zhf, zlf = zh[:, :, :].rearrange("p j c -> p (j c)"), zl[:, :, :].rearrange("p j c -> p (j c)")
                        cols = slice(q * TILE, (q + 1) * TILE)
                        products(ops[q][:, :], ((zhf[:, w], znh[:, cols]), (zhf[:, w], znl[:, cols]),
                                                (zlf[:, w], znh[:, cols]))).then_inc(o_summed, 1)

                def batch(b, first=False):
                    if not first:
                        pe.wait_ge(o_done, b * OT)
                    rows(b, 0, first)
                    with pe.Fori(1, NB) as i:
                        rows(b, i, False)
                    with pe.Fori(0, NB // 2) as i:
                        columns(b, i)
                    triangle(b, first)
                    outer(b, 0, True)
                    with pe.Fori(1, JB) as jj:
                        outer(b, jj, False)

                batch(0, True)
                with pe.Fori(1, B) as b:
                    batch(b)

            @block.scalar
            def _(act):
                def hi(b, i, k):
                    act.wait_ge(x_in[k], 16)
                    act.wait_ge(x_in[k], b * (16 * NB) + i * 16 + 16)
                    for u in range(PT):
                        cols = bass.ds(i * (2 * PT * TILE) + (k * PT + u) * TILE, TILE)
                        nc.scalar.activation(xh[:, cols], xin[:, k, u * TILE:(u + 1) * TILE], ACT.Identity,
                                             bias=coef[:, bass.ds(b, 1), 1:2].rearrange("c a s -> c (a s)"),
                                             scale=coef[:, bass.ds(b, 1), 0:1].rearrange("c a s -> c (a s)")
                                             ).then_inc(hi_done, 1)

                def sig(b, i, k, first):
                    for u in range(PT):
                        tt = k * PT + u
                        T = b * TILES + (i * (2 * PT) + tt)
                        act.wait_ge(g_summed, T + 1)
                        if not first:
                            act.wait_ge(x2_done, T - (TILES - 1))
                        act.wait_ge(g_summed, 1)
                        nc.scalar.activation(gate[:, bass.ds(i * (2 * PT * TILE) + tt * TILE, TILE)], gps[tt % 2][:, :],
                                             ACT.Sigmoid, bias=bgc[:, 0:1], scale=DESCALE).then_inc(g_done, 1)

                def group(n_, bank):
                    act.wait_ge(p_summed, n_ + 1)
                    v = pps[bank][:, :].rearrange("p (r s c) -> p r s c", s=2, c=CI)
                    nc.scalar.activation(half[:, bank, :, :], v[:, :, 0, :], ACT.Copy).then_inc(half_done, 1)
                    act.wait_ge(prod_done, n_ + 1)
                    nc.scalar.activation(ab[:, bank, :, :], prod[:, bank, :, :], ACT.Sigmoid, scale=DESCALE * DESCALE
                                         ).then_inc(ab_done, 1)

                def batch(b, first=False):
                    if not first:
                        act.wait_ge(p_summed, b * (2 * NGR))
                    hi(b, 0, 0)
                    hi(b, 0, 1)
                    sig(b, 0, 0, first)
                    with act.Fori(1, NB) as i:
                        hi(b, i, 0)
                        sig(b, i - 1, 1, first)
                        hi(b, i, 1)
                        group(b * (2 * NGR) + i - 1, 0)
                        sig(b, i, 0, first)
                    sig(b, NB - 1, 1, first)
                    group(b * (2 * NGR) + (NGR - 1), 0)
                    with act.Fori(0, NB // 2) as i:
                        group(b * (2 * NGR) + NGR + i * 2, 1)
                        group(b * (2 * NGR) + NGR + i * 2 + 1, 0)
                    act.wait_ge(zc_done, b + 1)
                    if not first:
                        act.wait_ge(o_summed, b * OT)
                    nc.scalar.activation(zq[:, :], zc[:, :, :].rearrange("i j c -> i (j c)"), ACT.Square
                                         ).then_inc(sq_done, 1)
                    act.wait_ge(var_ready, b + 1)
                    nc.scalar.activation(zs[:, 2, :], zs[:, 1, :], ACT.Sqrt).then_inc(root_ready, 1)
                    for q in range(4):
                        cols = slice(q * TILE, (q + 1) * TILE)
                        act.wait_ge(z_turned, b * 4 + (q + 1))
                        nc.scalar.activation(znh[:, cols], zps[:, cols], ACT.Copy, scale=SA).then_inc(znh_done, 1)

                batch(0, True)
                with act.Fori(1, B) as b:
                    batch(b)

            @block.vector
            def _(dve):
                def norm(b, i, tt, first):
                    T = b * TILES + (i * (2 * PT) + tt)
                    k, u = divmod(tt, PT)
                    if u == 0:
                        dve.wait_ge(x_in[k], b * (16 * NB) + i * 16 + 16)
                    if not (first and tt < 2):
                        dve.wait_ge(lo_done, T - 1)
                    nc.vector.tensor_scalar(xn[:, tt % 2, :], xin[:, k, u * TILE:(u + 1) * TILE],
                                            coef[:, bass.ds(b, 1), 0:1].rearrange("c a s -> c (a s)"),
                                            coef[:, bass.ds(b, 1), 1:2].rearrange("c a s -> c (a s)"),
                                            ALU.mult, ALU.add).then_inc(xn_done, 1)

                def add(b, i, tt):
                    T = b * TILES + (i * (2 * PT) + tt)
                    k, u = divmod(tt, PT)
                    if u == 0:
                        dve.wait_ge(r_in[k], b * (16 * NB) + i * 16 + 16)
                        dve.wait_ge(stored[k], b * (16 * NB) + i * 16 + 16)
                    nc.vector.scalar_tensor_tensor(xo[:, k, u * TILE:(u + 1) * TILE],
                                                   gate[:, bass.ds(i * (2 * PT * TILE) + tt * TILE, TILE)], DESCALE,
                                                   xr[:, k, u * TILE:(u + 1) * TILE], ALU.mult, ALU.add
                                                   ).then_inc(x2_done, 1)
                    dve.wait_ge(x2_done, T + 1)
                    nc.vector.bn_stats(st[:, bass.ds(T, 1), :].rearrange("c a s -> c (a s)"),
                                       xo[:, k, u * TILE:(u + 1) * TILE]).then_inc(st_done, 1)

                def group(n_, k, r0, bank):
                    dve.wait_ge(half_done, n_ + 1)
                    v = pps[bank][:, :].rearrange("p (r s c) -> p r s c", s=2, c=CI)
                    nc.vector.tensor_tensor(prod[:, bank, :, :], v[:, :, 1, :], half[:, bank, :, :], ALU.mult
                                            ).then_inc(prod_done, 1)
                    dve.wait_ge(ab_done, n_ + 1)
                    src = ab[:, bank, :, :].rearrange("p r c -> p c r")
                    nc.vector.tensor_scalar(abh[:, k, :, bass.ds(r0, GR)], src, SA, None, ALU.mult).then_inc(abh_done, 1)
                    dve.wait_ge(abh_done, n_ + 1)
                    nc.vector.scalar_tensor_tensor(abl[:, k, :, bass.ds(r0, GR)], src, SA, abh[:, k, :, bass.ds(r0, GR)],
                                                   ALU.mult, ALU.subtract).then_inc(abl_done, 1)

                def normalise(b):
                    LINKS = 9
                    count = [0]

                    def link(ins):
                        count[0] += 1
                        ins.then_inc(zstep, 1)
                        dve.wait_ge(zstep, b * LINKS + count[0])

                    dve.wait_ge(z_summed, b + 1)
                    zv = zps[:, :].rearrange("i (c j) -> i j c", j=W)
                    link(nc.vector.reduce_sum(zs[:, 0, :], zv, AX.X))
                    nc.vector.scalar_tensor_tensor(zc[:, :, :], zs[:, 0, :].unsqueeze(2).broadcast_to([P, W, CI]),
                                                   -1.0 / CI, zv, ALU.mult, ALU.add).then_inc(zc_done, 1)
                    dve.wait_ge(sq_done, b + 1)
                    link(nc.vector.reduce_sum(zs[:, 0, :], zq[:, :].rearrange("i (j c) -> i j c", c=CI), AX.X))
                    link(nc.vector.tensor_scalar(zs[:, 1, :], zs[:, 0, :], 1.0 / CI, LN_EPS * (SA * SA) ** 2,
                                                 ALU.mult, ALU.add))
                    dve.sem_inc(var_ready, 1)
                    dve.wait_ge(root_ready, b + 1)
                    link(nc.vector.reciprocal(zs[:, 3, :], zs[:, 2, :]))
                    link(nc.vector.tensor_tensor(zs[:, 4, :], zs[:, 3, :], zs[:, 3, :], ALU.mult))
                    link(nc.vector.tensor_tensor(zs[:, 4, :], zs[:, 4, :], zs[:, 1, :], ALU.mult))
                    link(nc.vector.tensor_scalar(zs[:, 4, :], zs[:, 4, :], -0.5, 1.5, ALU.mult, ALU.add))
                    link(nc.vector.tensor_tensor(zs[:, 3, :], zs[:, 3, :], zs[:, 4, :], ALU.mult))
                    link(nc.vector.tensor_tensor(zc[:, :, :], zc[:, :, :],
                                                 zs[:, 3, :].unsqueeze(2).broadcast_to([P, W, CI]), ALU.mult))
                    assert count[0] == LINKS, count[0]
                    dve.sem_inc(zn_done, 1)
                    dve.wait_ge(g_done, b * TILES + TILES)
                    for q in range(4):
                        cols = slice(q * TILE, (q + 1) * TILE)
                        dve.wait_ge(znh_done, b * 4 + (q + 1))
                        nc.vector.scalar_tensor_tensor(znl[:, cols], zps[:, cols], SA, znh[:, cols],
                                                       ALU.mult, ALU.subtract).then_inc(znl_done, 1)

                def outer(b, jj):
                    for q in range(4):
                        dve.wait_ge(o_summed, b * OT + jj * 4 + (q + 1))
                        gv = gate[:, :].rearrange("c (i g j) -> c g i j", g=W // JB, j=JB)[:, 4 * q:4 * q + 4, :,
                                                                                       bass.ds(jj, 1)
                                                                                       ].rearrange("c g i a -> c g (i a)")
                        nc.vector.scalar_tensor_tensor(gv, ops[q][:, :].rearrange("c (g i) -> c g i", i=P), bzc[:, 0:1],
                                                       gv, ALU.add, ALU.mult).then_inc(o_done, 1)

                def batch(b, first=False):
                    if not first:
                        dve.wait_ge(o_done, b * OT)

                    def tiles(i, start):
                        for tt in range(2 * PT):
                            norm(b, i, tt, first and start)
                            if not first:
                                add(b - 1, i, tt)
                            if tt == 1 and not start:
                                group(b * (2 * NGR) + i - 1, 0, i * GR - GR, 0)
                    tiles(0, True)
                    with dve.Fori(1, NB) as i:
                        tiles(i, False)
                    group(b * (2 * NGR) + (NGR - 1), 0, (NGR - 1) * GR, 0)
                    with dve.Fori(0, NB // 2) as i:
                        group(b * (2 * NGR) + NGR + i * 2, 1, i * (2 * GR), 1)
                        group(b * (2 * NGR) + NGR + i * 2 + 1, 1, i * (2 * GR) + GR, 0)
                    normalise(b)
                    with dve.Fori(0, JB) as jj:
                        outer(b, jj)

                batch(0, True)
                with dve.Fori(1, B) as b:
                    batch(b)
                dve.wait_ge(o_done, B * OT)
                with dve.Fori(0, NB) as i:
                    for tt in range(2 * PT):
                        add(B - 1, i, tt)


def stage_lstm(nc, x2, stats2, wx, wm, bias, x3, stats3):
    n = Names(nc, "lstm")
    HALF = B // 2
    N = HALF * W
    GATES = 4
    IN, CELL, FORGET, OUT = range(GATES)
    NT = H // ROWS
    SPAN = ROWS * TILE
    SPAN2 = 2 * SPAN
    with n.stack:
        coef = n.sb("coef", [C, B, 2])
        w32 = n.sb("w32", [C, 2 * GATES, C])
        wh = n.sb("wh", [C, 2 * GATES, C], F16)
        wl = n.sb("wl", [C, 2 * GATES, C], F16)
        bc = n.sb("bias", [C, GATES])
        xin = n.sb("xin", [C, 2, B, TILE])
        xn = n.sb("xn", [C, B, TILE])
        xh = n.sb("xh", [C, 2, B, TILE], F16)
        xl = n.sb("xl", [C, 2, B, TILE], F16)
        hh = n.sb("hh", [C, 2, N], F16)
        hl = n.sb("hl", [C, 2, N], F16)
        cell = n.sb("cell", [C, 2, N])
        gate = n.sb("gate", [C, 2, GATES, N])
        ig = n.sb("ig", [C, 2, N])
        tc = n.sb("tanh_c", [C, 2, N])
        h = n.sb("h", [C, 2, 2, N])
        xres = n.sb("xres", [C, 2, ROWS, TILE])
        xout = n.sb("xout", [C, 2, ROWS, TILE])
        st = n.sb("st", [C, B * TILES, 6])
        group_norm_coefficients(nc, n, stats2, coef, SA)
        w_in, w_hi, setup = (n.sem(x) for x in ("w_in", "w_hi", "setup"))
        with nc.Block() as block:
            @block.sync
            def _(sp):
                for g in range(GATES):
                    sp.dma_start(w32[:, g, :], wx[g]).then_inc(w_in, 16)
                    sp.dma_start(w32[:, GATES + g, :], wm[g]).then_inc(w_in, 16)
                    sp.dma_start(bc[:, g:g + 1], bias[g].rearrange("a h -> h a")).then_inc(w_in, 16)
                sp.wait_ge(w_in, 16 * 3 * GATES)

            @block.vector
            def _(dve):
                nc.vector.memset(hh[:, :, :], 0.0)
                nc.vector.memset(hl[:, :, :], 0.0)
                nc.vector.memset(cell[:, :, :], 0.0)
                dve.wait_ge(w_in, 16 * 3 * GATES)
                split_weights(nc, dve, w_hi, 1, w32[:, :, :], wh[:, :, :], wl[:, :, :]).then_inc(setup, 1)

        z = [[n.ps(f"z{q}{s}", [C, GATES * N]) for s in range(2)] for q in range(2)]
        x_in = [n.sem(f"x_in{k}") for k in range(2)]
        res_in = [n.sem(f"res_in{k}") for k in range(2)]
        hi_done = n.sem("x_hi_done")
        xn_done = n.sem("xn_done")
        xl_done = n.sem("xl_done")
        z_first = [n.sem(f"z_first{q}") for q in range(2)]
        z_second = [n.sem(f"z_second{q}") for q in range(2)]
        g_first = [n.sem(f"g_first{q}") for q in range(2)]
        g_forget = [n.sem(f"g_forget{q}") for q in range(2)]
        g_out = [n.sem(f"g_out{q}") for q in range(2)]
        ig_done = [n.sem(f"ig_done{q}") for q in range(2)]
        fc_done = [n.sem(f"fc_done{q}") for q in range(2)]
        c_ready = [n.sem(f"c_ready{q}") for q in range(2)]
        tc_ready = [n.sem(f"tc_ready{q}") for q in range(2)]
        h_done = [n.sem(f"h_done{q}") for q in range(2)]
        hh_done = [n.sem(f"hh_done{q}") for q in range(2)]
        h_ready = [n.sem(f"h_ready{q}") for q in range(2)]
        x3_rows = n.sem("x3_rows")
        st_done = n.sem("st_done")
        stored = [n.sem(f"stored{k}") for k in range(2)]
        st_stored = n.sem("st_stored")
        x2_t = x2.rearrange("c (b t) -> c b t", b=B)
        GATE_W = {IN: 0, FORGET: 1, OUT: 2, CELL: 3}

        with nc.Block() as block:
            @block.sync
            def _(sp):
                def load_x(i, k, reused=True):
                    if reused:
                        sp.wait_ge(xn_done, (i * 2 + (k - 1)) * B)
                        sp.wait_ge(hi_done, (i * 2 + (k - 1)) * B)
                    sp.dma_start(xin[:, k, :, :], x2_t[:, :, bass.ds(i * (2 * TILE) + k * TILE, TILE)]
                                 ).then_inc(x_in[k], 16)

                def load_res(i, k):
                    sp.dma_start(xres[:, k, :, :], x2[:, bass.ds(i * SPAN2 + k * SPAN, SPAN)]).then_inc(res_in[k], 16)

                def store(i, k):
                    sp.wait_ge(x3_rows, i * (4 * ROWS) + (k + 1) * 2 * ROWS)
                    sp.dma_start(x3[:, bass.ds(i * SPAN2 + k * SPAN, SPAN)], xout[:, k, :, :]
                                 ).then_inc(stored[k], 16)

                for k in range(2):
                    load_x(0, k, False)
                    load_res(0, k)
                with sp.Fori(0, NT // 2 - 1) as i:
                    for k in range(2):
                        load_x(i + 1, k)
                        store(i, k)
                        load_res(i + 1, k)
                store(NT // 2 - 1, 0)
                store(NT // 2 - 1, 1)
                sp.wait_ge(st_done, B * NT)
                sp.dma_start(stats3, st[:, :, :].rearrange("c (b t) s -> c b (t s)", b=B)).then_inc(st_stored, 16)
                sp.wait_ge(st_stored, 16)
                for k in range(2):
                    sp.wait_ge(stored[k], 16 * NT // 2)

            @block.tensor
            def _(pe):
                def x_part(k, r, q):
                    hi = xh[:, k, q * HALF:(q + 1) * HALF, r * W:(r + 1) * W]
                    lo = xl[:, k, q * HALF:(q + 1) * HALF, r * W:(r + 1) * W]
                    for g in range(GATES):
                        w = GATE_W[g]
                        for p, (a, b) in enumerate(((wh, hi), (wh, lo), (wl, hi))):
                            nc.tensor.matmul(z[q][r % 2][:, g * N:(g + 1) * N], a[:, w, :], b,
                                             start=(g % 2 == 0 and p == 0), stop=False, skip_group_check=True)

                def h_part(t, r, q, wait=True):
                    def product(g, a, b):
                        return nc.tensor.matmul(z[q][r % 2][:, g * N:(g + 1) * N], a[:, GATES + GATE_W[g], :], b[:, q, :],
                                                start=False, stop=True, skip_group_check=True)

                    if wait:
                        pe.wait_ge(hh_done[q], t)
                    for g in (IN, CELL):
                        product(g, wh, hh)
                        product(g, wl, hh)
                    if wait:
                        pe.wait_ge(h_ready[q], t)
                    product(IN, wh, hl)
                    product(CELL, wh, hl).then_inc(z_first[q], 1)
                    for g in (FORGET, OUT):
                        product(g, wh, hh)
                        product(g, wl, hh)
                        last = product(g, wh, hl)
                    last.then_inc(z_second[q], 1)

                def tile(i, k, first=False, last=False):
                    for r in range(ROWS):
                        t = i * (2 * ROWS) + (k * ROWS + r)
                        for q in range(2):
                            h_part(t, r, q, not (first and r == 0))
                            if r < ROWS - 1:
                                x_part(k, r + 1, q)
                            elif not last:
                                if q == 0:
                                    pe.wait_ge(xl_done, i * (2 * B) + (k + 2) * B)
                                x_part(1 - k, 0, q)

                pe.wait_ge(xl_done, B)
                x_part(0, 0, 0)
                x_part(0, 0, 1)
                tile(0, 0, first=True)
                tile(0, 1)
                with pe.Fori(1, NT // 2 - 1) as i:
                    tile(i, 0)
                    tile(i, 1)
                tile(NT // 2 - 1, 0)
                tile(NT // 2 - 1, 1, last=True)

            @block.scalar
            def _(act):
                def gate_fn(q, s, g, fn):
                    return nc.scalar.activation(gate[:, q, g, :], z[q][s][:, g * N:(g + 1) * N], fn,
                                                bias=bc[:, GATE_W[g]:GATE_W[g] + 1], scale=DESCALE)

                def norm(i, k, b):
                    if b == 0:
                        act.wait_ge(x_in[k], i * 16 + 16)
                    nc.scalar.activation(xh[:, k, b, :], xin[:, k, b, :], ACT.Identity, bias=coef[:, b, 1:2],
                                         scale=coef[:, b, 0:1]).then_inc(hi_done, 1)

                def tile(i, k, last=False):
                    for r in range(ROWS):
                        t, s = i * (2 * ROWS) + (k * ROWS + r), r % 2
                        for q in range(2):
                            act.wait_ge(z_first[q], t + 1)
                            gate_fn(q, s, IN, ACT.Sigmoid)
                            gate_fn(q, s, CELL, ACT.Tanh).then_inc(g_first[q], 1)
                            act.wait_ge(z_second[q], t + 1)
                            gate_fn(q, s, FORGET, ACT.Sigmoid).then_inc(g_forget[q], 1)
                            gate_fn(q, s, OUT, ACT.Sigmoid).then_inc(g_out[q], 1)
                            act.wait_ge(c_ready[q], t + 1)
                            nc.scalar.activation(tc[:, q, :], cell[:, q, :], ACT.Tanh).then_inc(tc_ready[q], 1)
                            if r < 2 and not last:
                                norm(i + (k == 1), 1 - k, 2 * r + q)

                act.preload_act_table_set("sigmoid_and_others")
                for b in range(B):
                    norm(0, 0, b)
                with act.Fori(0, NT // 2 - 1) as i:
                    tile(i, 0)
                    tile(i, 1)
                tile(NT // 2 - 1, 0)
                tile(NT // 2 - 1, 1, last=True)

            @block.vector
            def _(dve):
                def norm(i, k, b, used=True):
                    if b == 0:
                        dve.wait_ge(x_in[k], i * 16 + 16)
                    if used:
                        dve.wait_ge(xl_done, (i * 2 + (k - 1)) * B + (b + 1))
                    nc.vector.tensor_scalar(xn[:, b, :], xin[:, k, b, :], coef[:, b, 0:1], coef[:, b, 1:2],
                                            ALU.mult, ALU.add).then_inc(xn_done, 1)

                def stat(i, k, r):
                    dve.wait_ge(x3_rows, i * (4 * ROWS) + (k * ROWS + r + 1) * 2)
                    nc.vector.bn_stats(st[:, bass.ds(i * (2 * ROWS) + (k * ROWS + r), 1), :].rearrange("c a s -> c (a s)"),
                                       xout[:, k, r, :]).then_inc(st_done, 1)

                def tile(i, k, first=False, last=False):
                    for r in range(ROWS):
                        t = i * (2 * ROWS) + (k * ROWS + r)
                        s = r % 2
                        for q in range(2):
                            dve.wait_ge(g_first[q], t + 1)
                            nc.vector.tensor_tensor(ig[:, q, :], gate[:, q, IN, :], gate[:, q, CELL, :],
                                                    ALU.mult).then_inc(ig_done[q], 1)
                            dve.wait_ge(g_forget[q], t + 1)
                            nc.vector.tensor_tensor(cell[:, q, :], gate[:, q, FORGET, :], cell[:, q, :],
                                                    ALU.mult).then_inc(fc_done[q], 1)
                            dve.wait_ge(ig_done[q], t + 1)
                            dve.wait_ge(fc_done[q], t + 1)
                            nc.vector.tensor_tensor(cell[:, q, :], cell[:, q, :], ig[:, q, :],
                                                    ALU.add).then_inc(c_ready[q], 1)
                            if r < 2 and not last:
                                norm(i + (k == 1), 1 - k, 2 * r + q)
                            if r >= 2 and not first:
                                stat(i - (k == 0), 1 - k, 2 * (r - 2) + q)
                            dve.wait_ge(tc_ready[q], t + 1)
                            dve.wait_ge(g_out[q], t + 1)
                            if not (first and r < 2):
                                dve.wait_ge(x3_rows, (t - 2) * 2 + (q + 1))
                            nc.vector.scalar_tensor_tensor(hh[:, q, :], gate[:, q, OUT, :], SA, tc[:, q, :],
                                                           ALU.mult, ALU.mult).then_inc(hh_done[q], 1)
                            nc.vector.tensor_tensor(h[:, q, s, :], gate[:, q, OUT, :], tc[:, q, :],
                                                    ALU.mult).then_inc(h_done[q], 1)
                            dve.wait_ge(hh_done[q], t + 1)
                            dve.wait_ge(h_done[q], t + 1)
                            nc.vector.scalar_tensor_tensor(hl[:, q, :], h[:, q, s, :], SA, hh[:, q, :],
                                                           ALU.mult, ALU.subtract).then_inc(h_ready[q], 1)

                for b in range(B):
                    norm(0, 0, b, used=False)
                tile(0, 0, first=True)
                tile(0, 1)
                with dve.Fori(1, NT // 2 - 1) as i:
                    tile(i, 0)
                    tile(i, 1)
                tile(NT // 2 - 1, 0)
                tile(NT // 2 - 1, 1, last=True)
                for r in range(ROWS):
                    stat(NT // 2 - 1, 1, r)

            @block.gpsimd
            def _(pool):
                def split(i, k, b):
                    pool.wait_ge(hi_done, (i * 2 + k) * B + (b + 1))
                    pool.wait_ge(xn_done, (i * 2 + k) * B + (b + 1))
                    nc.gpsimd.tensor_tensor(xl[:, k, b, :], xn[:, b, :], xh[:, k, b, :],
                                            ALU.subtract).then_inc(xl_done, 1)

                def tile(i, k, first=False, last=False, reused=True):
                    for r in range(ROWS):
                        t = i * (2 * ROWS) + (k * ROWS + r)
                        for q in range(2):
                            cols = slice(q * N, (q + 1) * N)
                            pool.wait_ge(h_done[q], t + 1)
                            if r == 0 and q == 0 and reused:
                                pool.wait_ge(stored[k], i * 16)
                                pool.wait_ge(st_done, (i * 2 + (k - 1)) * B)
                            if r == 0 and q == 0:
                                pool.wait_ge(res_in[k], i * 16 + 16)
                            nc.gpsimd.tensor_tensor(xout[:, k, r, cols], h[:, q, r % 2, :], xres[:, k, r, cols],
                                                    ALU.add).then_inc(x3_rows, 1)
                            if r < 2 and not last:
                                split(i + (k == 1), 1 - k, 2 * r + q)

                for b in range(B):
                    split(0, 0, b)
                tile(0, 0, first=True, reused=False)
                tile(0, 1, reused=False)
                with pool.Fori(1, NT // 2 - 1) as i:
                    tile(i, 0)
                    tile(i, 1)
                tile(NT // 2 - 1, 0)
                tile(NT // 2 - 1, 1, last=True)


TAPS = 9
PAD = TAPS // 2


def stage_rowconv(nc, x3, stats3, w_conv, out):
    n = Names(nc, "rc")
    PADW = W + 2 * PAD
    HALF = B // 2
    NEW_SCALE = SA * SW
    with n.stack:
        coef = n.sb("coef", [C, B, 2])
        ident = n.sb("ident", [P, P])
        w32 = n.sb("w32", [C, TAPS, C])
        wh = n.sb("wh", [C, TAPS, C], F16)
        wl = n.sb("wl", [C, TAPS, C], F16)
        xin = n.sb("xin", [C, 2, B, TILE])
        rowx = n.sb("rowx", [C, 2, B, TILE])
        ch = n.sb("carry_hi", [C, 2, HALF, PADW], F16)
        cl = n.sb("carry_lo", [C, 2, HALF, PADW], F16)
        new = n.sb("new", [C, 2, 2, HALF, W])
        fin = n.sb("fin", [C, 2, B, W])
        ot = n.sb("ot", [P, 4, B, C])
        group_norm_coefficients(nc, n, stats3, coef, NEW_SCALE)
        (w_in, w_hi, setup, ident_ready) = (n.sem(x) for x in ("w_in", "w_hi", "setup", "ident_ready"))
        with nc.Block() as block:
            @block.sync
            def _(sp):
                sp.dma_start(w32[:, :, :], w_conv.rearrange("k i o -> i k o")).then_inc(w_in, 16)

            @block.gpsimd
            def _(pool):
                nc.gpsimd.memset(ident[:, :], 0.0).then_inc(ident_ready, 1)
                pool.wait_ge(ident_ready, 1)
                nc.gpsimd.affine_select(out=ident[:, :], in_=ident[:, :], compare_op=ALU.not_equal, fill=1.0,
                                        base=0, pattern=[[-1, P]], channel_multiplier=1).then_inc(ident_ready, 1)

            @block.vector
            def _(dve):
                nc.vector.memset(ch[:, :, :, :], 0.0)
                nc.vector.memset(cl[:, :, :, :], 0.0)
                dve.wait_ge(w_in, 16)
                nc.vector.tensor_scalar(wh[:, :, :], w32[:, :, :], SW, None, ALU.mult).then_inc(w_hi, 1)
                dve.wait_ge(w_hi, 1)
                nc.vector.scalar_tensor_tensor(wl[:, :, :], w32[:, :, :], SW, wh[:, :, :],
                                               ALU.mult, ALU.subtract).then_inc(setup, 1)

        conv_ps = [n.ps(f"conv{k}", [C, 512]) for k in range(2)]
        tr_ps = [n.ps(f"tr{k}", [P, 512]) for k in range(2)]
        x_in = [n.sem(f"x_in{k}") for k in range(2)]
        x_used = n.sem("x_used")
        row_ready = n.sem("row_ready")
        conv_done = [n.sem(f"conv_done{k}") for k in range(2)]
        new_ready = [n.sem(f"new_ready{k}") for k in range(2)]
        hi_ready = [n.sem(f"hi_ready{k}") for k in range(2)]
        carry_ready = [n.sem(f"carry_ready{k}") for k in range(2)]
        fin_ready = n.sem("fin_ready")
        turned = n.sem("turned")
        turned_copied = n.sem("turned_copied")
        stored = [n.sem(f"stored{k}") for k in range(4)]
        NT = H // ROWS
        x3_t = x3.rearrange("c (b t) -> c b t", b=B)
        out_t = out.rearrange("b h w c -> w b h c")

        with nc.Block() as block:
            @block.sync
            def _(sp):
                for k in range(2):
                    sp.dma_start(xin[:, k, :, :], x3_t[:, :, k * TILE:(k + 1) * TILE]).then_inc(x_in[k], 16)
                with sp.Fori(1, NT // 2) as i:
                    for k in range(2):
                        sp.wait_ge(x_used, i * 2 + (k - 1))
                        sp.dma_start(xin[:, k, :, :], x3_t[:, :, bass.ds(i * (2 * TILE) + k * TILE, TILE)]).then_inc(x_in[k], 16)

            @block.tensor
            def _(pe):
                def conv(t, k):
                    if t is not None:
                        pe.wait_ge(carry_ready[k], t)
                    for tap in range(TAPS):
                        for part, (w, c) in enumerate(((wh, ch), (wh, cl), (wl, ch))):
                            last = nc.tensor.matmul(conv_ps[k][:, 0:HALF * W], w[:, tap, :],
                                                    c[:, k, :, tap:tap + W],
                                                    start=(tap == 0 and part == 0),
                                                    stop=(tap == TAPS - 1 and part == 2))
                    last.then_inc(conv_done[k], 1)

                def turn(t, slot, reused=True):
                    pe.wait_ge(fin_ready, t + 1)
                    if reused:
                        pe.wait_ge(turned_copied, t - 1)
                    for b in range(B):
                        last = nc.tensor.transpose(tr_ps[slot][:, b * C:(b + 1) * C], fin[:, slot, b, :], ident[:, :])
                    last.then_inc(turned, 1)

                for t in range(4):
                    conv(t or None, 0)
                    conv(t or None, 1)
                    if t:
                        turn(t - 1, (t - 1) % 2, t > 2)
                with pe.Fori(2, H // 2) as i:
                    for r in range(2):
                        conv(i * 2 + r, 0)
                        conv(i * 2 + r, 1)
                        turn(i * 2 + (r - 1), 1 - r)
                turn(H - 1, 1)

            @block.vector
            def _(dve):
                def tile(i, k, first):
                    dve.wait_ge(x_in[k], i * 16 + 16)
                    for b in range(B):
                        last = nc.vector.tensor_scalar(rowx[:, k, b, :], xin[:, k, b, :], coef[:, b, 0:1],
                                                       coef[:, b, 1:2], ALU.mult, ALU.add)
                    last.then_inc(row_ready, 1)
                    dve.wait_ge(row_ready, i * 2 + (k + 1))
                    for r in range(ROWS):
                        t = i * (2 * ROWS) + (k * ROWS + r)
                        s = r % 2
                        cols = slice(r * W, (r + 1) * W)
                        for q in range(2):
                            bs = slice(q * HALF, (q + 1) * HALF)
                            dve.wait_ge(conv_done[q], t + 1)
                            nc.vector.scalar_tensor_tensor(
                                new[:, s, q, :, :], conv_ps[q][:, 0:HALF * W].rearrange("c (b w) -> c b w", b=HALF),
                                0.0, rowx[:, k, bs, cols], ALU.max, ALU.add).then_inc(new_ready[q], 1)
                            dve.wait_ge(new_ready[q], t + 1)
                            nc.vector.tensor_scalar(ch[:, q, :, PAD:PAD + W], new[:, s, q, :, :], SA / NEW_SCALE,
                                                    None, ALU.mult).then_inc(hi_ready[q], 1)
                            dve.wait_ge(hi_ready[q], t + 1)
                            nc.vector.scalar_tensor_tensor(
                                cl[:, q, :, PAD:PAD + W], new[:, s, q, :, :], SA / NEW_SCALE,
                                ch[:, q, :, PAD:PAD + W], ALU.mult, ALU.subtract).then_inc(carry_ready[q], 1)
                        if not (first and r < 2):
                            dve.wait_ge(turned, t - 1)
                        last = nc.vector.scalar_tensor_tensor(
                            fin[:, s, :, :], new[:, s, :, :, :].rearrange("c q b w -> c (q b) w"), 1.0 / NEW_SCALE,
                            xin[:, k, :, cols], ALU.mult, ALU.add)
                        last.then_inc(fin_ready, 1)
                    dve.wait_ge(fin_ready, i * (2 * ROWS) + (k + 1) * ROWS)
                    dve.sem_inc(x_used, 1)

                tile(0, 0, True)
                tile(0, 1, False)
                with dve.Fori(1, NT // 2) as i:
                    tile(i, 0, False)
                    tile(i, 1, False)

            @block.scalar
            def _(act):
                def rows4(i, first):
                    for r in range(4):
                        t = i * 4 + r
                        act.wait_ge(turned, t + 1)
                        if not first:
                            act.wait_ge(stored[r], i * 16)
                        nc.scalar.activation(ot[:, r, :, :].rearrange("w b c -> w (b c)"), tr_ps[r % 2][:, :],
                                             ACT.Copy).then_inc(turned_copied, 1)
                        act.wait_ge(turned_copied, t + 1)
                        act.dma_start(out_t[:, :, bass.ds(t, 1), :].rearrange("w b h c -> w (b h) c"), ot[:, r, :, :]).then_inc(stored[r], 16)

                rows4(0, True)
                with act.Fori(1, H // 4) as i:
                    rows4(i, False)
                for r in range(4):
                    act.wait_ge(stored[r], 16 * (H // 4))


def conv_preact_stack(nc, a, out):
    scratch = lambda name, shape, dt=F32: nc.dram_tensor(name, shape, dt, kind="Internal").ap()
    taps = scratch("taps", (PER, C, 2 * SUMS * PER), F16)
    coef0 = scratch("coef0", (NCG, QG * B * 2))
    hf = scratch("hf", (C, B * PLANE))
    x1, x2, x3 = (scratch(f"x{k}", (C, B * PLANE)) for k in (1, 2, 3))
    stats1, stats2, stats3 = (scratch(f"stats{k}", (C, B, TILES * 6)) for k in (1, 2, 3))
    l0, l1, l2 = (lambda s, p=p: a[f"{p}_conv_{s}"] for p in ("L0", "L1", "L2"))
    stage_taps(nc, l0("B_kernel"), l0("gate_B_kernel"), taps)
    stage_depthwise(nc, a["x"], taps, coef0, hf)
    stage_origin(nc, a["x"], l0("A_kernel"), l0("gate_A_kernel"),
                 coef0.rearrange("n (g b s) -> (n g) b s", g=QG, b=B), hf)
    stage_mix(nc, a["x"], hf, l0("W_out"), l0("b_out"), x1, stats1)
    stage_triangle(nc, x1, stats1, (l1("Wa1"), l1("Wa2")), (l1("ba1"), l1("ba2")), (l1("Wb1"), l1("Wb2")),
                   (l1("bb1"), l1("bb2")), l1("ln2_g"), l1("ln2_b"), l1("Wg"), l1("bg"), l1("Wz"), l1("bz"), x2, stats2)
    stage_lstm(nc, x2, stats2, [l2(f"W{g}x") for g in "ifoc"], [l2(f"W{g}m") for g in "ifoc"],
               [l2(f"b{g}") for g in "ifoc"], x3, stats3)
    stage_rowconv(nc, x3, stats3, a["L3_conv_W"], out)


def kernel(**inputs):
    import numpy as _np
    import concourse.bacc as _bacc
    from concourse import mybir as _mybir
    from concourse.bass_utils import run_bass_kernel_spmd as _run

    nc = _bacc.Bacc("TRN2", target_bir_lowering=False, num_devices=1)
    arrays, aps = {}, {}
    for name, value in inputs.items():
        array = _np.ascontiguousarray(value)
        arrays[f"in_{name}_dram"] = array
        aps[name] = nc.dram_tensor(f"in_{name}_dram", array.shape, _mybir.dt.from_np(array.dtype),
                                   kind="ExternalInput").ap()
    out = nc.dram_tensor("out_dram", (B, H, W, C), F32, kind="ExternalOutput").ap()
    conv_preact_stack(nc, aps, out)
    r = _run(nc, [arrays], core_ids=[0])
    return r.results[0]["out_dram"]
```

```python
import concourse.bass as bass
import concourse.mybir as mybir
from contextlib import ExitStack

F32 = mybir.dt.float32
F16 = mybir.dt.float16
ALU = mybir.AluOpType
ACT = mybir.ActivationFunctionType
AX = mybir.AxisListType

B, H, W, C = 4, 128, 128, 128
P = 128
PLANE = H * W
TILE = 512
ROWS = TILE // W
TILES = PLANE // TILE
GROUP = 4
GN_EPS = 1e-5

SA = 64.0
SW = 64.0
DESCALE = 1.0 / (SA * SW)


class Names:

    def __init__(self, nc, stage):
        self.nc, self.stage, self.stack, self.sems = nc, stage, ExitStack(), []
        self.stack.callback(self.clear)

    def sb(self, name, shape, dt=F32):
        return self.stack.enter_context(self.nc.sbuf_tensor(f"{self.stage}_{name}", shape, dt))

    def ps(self, name, shape, dt=F32):
        return self.stack.enter_context(self.nc.psum_tensor(f"{self.stage}_{name}", shape, dt))

    def sem(self, name):
        self.sems.append(self.nc.alloc_semaphore(f"{self.stage}_{name}"))
        return self.sems[-1]

    def clear(self):
        if self.sems:
            self.nc.clear_and_free_semaphores(self.sems)
            self.nc.all_engine_barrier()


def group_matrix(nc, pool, zeros_done, g):
    nc.gpsimd.memset(g[:, :], 1.0 / GROUP).then_inc(zeros_done, 1)
    pool.wait_ge(zeros_done, 1)
    v = g[:, :].rearrange("c (q r) -> c q r", r=GROUP)
    nc.gpsimd.affine_select(out=v, in_=v, compare_op=ALU.is_ge, fill=0.0, base=0,
                            pattern=[[-GROUP, P // GROUP], [0, GROUP]], channel_multiplier=1).then_inc(zeros_done, 1)
    pool.wait_ge(zeros_done, 2)
    nc.gpsimd.affine_select(out=v, in_=v, compare_op=ALU.is_ge, fill=0.0, base=GROUP - 1,
                            pattern=[[GROUP, P // GROUP], [0, GROUP]], channel_multiplier=-1).then_inc(zeros_done, 1)


def group_norm_coefficients(nc, n, stats, coef, gain, first_loads):
    own = Names(nc, n.stage)
    with own.stack:
        st = own.sb("gn_st", [C, B, TILES * 6])
        mv = own.sb("gn_mv", [C, B, 2])
        mom = own.sb("gn_mom", [C, 2, B])
        mg = own.sb("gn_mg", [C, 2, B])
        t = own.sb("gn_t", [C, 6, B])
        g = own.sb("gn_group", [C, C])
        pm = own.ps("gn_pm", [C, 512])
        loaded, group_ready, moments, averaged, var_ready, root_ready, step = (
            n.sem(f"gn_{x}") for x in ("loaded", "group_ready", "moments", "averaged", "var_ready", "root_ready", "step"))

        with nc.Block() as block:
            @block.sync
            def _(sp):
                sp.dma_start(st[:, :, :], stats).then_inc(loaded, 16)
                first_loads(sp)

            @block.gpsimd
            def _(pool):
                group_matrix(nc, pool, group_ready, g)

            @block.tensor
            def _(pe):
                pe.wait_ge(group_ready, 3)
                pe.wait_ge(moments, 1)
                nc.tensor.matmul(pm[:, 0:2 * B], g[:, :], mom[:, :, :].rearrange("c a b -> c (a b)"),
                                 start=True, stop=True).then_inc(averaged, 1)

            @block.scalar
            def _(act):
                act.wait_ge(var_ready, 1)
                nc.scalar.activation(t[:, 2, :], t[:, 1, :], ACT.Sqrt).then_inc(root_ready, 1)

            @block.vector
            def _(dve):
                done = [0]

                def link(ins):
                    done[0] += 1
                    ins.then_inc(step, 1)
                    dve.wait_ge(step, done[0])

                dve.wait_ge(loaded, 16)
                for b in range(B):
                    last = nc.vector.bn_aggr(mv[:, b, :], st[:, b, :])
                link(last)
                nc.vector.tensor_copy(mom[:, 0, :], mv[:, :, 0])
                link(nc.vector.tensor_tensor(t[:, 0, :], mv[:, :, 0], mv[:, :, 0], ALU.mult))
                nc.vector.tensor_tensor(mom[:, 1, :], t[:, 0, :], mv[:, :, 1], ALU.add).then_inc(moments, 1)
                dve.wait_ge(averaged, 1)
                rsqrt_and_shift(nc, link, lambda ins: ins.then_inc(var_ready, 1), lambda: dve.wait_ge(root_ready, 1),
                                pm[:, 0:B], pm[:, B:2 * B], mg, t,
                                coef[:, :, 0], coef[:, :, 1], gain, GN_EPS)


def rsqrt_and_shift(nc, link, to_root, from_root, mean_ps, second_ps, mg, t, scale_out, shift_out, gain, eps):
    link(nc.vector.tensor_copy(mg[:, 0, :], mean_ps))
    link(nc.vector.tensor_tensor(t[:, 0, :], mg[:, 0, :], mg[:, 0, :], ALU.mult))
    link(nc.vector.scalar_tensor_tensor(t[:, 1, :], second_ps, eps, t[:, 0, :], ALU.add, ALU.subtract))
    to_root(nc.vector.tensor_copy(t[:, 0, :], t[:, 1, :]))
    from_root()
    link(nc.vector.reciprocal(t[:, 3, :], t[:, 2, :]))
    link(nc.vector.tensor_tensor(t[:, 4, :], t[:, 3, :], t[:, 3, :], ALU.mult))
    link(nc.vector.tensor_tensor(t[:, 5, :], t[:, 4, :], t[:, 1, :], ALU.mult))
    link(nc.vector.tensor_scalar(t[:, 4, :], t[:, 5, :], -0.5 * gain, 1.5 * gain, ALU.mult, ALU.add))
    link(nc.vector.tensor_tensor(scale_out, t[:, 4, :], t[:, 3, :], ALU.mult))
    link(nc.vector.scalar_tensor_tensor(shift_out, mg[:, 0, :], -1.0, scale_out, ALU.mult, ALU.mult))


def split_weights(nc, dve, hi_ready, count, w32, wh, wl):
    nc.vector.tensor_scalar(wh, w32, SW, None, ALU.mult).then_inc(hi_ready, 1)
    dve.wait_ge(hi_ready, count)
    return nc.vector.scalar_tensor_tensor(wl, w32, SW, wh, ALU.mult, ALU.subtract)


KS = 7
R = KS // 2
STEPS = 8
EPS0 = 1e-6
S0 = 1.0 - 0.5 ** STEPS


SIDE = 2 * KS - 1


def around(side):
    return [(H - side // 2, 0, side // 2), (0, side // 2, side // 2 + 1)]


def stage_origin(nc, raw, gsum, ka, coef0, hf):
    n = Names(nc, "org")
    with n.stack:
        a32 = n.sb("a32", [C, KS, KS])
        co = n.sb("co", [C, B, 2])
        v = n.sb("v", [C, 6, B, KS, KS])
        sp_ = n.sb("sp", [C, 2, B, KS, KS])
        (in_w, in_h, done, sig_go, sig_done, ready, stored) = (
            n.sem(s) for s in ("in_w", "in_h", "done", "sig_go", "sig_done", "ready", "stored"))
        hf_t = hf.rearrange("c (b h w) -> c b h w", b=B, h=H)
        near = around(KS)
        with nc.Block() as block:
            @block.sync
            def _(sp):
                for r in range(GROUP):
                    sp.dma_start(co[r:C:GROUP, :, :], coef0).then_inc(in_w, 16)
                sp.dma_start(a32[:, :, :], ka).then_inc(in_w, 16)
                for h0, r0, hn in near:
                    for w0, c0, wn in near:
                        for b in range(B):
                            sp.dma_start(sp_[:, 0, b, r0:r0 + hn, c0:c0 + wn], hf_t[:, b, h0:h0 + hn, w0:w0 + wn]
                                         ).then_inc(in_h, 16)
                sp.wait_ge(ready, 1)
                for h0, r0, hn in near:
                    for w0, c0, wn in near:
                        for b in range(B):
                            sp.dma_start(hf_t[:, b, h0:h0 + hn, w0:w0 + wn], sp_[:, 1, b, r0:r0 + hn, c0:c0 + wn]
                                         ).then_inc(stored, 16)
                sp.wait_ge(stored, 16 * 4 * B)

            @block.scalar
            def _(act):
                f = lambda k: v[:, k, :, :, :].rearrange("c b i j -> c (b i j)")
                act.wait_ge(sig_go, 1)
                nc.scalar.activation(f(1), f(0), ACT.Sigmoid).then_inc(sig_done, 1)
                act.wait_ge(sig_go, 2)
                nc.scalar.activation(f(3), f(2), ACT.Sigmoid).then_inc(sig_done, 1)
                nc.scalar.activation(f(4), f(2), ACT.Sigmoid, scale=-1.0).then_inc(sig_done, 1)

            @block.vector
            def _(dve):
                count = [0]

                def link(ins):
                    count[0] += 1
                    ins.then_inc(done, 1)
                    dve.wait_ge(done, count[0])

                full = raw[:, :, :].rearrange("c (j b) i -> c b i j", b=B)
                dve.wait_ge(in_w, 16 * (1 + GROUP))
                link(nc.vector.tensor_scalar(v[:, 5, 0, 0, 0:B], co[:, :, 1], gsum[:, :], 1.0 / SA, ALU.mult, ALU.mult))
                link(nc.vector.tensor_scalar(v[:, 5, 0, 1, 0:B], co[:, :, 0], 1.0 / SA, None, ALU.mult))
                for b in range(B):
                    last = nc.vector.tensor_scalar(v[:, 0, b, :, :], full[:, b, :, :], v[:, 5, 0, 1, b:b + 1],
                                                   v[:, 5, 0, 0, b:b + 1], ALU.mult, ALU.add)
                link(last)
                dve.sem_inc(sig_go, 1)
                dve.wait_ge(sig_done, 1)
                for b in range(B):
                    last = nc.vector.tensor_tensor(v[:, 2, b, :, :], v[:, 1, b, :, :], a32[:, :, :], ALU.mult)
                link(last)
                dve.sem_inc(sig_go, 1)
                dve.wait_ge(sig_done, 3)
                f = lambda k: v[:, k, :, :, :].rearrange("c b i j -> c (b i j)")
                s, c, t, u = f(3), f(4), f(5), f(0)
                link(nc.vector.scalar_tensor_tensor(t, c, 1.0, s, ALU.add, ALU.mult))
                link(nc.vector.tensor_tensor(u, c, c, ALU.mult))
                link(nc.vector.scalar_tensor_tensor(s, u, 1.0, t, ALU.add, ALU.mult))
                link(nc.vector.tensor_tensor(c, u, u, ALU.mult))
                link(nc.vector.scalar_tensor_tensor(t, c, 1.0, s, ALU.add, ALU.mult))
                link(nc.vector.tensor_scalar(u, t, 1.0 / S0, None, ALU.mult))
                dve.wait_ge(in_h, 16 * 4 * B)
                g = lambda k: sp_[:, k, :, :, :].rearrange("c b i j -> c (b i j)")
                link(nc.vector.scalar_tensor_tensor(t, g(0), EPS0, u, ALU.add, ALU.mult))
                nc.vector.tensor_scalar(g(1), t, -EPS0, None, ALU.add).then_inc(ready, 1)


def stage_mix(nc, x, hf, w_out, b_out, x1, stats1):
    n = Names(nc, "mix")
    PAIR = 2 * TILE
    NP = B * PLANE // PAIR
    SUB = PAIR // P
    with n.stack:
        w32 = n.sb("w32", [C, C])
        wh = n.sb("wh", [C, C], F16)
        wl = n.sb("wl", [C, C], F16)
        ident = n.sb("ident", [P, P])
        eps = n.sb("eps", [C, 1])
        bo = n.sb("bo", [C, 1])
        bias = n.sb("bias", [C, 1])
        ws = n.sb("ws", [C, C])
        w_in, ws_ready, w_hi, ident_ready, summed = (n.sem(s) for s in ("w_in", "ws_ready", "w_hi", "ident_ready", "summed"))
        own = Names(nc, "mixw")
        with own.stack:
            pb = own.ps("pb", [C, TILE])
            with nc.Block() as block:
                @block.sync
                def _(sp):
                    sp.dma_start(w32[:, :], w_out).then_inc(w_in, 16)
                    sp.dma_start(bo[:, :], b_out.rearrange("(c a) -> c a", a=1)).then_inc(w_in, 16)

                @block.gpsimd
                def _(pool):
                    nc.gpsimd.memset(ident[:, :], 0.0).then_inc(ident_ready, 1)
                    pool.wait_ge(ident_ready, 1)
                    nc.gpsimd.affine_select(out=ident[:, :], in_=ident[:, :], compare_op=ALU.not_equal, fill=SA * SW,
                                            base=0, pattern=[[-1, P]], channel_multiplier=1).then_inc(ident_ready, 1)

                @block.tensor
                def _(pe):
                    pe.wait_ge(ws_ready, 2)
                    nc.tensor.matmul(pb[:, 0:1], ws[:, :], eps[:, :], start=True, stop=True).then_inc(summed, 1)

                @block.vector
                def _(dve):
                    nc.vector.memset(eps[:, :], EPS0).then_inc(ws_ready, 1)
                    dve.wait_ge(w_in, 32)
                    nc.vector.tensor_scalar(ws[:, :], w32[:, :], S0, None, ALU.mult).then_inc(ws_ready, 1)
                    dve.wait_ge(ws_ready, 2)
                    split_weights(nc, dve, w_hi, 1, ws[:, :], wh[:, :], wl[:, :])
                    dve.wait_ge(summed, 1)
                    nc.vector.tensor_tensor(bias[:, :], pb[:, 0:1], bo[:, :], ALU.add)

        xin = n.sb("xin", [P, 2, SUB, C])
        hin = n.sb("hin", [C, 2, PAIR])
        hh = n.sb("hh", [C, 2, PAIR], F16)
        hl = n.sb("hl", [C, 2, PAIR], F16)
        xo = n.sb("xo", [C, 2, PAIR])
        st = n.sb("st", [C, B * TILES, 6])
        acc = [n.ps(f"acc{k}", [C, TILE]) for k in range(4)]
        x_in = [n.sem(f"x_in{k}") for k in range(2)]
        h_in = [n.sem(f"h_in{k}") for k in range(2)]
        stored = [n.sem(f"stored{k}") for k in range(2)]
        hi_done, lo_done, acc_done, out_done, st_done, st_stored = (
            n.sem(s) for s in ("hi_done", "lo_done", "acc_done", "out_done", "st_done", "st_stored"))
        x_t = x.rearrange("b h w c -> (b h w) c").rearrange("(t s p) c -> p t s c", p=P, s=SUB)
        with nc.Block() as block:
            @block.sync
            def _(sp):
                def load(i, k):
                    sp.dma_start(xin[:, k, :, :], x_t[:, bass.ds(i * 2 + k, 1), :, :].rearrange("p a s c -> p (a s) c")
                                 ).then_inc(x_in[k], 16)
                    sp.dma_start(hin[:, k, :], hf[:, bass.ds(i * (2 * PAIR) + k * PAIR, PAIR)]).then_inc(h_in[k], 16)

                load(0, 0)
                load(0, 1)
                with sp.Fori(1, NP // 2) as i:
                    for k in range(2):
                        sp.wait_ge(acc_done, i * 4 + (2 * k - 2))
                        sp.wait_ge(lo_done, i * 4 + (2 * k - 2))
                        load(i, k)

            @block.scalar
            def _(act):
                def split(i, k):
                    act.wait_ge(h_in[k], i * 16 + 16)
                    for u in range(2):
                        nc.scalar.activation(hh[:, k, u * TILE:(u + 1) * TILE], hin[:, k, u * TILE:(u + 1) * TILE],
                                             ACT.Copy, scale=SA).then_inc(hi_done, 1)

                def leave(i, k, first):
                    if not first:
                        act.wait_ge(stored[k], i * 16)
                        act.wait_ge(st_done, i * 4 + (2 * k - 2))
                    for u in range(2):
                        act.wait_ge(acc_done, i * 4 + (2 * k + u + 1))
                        nc.scalar.activation(xo[:, k, u * TILE:(u + 1) * TILE], acc[2 * k + u][:, :], ACT.Identity,
                                             bias=bias[:, 0:1], scale=DESCALE).then_inc(out_done, 1)
                    act.wait_ge(out_done, i * 4 + (2 * k + 2))
                    act.dma_start(x1[:, bass.ds(i * (2 * PAIR) + k * PAIR, PAIR)], xo[:, k, :]).then_inc(stored[k], 16)

                split(0, 0)
                split(0, 1)
                leave(0, 0, True)
                act.wait_ge(acc_done, 2)
                split(1, 0)
                leave(0, 1, True)
                with act.Fori(1, NP // 2 - 1) as i:
                    act.wait_ge(acc_done, i * 4)
                    split(i, 1)
                    leave(i, 0, False)
                    act.wait_ge(acc_done, i * 4 + 2)
                    split(i + 1, 0)
                    leave(i, 1, False)
                i = NP // 2 - 1
                act.wait_ge(acc_done, i * 4)
                split(i, 1)
                leave(i, 0, False)
                leave(i, 1, False)
                act.wait_ge(st_done, B * TILES)
                act.dma_start(stats1, st[:, :, :].rearrange("c (b t) s -> c b (t s)", b=B)).then_inc(st_stored, 16)
                act.wait_ge(st_stored, 16)
                act.wait_ge(stored[0], 16 * NP // 2)
                act.wait_ge(stored[1], 16 * NP // 2)

            @block.vector
            def _(dve):
                def rest(i, k):
                    for u in range(2):
                        cols = slice(u * TILE, (u + 1) * TILE)
                        dve.wait_ge(hi_done, i * 4 + (2 * k + u + 1))
                        nc.vector.scalar_tensor_tensor(hl[:, k, cols], hin[:, k, cols], SA, hh[:, k, cols],
                                                       ALU.mult, ALU.subtract).then_inc(lo_done, 1)

                def stat(i, k):
                    for u in range(2):
                        dve.wait_ge(out_done, i * 4 + (2 * k + u + 1))
                        nc.vector.bn_stats(st[:, bass.ds(i * 4 + 2 * k + u, 1), :].rearrange("c a s -> c (a s)"),
                                           xo[:, k, u * TILE:(u + 1) * TILE]).then_inc(st_done, 1)

                rest(0, 0)
                with dve.Fori(0, NP // 2 - 1) as i:
                    rest(i, 1)
                    stat(i, 0)
                    rest(i + 1, 0)
                    stat(i, 1)
                rest(NP // 2 - 1, 1)
                stat(NP // 2 - 1, 0)
                stat(NP // 2 - 1, 1)

            @block.tensor
            def _(pe):
                def pair(i, k, first):
                    pe.wait_ge(x_in[k], i * 16 + 16)
                    for u in range(2):
                        cols = slice(u * TILE, (u + 1) * TILE)
                        if not first:
                            pe.wait_ge(out_done, i * 4 + (2 * k + u - 3))
                        for s in range(TILE // P):
                            nc.tensor.matmul(acc[2 * k + u][:, s * P:(s + 1) * P], xin[:, k, u * (TILE // P) + s, :],
                                             ident[:, :], start=(s == 0), stop=False, skip_group_check=True)
                        pe.wait_ge(lo_done, i * 4 + (2 * k + u + 1))
                        for a, b in ((wh, hh), (wh, hl), (wl, hh)):
                            last = nc.tensor.matmul(acc[2 * k + u][:, :], a[:, :], b[:, k, cols], start=False,
                                                    stop=(a is wl), skip_group_check=True)
                        last.then_inc(acc_done, 1)

                pair(0, 0, True)
                pair(0, 1, True)
                with pe.Fori(1, NP // 2) as i:
                    pair(i, 0, False)
                    pair(i, 1, False)


QUADS = C // GROUP
CG = 32
QG = CG // GROUP
NCG = C // CG
PER = 8
SUMS = 2 * KS
WP = W + 2 * R


def load_channels(eng, x, xg, x_in, cg, piece):
    b, half = divmod(piece, 2)
    cols = slice(half * (W // 2), (half + 1) * (W // 2))
    eng.dma_start(xg[:, bass.ds((cg % 2) * B + b, 1), cols, :].rearrange("h a w c -> h (a w) c"),
                  x.rearrange("b h w c -> h b w c")[:, b, cols, bass.ds(cg * CG, CG)]).then_inc(x_in[b], 16)


def stage_ahead(nc, x, kb, kg, kga, taps, xg, x_in, taps_stored, raw, gsum):
    n = Names(nc, "ahd")
    M = B * SIDE
    with n.stack:
        k32 = n.sb("k32", [C, 2, KS, KS])
        dbl = n.sb("dbl", [C, 2, 2, KS, 2 * PER], F16)
        rot = n.sb("rot", [C, PER, 2 * SUMS, PER], F16)
        xp = n.sb("xp", [M, SIDE, C])
        ident = n.sb("ident", [P, P])
        ga = n.sb("ga", [C, KS * KS])
        pat = n.sb("pat", [C, SIDE * B, SIDE])
        acc = n.sb("acc", [C, KS * B, KS])
        SPLIT = TILE // M
        pt = n.ps("pt", [C, 2 * TILE])
        k_in, cleared, hi_done, lo_done, rotated, in_x, in_w, ident_ready, turned, done = (
            n.sem(s) for s in ("k_in", "cleared", "hi_done", "lo_done", "rotated", "in_x", "in_w", "ident_ready",
                               "turned", "done"))
        with nc.Block() as block:
            @block.sync
            def _(sp):
                sp.dma_start(k32[:, 0, :, :], kg).then_inc(k_in, 16)
                sp.dma_start(k32[:, 1, :, :], kb).then_inc(k_in, 16)
                sp.dma_start(ga[:, :], kga.rearrange("c i j -> c (i j)")).then_inc(in_w, 16)
                for b in range(B):
                    for h0, r0, hn in around(SIDE):
                        for w0, c0, wn in around(SIDE):
                            sp.dma_start(xp[b * SIDE + r0:b * SIDE + r0 + hn, c0:c0 + wn, :],
                                         x[b, h0:h0 + hn, w0:w0 + wn, :]).then_inc(in_x, 16)
                for piece in range(B):
                    load_channels(sp, x, xg, x_in, 0, piece)
                sp.wait_ge(rotated, 1)
                sp.dma_start(taps.rearrange("p c n -> c p n"), rot[:, :, :, :].rearrange("c p n m -> c p (n m)")
                             ).then_inc(taps_stored, 16)
                for piece in range(B, 2 * B):
                    load_channels(sp, x, xg, x_in, 0, piece)

            @block.gpsimd
            def _(pool):
                nc.gpsimd.memset(ident[:, :], 0.0).then_inc(ident_ready, 1)
                pool.wait_ge(ident_ready, 1)
                nc.gpsimd.affine_select(out=ident[:, :], in_=ident[:, :], compare_op=ALU.not_equal, fill=1.0,
                                        base=0, pattern=[[-1, P]], channel_multiplier=1).then_inc(ident_ready, 1)

            @block.tensor
            def _(pe):
                pe.wait_ge(ident_ready, 2)
                pe.wait_ge(in_x, 16 * 4 * B)
                for k in range(SIDE):
                    at = k * M if k < SPLIT else TILE + (k - SPLIT) * M
                    last = nc.tensor.transpose(pt[:, at:at + M], xp[:, k, :], ident[0:M, 0:M])
                last.then_inc(turned, 1)

            @block.vector
            def _(dve):
                count = [0]

                def link(ins):
                    count[0] += 1
                    ins.then_inc(done, 1)
                    dve.wait_ge(done, count[0])

                nc.vector.memset(dbl[:, :, :, :, :], 0.0).then_inc(cleared, 1)
                dve.wait_ge(cleared, 1)
                dve.wait_ge(k_in, 32)
                for k in range(2):
                    src = k32[:, k, :, :].rearrange("c i j -> c j i")
                    last = nc.vector.tensor_scalar(dbl[:, 0, k, :, 0:KS], src, SW, None, ALU.mult)
                last.then_inc(hi_done, 1)
                dve.wait_ge(hi_done, 1)
                for k in range(2):
                    src = k32[:, k, :, :].rearrange("c i j -> c j i")
                    last = nc.vector.scalar_tensor_tensor(dbl[:, 1, k, :, 0:KS], src, SW, dbl[:, 0, k, :, 0:KS],
                                                          ALU.mult, ALU.subtract)
                last.then_inc(lo_done, 1)
                dve.wait_ge(lo_done, 1)
                d = dbl[:, :, :, :, :].rearrange("c a k j m -> c (a k j) m")
                nc.vector.tensor_copy(d[:, :, PER:2 * PER], d[:, :, 0:PER]).then_inc(lo_done, 1)
                dve.wait_ge(lo_done, 2)
                for p in range(PER):
                    s = (R - p) % PER
                    last = nc.vector.tensor_copy(rot[:, p, :, :], d[:, :, s:s + PER])
                last.then_inc(rotated, 1)
                dve.wait_ge(in_w, 16)
                nc.vector.reduce_sum(gsum[:, :], ga[:, :], AX.X)
                dve.wait_ge(turned, 1)
                pf = pat[:, :, :].rearrange("c m s -> c (m s)")
                nc.vector.tensor_copy(pf[:, 0:SPLIT * M], pt[:, 0:SPLIT * M])
                link(nc.vector.tensor_copy(pf[:, SPLIT * M:SIDE * M], pt[:, TILE:TILE + (SIDE - SPLIT) * M]))
                bufs = (raw, acc)
                for i in range(KS):
                    for j in range(KS):
                        k = i * KS + j
                        win = pat[:, (KS - 1 - j) * B:(SIDE - j) * B, KS - 1 - i:SIDE - i]
                        if k == 0:
                            link(nc.vector.tensor_scalar(bufs[0][:, :, :], win, ga[:, 0:1], None, ALU.mult))
                        else:
                            link(nc.vector.scalar_tensor_tensor(bufs[k % 2][:, :, :], win, ga[:, k:k + 1],
                                                                bufs[1 - k % 2][:, :, :], ALU.mult, ALU.add))


def stage_depthwise(nc, x, xg, x_in, taps, taps_stored, coef0, hf):
    n = Names(nc, "dw")
    with n.stack:
        xn = n.sb("xn", [H, GROUP, B, W])
        xh = n.sb("xh", [H, 2, GROUP, B, WP], F16)
        xl = n.sb("xl", [H, 2, GROUP, B, WP], F16)
        vt = n.sb("v", [H, 2, GROUP, 2 * SUMS, PER], F16)
        circ = n.sb("circ", [H, 2, 2 * SUMS, H], F16)
        mask = n.sb("mask", [H, H], F16)
        mk = n.sb("mk", [H, 3, H])
        ones = n.sb("ones", [H, H])
        e = n.sb("e", [H, 2, B * W])
        bt = n.sb("bt", [H, 2, B * W])
        ln = n.sb("ln", [H, 2, B * W])
        so = n.sb("so", [H, 2, B * W])
        NG = QG * B
        bs = n.sb("bs", [H, NG, 6])
        mom = n.sb("mom", [H, 2, NG])
        sq = n.sb("sq", [H, 3, NG])
        mg = n.sb("mg", [H, 2, NG])
        t = n.sb("t", [H, 6, NG])
        coef = n.sb("coef", [H, NG, 2])
        gate_ps = [n.ps(f"gate{k}", [H, B * W]) for k in range(2)]
        val_ps = [n.ps(f"val{k}", [H, B * W]) for k in range(2)]
        pm = n.ps("pm", [H, TILE])
        v_in = [n.sem(f"v_in{k}") for k in range(2)]
        stored = [n.sem(f"stored{k}") for k in range(2)]
        (mask_parts, mask_ready, xn_done, hi_done, lo_done, xh_wrapped, xl_wrapped, circ_ready, gate_done, val_done, e_ready,
         cap_done, sig_done, bt_done, abs_done, lge_done, exp_done, ln_done, so_ready, stats_step, moments, averaged,
         var_ready, root_ready, coef_ready, coef_stored) = (
            n.sem(s) for s in (
                "mask_parts", "mask_ready", "xn_done", "hi_done", "lo_done", "xh_wrapped", "xl_wrapped", "circ_ready", "gate_done",
                "val_done", "e_ready", "cap_done", "sig_done", "bt_done", "abs_done", "lge_done", "exp_done", "ln_done",
                "so_ready", "stats_step", "moments", "averaged", "var_ready", "root_ready", "coef_ready",
                "coef_stored"))
        hf_t = hf.rearrange("c (b h w) -> h c b w", b=B, h=H)
        PERQ = GROUP
        LINKS = 5 + 9

        with nc.Block() as block:
            @block.sync
            def _(sp):
                def load_x(cg, piece):
                    load_channels(sp, x, xg, x_in, cg, piece)

                def load_v(q, s):
                    src = taps[:, bass.ds(q * GROUP, GROUP), :].rearrange("p c n -> p (c n)")
                    sp.dma_start(vt[:, s, :, :, :].rearrange("p c n m -> p (c n m)"),
                                 src.partition_broadcast(H // PER)).then_inc(v_in[s], 16)

                def store_coef(cg):
                    sp.wait_ge(coef_ready, cg + 1)
                    sp.dma_start(coef0[bass.ds(cg, 1), :], coef[0:1, :, :].rearrange("p g s -> p (g s)")
                                 ).then_inc(coef_stored, 16)

                def body(cg, first=False, ahead=True, last=False):
                    for g in range(QG):
                        if not (last and g == QG - 1):
                            if not (first and g == 0):
                                sp.wait_ge(circ_ready, cg * CG + g * PERQ)
                            load_v(cg * QG + (g + 1), (g + 1) % 2)
                        if g == QG - 1 and ahead:
                            sp.wait_ge(xn_done, (cg + 1) * (QG * B))
                            sp.wait_ge(hi_done, (cg + 1) * (QG * B))
                        for r in range(PERQ):
                            c = cg * CG + (g * PERQ + r)
                            sp.wait_ge(so_ready, c + 1)
                            sp.dma_start(hf_t[:, bass.ds(c, 1), :, :].rearrange("h a b w -> h (a b) w"),
                                         so[:, r % 2, :].rearrange("h (b w) -> h b w", b=B)).then_inc(stored[r % 2], 16)
                            if g == QG - 1 and ahead:
                                load_x(cg + 2, r)
                            if g == 0 and not first and not last:
                                load_x(cg + 1, PERQ + r)
                        if g == QG - 1 and not last:
                            store_coef(cg + 1)

                sp.wait_ge(taps_stored, 16)
                load_v(0, 0)
                for b in range(B):
                    sp.wait_ge(x_in[b], 32)
                for piece in range(2 * B):
                    load_x(1, piece)
                store_coef(0)
                body(0, first=True)
                with sp.Fori(1, NCG - 2) as cg:
                    body(cg)
                body(NCG - 2, ahead=False)
                body(NCG - 1, ahead=False, last=True)
                for k in range(2):
                    sp.wait_ge(stored[k], 16 * C // 2)
                sp.wait_ge(coef_stored, 16 * NCG)

            @block.gpsimd
            def _(pool):
                nc.gpsimd.memset(mk[:, :, :], 1.0).then_inc(mask_parts, 1)
                pool.wait_ge(mask_parts, 1)
                nc.gpsimd.affine_select(out=mk[:, 0, :], in_=mk[:, 0, :], compare_op=ALU.is_ge, fill=0.0, base=R,
                                        pattern=[[1, H]], channel_multiplier=-1).then_inc(mask_parts, 1)
                nc.gpsimd.affine_select(out=mk[:, 1, :], in_=mk[:, 1, :], compare_op=ALU.is_ge, fill=0.0,
                                        base=-(H - R), pattern=[[-1, H]], channel_multiplier=1).then_inc(mask_parts, 1)
                nc.gpsimd.affine_select(out=mk[:, 2, :], in_=mk[:, 2, :], compare_op=ALU.is_ge, fill=0.0,
                                        base=-(H - R), pattern=[[1, H]], channel_multiplier=-1).then_inc(mask_parts, 1)
                pool.wait_ge(mask_parts, 4)
                nc.gpsimd.affine_select(out=mk[:, 0, :], in_=mk[:, 0, :], compare_op=ALU.is_ge, fill=0.0, base=R,
                                        pattern=[[-1, H]], channel_multiplier=1).then_inc(mask_parts, 1)

                def split(q, s):
                    for b in range(B):
                        pool.wait_ge(hi_done, q * B + (b + 1))
                        pool.wait_ge(xn_done, q * B + (b + 1))
                        nc.gpsimd.tensor_tensor(xl[:, s, :, b, R:R + W], xn[:, :, b, :], xh[:, s, :, b, R:R + W],
                                                ALU.subtract).then_inc(lo_done, 1)
                    rest = lambda at, src: nc.gpsimd.tensor_tensor(
                        xl[:, s, :, :, at:at + R], xn[:, :, :, src:src + R], xh[:, s, :, :, R + src:2 * R + src],
                        ALU.subtract)
                    rest(0, W - R)
                    rest(R + W, 0).then_inc(xl_wrapped, 1)

                with pool.Fori(0, QUADS // 2) as i:
                    split(i * 2, 0)
                    split(i * 2 + 1, 1)

            @block.tensor
            def _(pe):
                def channel(c, s, u, k, reused):
                    pe.wait_ge(circ_ready, c + 1)
                    if reused:
                        pe.wait_ge(bt_done, c - 1)
                    for kern, ps, done in ((0, gate_ps, gate_done), (1, val_ps, val_done)):
                        for j in range(KS):
                            hi = circ[:, k, kern * KS + j, :]
                            lo = circ[:, k, SUMS + kern * KS + j, :]
                            cols = slice(KS - 1 - j, KS - 1 - j + W)
                            for p, (a, b) in enumerate(((hi, xh), (hi, xl), (lo, xh))):
                                last = nc.tensor.matmul(ps[k][:, :], a, b[:, s, u, :, cols],
                                                        start=(j == 0 and p == 0), stop=(j == KS - 1 and p == 2))
                        last.then_inc(done, 1)

                def average(cg):
                    pe.wait_ge(moments, cg + 1)
                    nc.tensor.matmul(pm[:, 0:2 * NG], ones[:, :], mom[:, :, :].rearrange("h a g -> h (a g)"),
                                     start=True, stop=True).then_inc(averaged, 1)

                def quad(q, s, first=False, avg=None):
                    pe.wait_ge(xh_wrapped, q + 1)
                    pe.wait_ge(xl_wrapped, q + 1)
                    for u in range(PERQ):
                        channel(q * PERQ + u, s, u, u % 2, not (first and u < 2))
                        if avg is not None and u == 2:
                            average(avg)

                average(0)
                def load(cg, first=False, last=False):
                    for g in range(QG):
                        quad(cg * QG + g, g % 2, first and g == 0, cg + 1 if g == QG - 2 and not last else None)
                load(0, first=True)
                with pe.Fori(1, NCG - 1) as cg:
                    load(cg)
                load(NCG - 1, last=True)

            @block.scalar
            def _(act):
                def norm(q, slot, g, s):
                    for b in range(B):
                        k = g * B + b
                        nc.scalar.activation(xh[:, s, :, b, R:R + W],
                                             xg[:, bass.ds(slot * B + b, 1), :, g * GROUP:(g + 1) * GROUP
                                                ].rearrange("h a w c -> h c (a w)"),
                                             ACT.Identity, bias=coef[:, k, 1:2], scale=coef[:, k, 0:1]
                                             ).then_inc(hi_done, 1)
                    act.wait_ge(hi_done, (q + 1) * B)
                    rows = xh[:, s, :, :, :].rearrange("h c b w -> h (c b) w")
                    nc.scalar.activation(rows[:, :, 0:R], rows[:, :, W:W + R], ACT.Copy)
                    nc.scalar.activation(rows[:, :, W + R:WP], rows[:, :, R:2 * R], ACT.Copy).then_inc(xh_wrapped, 1)

                def gate(c, k):
                    act.wait_ge(gate_done, c + 1)
                    nc.scalar.activation(e[:, k, :], gate_ps[k][:, :], ACT.Exp, scale=-DESCALE).then_inc(e_ready, 1)

                def sigmoid(c, k):
                    act.wait_ge(cap_done, c + 1)
                    nc.scalar.activation(e[:, k, :], e[:, k, :], ACT.Ln, bias=1.0).then_inc(lge_done, 1)
                    act.wait_ge(lge_done, c + 1)
                    nc.scalar.activation(e[:, k, :], e[:, k, :], ACT.Exp, scale=-1.0).then_inc(sig_done, 1)

                def log1p(c, k):
                    act.wait_ge(bt_done, c + 1)
                    nc.scalar.activation(ln[:, k, :], bt[:, k, :], ACT.Abs).then_inc(abs_done, 1)
                    act.wait_ge(abs_done, c + 1)
                    nc.scalar.activation(ln[:, k, :], ln[:, k, :], ACT.Exp, scale=-1.0).then_inc(exp_done, 1)
                    act.wait_ge(exp_done, c + 1)
                    nc.scalar.activation(ln[:, k, :], ln[:, k, :], ACT.Ln, bias=1.0).then_inc(ln_done, 1)

                def root(cg):
                    act.wait_ge(var_ready, cg + 1)
                    nc.scalar.activation(t[:, 2, :], t[:, 1, :], ACT.Sqrt).then_inc(root_ready, 1)
                    act.preload_act_table_set("natural_log_exp_and_others")

                def body(cg, first=False, last=False):
                    for g in range(QG):
                        for r in range(PERQ):
                            c = cg * CG + (g * PERQ + r)
                            if r == 1 and not (last and g == QG - 1):
                                q = cg * QG + (g + 1)
                                if not (first and g == 0):
                                    act.wait_ge(val_done, (q - 1) * PERQ)
                                if g == QG - 1:
                                    act.wait_ge(coef_ready, cg + 2)
                                norm(q, (cg + (g == QG - 1)) % 2, (g + 1) % QG, (g + 1) % 2)
                            gate(c, r % 2)
                            if g == QG - 2 and r == 2 and not last:
                                root(cg + 1)
                            sigmoid(c, r % 2)
                            log1p(c, r % 2)

                root(0)
                act.wait_ge(coef_ready, 1)
                norm(0, 0, 0, 0)
                body(0, first=True)
                with act.Fori(1, NCG - 1) as cg:
                    body(cg)
                body(NCG - 1, last=True)

            @block.vector
            def _(dve):
                def stat(cg, slot, k):
                    b, g = divmod(k, QG)
                    if g == 0:
                        dve.wait_ge(x_in[b], cg * 32 + 32)
                    k = g * B + b
                    nc.vector.bn_stats(bs[:, k, :], xg[:, bass.ds(slot * B + b, 1), :, g * GROUP:(g + 1) * GROUP
                                                       ].rearrange("h a w c -> h (a w) c")).then_inc(stats_step, 1)

                def coefficients(cg):
                    base = cg * (NG + LINKS) + NG
                    count = [0]

                    def link(ins):
                        count[0] += 1
                        ins.then_inc(stats_step, 1)
                        dve.wait_ge(stats_step, base + count[0])

                    dve.wait_ge(stats_step, base)
                    me, mo, ve, vo = bs[:, :, 1], bs[:, :, 4], bs[:, :, 2], bs[:, :, 5]
                    link(nc.vector.tensor_tensor(mom[:, 0, :], me, mo, ALU.add))
                    nc.vector.tensor_tensor(sq[:, 0, :], me, me, ALU.mult)
                    nc.vector.tensor_tensor(sq[:, 1, :], mo, mo, ALU.mult)
                    link(nc.vector.tensor_tensor(sq[:, 2, :], ve, vo, ALU.add))
                    link(nc.vector.tensor_tensor(sq[:, 0, :], sq[:, 0, :], sq[:, 1, :], ALU.add))
                    link(nc.vector.scalar_tensor_tensor(mom[:, 1, :], sq[:, 2, :], 1.0 / (W * GROUP // 2), sq[:, 0, :],
                                                        ALU.mult, ALU.add))
                    nc.vector.tensor_copy(mg[:, 1, 0:1], mom[:, 1, 0:1]).then_inc(moments, 1)
                    dve.wait_ge(averaged, cg + 1)
                    rsqrt_and_shift(nc, link, lambda ins: ins.then_inc(var_ready, 1),
                                    lambda: dve.wait_ge(root_ready, cg + 1), pm[:, 0:NG], pm[:, NG:2 * NG], mg, t,
                                    coef[:, :, 0], coef[:, :, 1], SA, GN_EPS)
                    link(nc.vector.tensor_copy(mg[:, 1, 0:1], mom[:, 1, 0:1]))
                    assert count[0] == LINKS, count[0]
                    dve.sem_inc(coef_ready, 1)

                def norm(q, slot, g, b):
                    nc.vector.tensor_scalar(xn[:, :, b, :],
                                            xg[:, bass.ds(slot * B + b, 1), :, g * GROUP:(g + 1) * GROUP
                                               ].rearrange("h a w c -> h c (a w)"),
                                            coef[:, g * B + b, 0:1], coef[:, g * B + b, 1:2],
                                            ALU.mult, ALU.add).then_inc(xn_done, 1)

                def circulants(s, u, k):
                    taps_ = vt[:, s, u, :, :].unsqueeze(2).broadcast_to([H, 2 * SUMS, H // PER, PER])
                    m = mask[:, :].rearrange("h (a m) -> h a m", m=PER).unsqueeze(1).broadcast_to(
                        [H, 2 * SUMS, H // PER, PER])
                    nc.vector.tensor_tensor(circ[:, k, :, :].rearrange("h n (a m) -> h n a m", m=PER), taps_, m,
                                            ALU.mult).then_inc(circ_ready, 1)

                def cap(c, k):
                    dve.wait_ge(e_ready, c + 1)
                    nc.vector.tensor_scalar(e[:, k, :], e[:, k, :], 2.0 ** 60, None, ALU.min).then_inc(cap_done, 1)

                def value(c, k):
                    dve.wait_ge(val_done, c + 1)
                    dve.wait_ge(sig_done, c + 1)
                    nc.vector.scalar_tensor_tensor(bt[:, k, :], val_ps[k][:, :], DESCALE, e[:, k, :],
                                                   ALU.mult, ALU.mult).then_inc(bt_done, 1)

                def softplus(c, k, reused):
                    dve.wait_ge(ln_done, c + 1)
                    if reused is not None:
                        dve.wait_ge(stored[k], reused)
                    nc.vector.scalar_tensor_tensor(so[:, k, :], bt[:, k, :], 0.0, ln[:, k, :], ALU.max, ALU.add
                                                   ).then_inc(so_ready, 1)

                def body(cg, first=False, last=False):
                    nslot = (cg + 1) % 2
                    for g in range(QG):
                        for r in range(PERQ):
                            start, end = first and g == 0 and r == 0, last and g == QG - 1 and r == PERQ - 1
                            c = cg * CG + (g * PERQ + r)
                            if not start:
                                value(c - 1, (r + 1) % 2)
                            if not end:
                                if r == PERQ - 1:
                                    s = (g + 1) % 2
                                    dve.wait_ge(v_in[s], (cg * (QG // 2) + (g + 1) // 2) * 16 + 16)
                                if not start:
                                    dve.wait_ge(val_done, c)
                                circulants((g + (r == PERQ - 1)) % 2, (r + 1) % PERQ, (r + 1) % 2)
                            if not start:
                                early = first and g == 0 and r < 3
                                softplus(c - 1, (r + 1) % 2,
                                         None if early else (cg * (CG // 2) + (g * PERQ + r - 1) // 2) * 16)
                            if r == 3:
                                cap(c, 1)
                            if r < 2 and not (last and g == QG - 1):
                                q = cg * QG + (g + 1)
                                for b in (2 * r, 2 * r + 1):
                                    dve.wait_ge(xl_wrapped, q)
                                    norm(q, (cg + (g == QG - 1)) % 2, (g + 1) % QG, b)
                            if r < 3:
                                cap(c, r % 2)
                            if not last and 2 <= g < 6:
                                for k in range(2):
                                    stat(cg + 1, nslot, ((g - 2) * PERQ + r) * 2 + k)
                            if not last and g == 6 and r == 2:
                                dve.wait_ge(hi_done, (cg + 1) * (QG * B))
                                dve.wait_ge(coef_stored, cg * 16 + 16)
                                coefficients(cg + 1)

                nc.vector.memset(ones[:, :], 1.0 / (2 * H))
                dve.wait_ge(mask_parts, 5)
                nc.vector.tensor_tensor(mk[:, 1, :], mk[:, 1, :], mk[:, 2, :], ALU.add).then_inc(mask_ready, 1)
                dve.wait_ge(mask_ready, 1)
                nc.vector.tensor_tensor(mask[:, :], mk[:, 0, :], mk[:, 1, :], ALU.add).then_inc(mask_ready, 1)
                dve.wait_ge(mask_ready, 2)
                for k in range(NG):
                    stat(0, 0, k)
                coefficients(0)
                for b in range(B):
                    norm(0, 0, 0, b)
                dve.wait_ge(v_in[0], 16)
                circulants(0, 0, 0)
                body(0, first=True)
                with dve.Fori(1, NCG - 1) as cg:
                    body(cg)
                body(NCG - 1, last=True)
                value(C - 1, 1)
                softplus(C - 1, 1, 16 * (C // 2 - 1))


CI = 16
LN_EPS = 1e-5
JB = P // CI


def halves_of(v):
    return v.rearrange("c (m r) -> c m r", m=2)


def plane_tile(v, i, tt):
    return halves_of(v[:, bass.ds(i * (4 * TILE), 4 * TILE)])[:, :, tt * TILE // 2:(tt + 1) * TILE // 2]


def slot_tile(v, k, u):
    return halves_of(v[:, k, :])[:, :, u * TILE // 2:(u + 1) * TILE // 2]


def stage_triangle(nc, x1, stats1, wa, ba, wb, bb, ln_g, ln_b, wg, bg, wz, bz, x2, stats2):
    n = Names(nc, "tri")
    PT = 2
    NL = TILES // PT
    GR = 16
    NGR = H // GR
    ZN = CI * W
    with n.stack:
        coef = n.sb("coef", [C, B, 2])
        ident = n.sb("ident", [P, P])
        gh = n.sb("gh", [C, C], F16)
        gl = n.sb("gl", [C, C], F16)
        ph = n.sb("ph", [C, 2, 2 * CI], F16)
        pl = n.sb("pl", [C, 2, 2 * CI], F16)
        pbias = n.sb("pbias", [P, 2, 2 * CI], F16)
        prow = n.sb("prow", [P, P], F16)
        zh = n.sb("zh", [P, JB, C], F16)
        zl = n.sb("zl", [P, JB, C], F16)
        bgc = n.sb("bg", [C, 1])
        bzc = n.sb("bz", [C, 1])
        xin = n.sb("xin", [C, 2, PT * TILE])
        x_in = [n.sem(f"x_in{k}") for k in range(2)]

        own = Names(nc, "triw")
        with own.stack:
            g32 = own.sb("g32", [C, C])
            p32 = own.sb("p32", [C, 2, 2 * CI])
            b32 = own.sb("b32", [1, 2, 2 * CI])
            bh = own.sb("bh", [1, 2, 2 * CI], F16)
            bl = own.sb("bl", [1, 2, 2 * CI], F16)
            rep = own.sb("rep", [P, C])
            lng = own.sb("lng", [P, 1])
            wz32 = own.sb("wz32", [CI, C])
            lnb = own.sb("lnb", [CI, 1])
            bzi = own.sb("bzi", [C, 1])
            mask = own.sb("mask", [P, JB])
            blk = own.sb("blk", [P, JB, C])
            pz = own.ps("pz", [C, TILE])
            w_in, made, step, summed, moved = (own.sem(s) for s in ("w_in", "made", "step", "summed", "moved"))
            LOADS = 5 + 8 + 2 * JB
            STEPS = 11

            def dram_tiles(v, i, k):
                rows = halves_of(v[:, bass.ds(i * (4 * TILE), 4 * TILE)])
                return rows[:, :, k * TILE:(k + 1) * TILE]

            def first_loads(sp):
                loads = [(g32[:, :], wg), (bgc[:, :], bg.rearrange("(c a) -> c a", a=1)), (wz32[:, :], wz),
                         (lnb[:, :], ln_b.rearrange("(c a) -> c a", a=1)),
                         (bzi[:, :], bz.rearrange("(c a) -> c a", a=1))]
                for k, (ws, bs) in enumerate(((wa, ba), (wb, bb))):
                    for u in range(2):
                        loads.append((p32[:, k, u * CI:(u + 1) * CI], ws[u]))
                        loads.append((b32[:, k, u * CI:(u + 1) * CI], bs[u].rearrange("(a c) -> a c", a=1)))
                for j in range(JB):
                    loads.append((rep[j * CI:(j + 1) * CI, :], wz))
                    loads.append((lng[j * CI:(j + 1) * CI, :], ln_g.rearrange("(c a) -> c a", a=1)))
                assert len(loads) == LOADS
                for dst, src in loads:
                    sp.dma_start(dst, src).then_inc(w_in, 16)
                for k in range(2):
                    sp.dma_start(halves_of(xin[:, k, :]), dram_tiles(x1, 0, k)).then_inc(x_in[k], 16)

            group_norm_coefficients(nc, n, stats1, coef, SA, first_loads)
            with nc.Block() as block:
                @block.sync
                def _(sp):
                    sp.wait_ge(step, STEPS)
                    sp.dma_start(pbias[0:1, :, :], bh[:, :, :]).then_inc(moved, 16)
                    sp.dma_start(pbias[1:2, :, :], bl[:, :, :]).then_inc(moved, 16)
                    sp.wait_ge(moved, 32)

                @block.gpsimd
                def _(pool):
                    nc.gpsimd.memset(ident[:, :], 0.0)
                    nc.gpsimd.memset(prow[:, :], SA)
                    nc.gpsimd.memset(mask[:, :], 1.0).then_inc(made, 1)
                    pool.wait_ge(made, 1)
                    nc.gpsimd.affine_select(out=ident[:, :], in_=ident[:, :], compare_op=ALU.not_equal, fill=1.0,
                                            base=0, pattern=[[-1, P]], channel_multiplier=1)
                    nc.gpsimd.affine_select(out=prow[:, :], in_=prow[:, :], compare_op=ALU.is_ge, fill=0.0,
                                            base=1, pattern=[[0, P]], channel_multiplier=-1)
                    nc.gpsimd.affine_select(out=mask[:, :], in_=mask[:, :], compare_op=ALU.is_ge, fill=0.0,
                                            base=0, pattern=[[-CI, JB]], channel_multiplier=1).then_inc(made, 1)
                    pool.wait_ge(made, 2)
                    nc.gpsimd.affine_select(out=mask[:, :], in_=mask[:, :], compare_op=ALU.is_ge, fill=0.0,
                                            base=CI - 1, pattern=[[CI, JB]], channel_multiplier=-1).then_inc(made, 1)

                @block.tensor
                def _(pe):
                    pe.wait_ge(w_in, 16 * LOADS)
                    nc.tensor.matmul(pz[:, 0:1], wz32[:, :], lnb[:, :], start=True, stop=True).then_inc(summed, 1)

                @block.vector
                def _(dve):
                    count = [0]

                    def link(ins):
                        count[0] += 1
                        ins.then_inc(step, 1)
                        dve.wait_ge(step, count[0])

                    link(nc.vector.memset(pbias[:, :, :], 0.0))
                    dve.wait_ge(w_in, 16 * LOADS)
                    link(nc.vector.tensor_scalar(bh[:, :, :], b32[:, :, :], SW, None, ALU.mult))
                    link(nc.vector.scalar_tensor_tensor(bl[:, :, :], b32[:, :, :], SW, bh[:, :, :],
                                                        ALU.mult, ALU.subtract))
                    link(nc.vector.tensor_scalar(gh[:, :], g32[:, :], SW, None, ALU.mult))
                    link(nc.vector.scalar_tensor_tensor(gl[:, :], g32[:, :], SW, gh[:, :], ALU.mult, ALU.subtract))
                    link(nc.vector.tensor_scalar(ph[:, :, :], p32[:, :, :], SW, None, ALU.mult))
                    link(nc.vector.scalar_tensor_tensor(pl[:, :, :], p32[:, :, :], SW, ph[:, :, :],
                                                        ALU.mult, ALU.subtract))
                    dve.wait_ge(made, 3)
                    for j in range(JB):
                        last = nc.vector.tensor_scalar(blk[:, j, :], rep[:, :], lng[:, 0:1], mask[:, j:j + 1],
                                                       ALU.mult, ALU.mult)
                    link(last)
                    link(nc.vector.tensor_scalar(zh[:, :, :], blk[:, :, :], SW, None, ALU.mult))
                    link(nc.vector.scalar_tensor_tensor(zl[:, :, :], blk[:, :, :], SW, zh[:, :, :],
                                                        ALU.mult, ALU.subtract))
                    dve.wait_ge(summed, 1)
                    link(nc.vector.tensor_scalar(bzc[:, :], pz[:, 0:1], bzi[:, 0:1], SA * SW, ALU.add, ALU.mult))
                    assert count[0] == STEPS, count[0]

        xh = n.sb("xh", [C, PLANE], F16)
        xl = n.sb("xl", [C, PLANE], F16)
        gate = n.sb("gate", [C, PLANE])
        xr = n.sb("xr", [C, 2, PT * TILE])
        xo = n.sb("xo", [C, 2, PT * TILE])
        xn = n.sb("xn", [C, 2 * PT, TILE])
        half = n.sb("half", [P, 2, GR, CI])
        ab = n.sb("ab", [P, 2, GR, CI])
        abh = n.sb("abh", [P, 2, CI, P], F16)
        abl = n.sb("abl", [P, 2, CI, P], F16)
        zc = n.sb("zc", [P, H, CI])
        zq = n.sb("zq", [P, ZN])
        zparts = zq[:, :].bitcast(F16)
        znh, znl = zparts[:, 0:ZN], zparts[:, ZN:2 * ZN]
        zs = n.sb("zs", [P, 4, H])
        st = n.sb("st", [C, B * TILES, 6])
        gps = [n.ps(f"g{k}", [C, TILE]) for k in range(2)]
        pps = [n.ps(f"p{k}", [P, TILE]) for k in range(2)]
        zps = n.ps("z", [P, ZN])
        ops = [zps[:, q * TILE:(q + 1) * TILE] for q in range(4)]

        r_in = [n.sem(f"r_in{k}") for k in range(2)]
        stored = [n.sem(f"stored{k}") for k in range(2)]
        (hi_done, xn_done, lo_done, g_summed, g_done, p_summed, half_done, prod_done, ab_done, abh_done, abl_done,
         z_summed, z_mean, zc_done, sq_done, var_ready, root_ready, zstep, zn_done, z_turned, znh_done, znl_done,
         o_summed, o_done, lifted, x2_done, st_done, st_stored) = (
            n.sem(s) for s in (
                "hi_done", "xn_done", "lo_done", "g_summed", "g_done", "p_summed", "half_done", "prod_done",
                "ab_done", "abh_done", "abl_done", "z_summed", "z_mean", "zc_done", "sq_done", "var_ready",
                "root_ready", "zstep", "zn_done", "z_turned", "znh_done", "znl_done", "o_summed", "o_done",
                "lifted", "x2_done", "st_done", "st_stored"))

        NB = NL // 2
        PAIRS = B * NL
        with nc.Block() as block:
            @block.sync
            def _(sp):
                def load(i, k):
                    sp.wait_ge(hi_done, i * (2 * PT) + (k - 1) * PT)
                    sp.wait_ge(xn_done, i * (2 * PT) + (k - 1) * PT)
                    sp.dma_start(halves_of(xin[:, k, :]), dram_tiles(x1, i, k)).then_inc(x_in[k], 16)

                def load_r(i, k, reused=True):
                    if reused:
                        sp.wait_ge(x2_done, i * (2 * PT) + (k - 1) * PT)
                    sp.dma_start(halves_of(xr[:, k, :]), dram_tiles(x1, i, k)).then_inc(r_in[k], 16)

                def store(i, k):
                    sp.wait_ge(x2_done, i * (2 * PT) + (k + 1) * PT)
                    sp.dma_start(dram_tiles(x2, i, k), halves_of(xo[:, k, :])).then_inc(stored[k], 16)

                sp.sem_inc(stored[0], 16)
                sp.sem_inc(stored[1], 16)
                with sp.Fori(1, NB + 1) as i:
                    load(i, 0)
                    load(i, 1)
                load(NB + 1, 0)
                load_r(0, 0, False)
                load(NB + 1, 1)
                load_r(0, 1, False)
                store(0, 0)
                with sp.Fori(1, PAIRS // 2 - NB - 1) as j:
                    load(j + (NB + 1), 0)
                    load_r(j, 0)
                    store(j - 1, 1)
                    load(j + (NB + 1), 1)
                    load_r(j, 1)
                    store(j, 0)
                with sp.Fori(PAIRS // 2 - NB - 1, PAIRS // 2) as j:
                    load_r(j, 0)
                    store(j - 1, 1)
                    load_r(j, 1)
                    store(j, 0)
                store(PAIRS // 2 - 1, 1)
                sp.wait_ge(st_done, B * TILES)
                sp.dma_start(stats2, st[:, :, :].rearrange("c (b t) s -> c b (t s)", b=B)).then_inc(st_stored, 16)
                sp.wait_ge(st_stored, 16)
                for k in range(2):
                    sp.wait_ge(stored[k], 16 * PAIRS // 2 + 16)

            @block.gpsimd
            def _(pool):
                with pool.Fori(0, B * NB) as i:
                    for tt in range(2 * PT):
                        pool.wait_ge(hi_done, i * (2 * PT) + (tt + 1))
                        pool.wait_ge(xn_done, i * (2 * PT) + (tt + 1))
                        j = i % NB
                        nc.gpsimd.tensor_tensor(plane_tile(xl, j, tt), halves_of(xn[:, tt, :]),
                                                plane_tile(xh, j, tt), ALU.subtract).then_inc(lo_done, 1)

                def gated(i, tt):
                    T = (B - 1) * TILES + (i * (2 * PT) + tt)
                    k, u = divmod(tt, PT)
                    pool.wait_ge(lifted, i * (2 * PT) + (tt + 1))
                    if u == 0:
                        pool.wait_ge(stored[k], (B - 1) * (16 * NB) + i * 16 + 16)
                    pool.wait_ge(st_done, T - 3)
                    nc.gpsimd.tensor_tensor(slot_tile(xo, k, u), halves_of(xn[:, tt, :]), plane_tile(gate, i, tt),
                                            ALU.mult).then_inc(o_done, 1)

                with pool.Fori(0, NB) as i:
                    for tt in range(2 * PT):
                        gated(i, tt)

            @block.tensor
            def _(pe):
                def products(out, parts, first=True, **kw):
                    for p, (a, b) in enumerate(parts):
                        last = nc.tensor.matmul(out, a, b, start=(first and p == 0), stop=(p == 2), **kw)
                    return last

                def project(bank, r, k, xhr, xlr):
                    return products(bank[:, r * 2 * CI:(r + 1) * 2 * CI],
                                    ((xhr, ph[:, k, :]), (xhr, pl[:, k, :]), (xlr, ph[:, k, :])), False,
                                    skip_group_check=True)

                def open_group(bank, k):
                    nc.tensor.matmul(bank[:, :].rearrange("p (r n) -> p r n", r=GR), prow[:, :],
                                     pbias[:, k, :].unsqueeze(1).broadcast_to([P, GR, 2 * CI]),
                                     start=True, stop=False, skip_group_check=True)

                def outer(b, i, tt, start):
                    if start and tt == 0:
                        pe.wait_ge(znl_done, b * 4 + 4)
                    if not start:
                        pe.wait_ge(o_done, b * TILES + (i * (2 * PT) + (tt - 3)))
                    zih, zil = (v[:, bass.ds(i * (2 * P), 2 * P)].rearrange("p (m w) -> p m w", m=2)
                                for v in (znh, znl))
                    for r in range(2):
                        out = ops[tt].rearrange("c (m r w) -> c r m w", m=2, w=W)[:, r, :, :]
                        zhr, zlr = zh[:, 2 * tt + r, :], zl[:, 2 * tt + r, :]
                        last = products(out, ((zhr, zih), (zhr, zil), (zlr, zih)))
                    last.then_inc(o_summed, 1)

                def rows(b, i, first, start):
                    xhi, xli = (v[:, bass.ds(i * (2 * PT * TILE), 2 * PT * TILE)] for v in (xh, xl))

                    def project_tile(tt):
                        for r in (2 * tt, 2 * tt + 1, JB + 2 * tt, JB + 2 * tt + 1):
                            cols = slice(r * W, (r + 1) * W)
                            last = project(pps[0], r, 0, xhi[:, cols], xli[:, cols])
                        return last

                    for tt in range(2 * PT):
                        T = b * TILES + (i * (2 * PT) + tt)
                        if not first:
                            outer(b - 1, i, tt, start)
                        pe.wait_ge(lo_done, T + 1)
                        if not (first and start and tt < 2):
                            pe.wait_ge(g_done, T - 1)
                        xht, xlt = plane_tile(xh, i, tt), plane_tile(xl, i, tt)
                        products(halves_of(gps[tt % 2][:, :]), ((gh[:, :], xht), (gh[:, :], xlt), (gl[:, :], xht))
                                 ).then_inc(g_summed, 1)
                        if tt == 1:
                            if not (first and start):
                                pe.wait_ge(prod_done, b * (2 * NGR) + i)
                            open_group(pps[0], 0)
                        if tt >= 1:
                            project_tile(tt - 1)
                    project_tile(2 * PT - 1).then_inc(p_summed, 1)

                def columns(b, i):
                    xhc, xlc = (v[:, :].rearrange("c (h w) -> c w h", w=W)[:, bass.ds(i * (2 * GR), 2 * GR), :]
                                for v in (xh, xl))
                    for u in range(2):
                        pe.wait_ge(prod_done, b * (2 * NGR) + NGR + i * 2 + (u - 1 if u == 0 else 0))
                        open_group(pps[1 - u], 1)
                        for r in range(GR):
                            last = project(pps[1 - u], r, 1, xhc[:, u * GR + r, :], xlc[:, u * GR + r, :])
                        last.then_inc(p_summed, 1)

                def triangle(b, first):
                    pe.wait_ge(abl_done, b * (2 * NGR) + 2 * NGR)
                    if not first:
                        pe.wait_ge(o_done, b * TILES)
                    for c in range(CI):
                        last = products(zps[:, c * H:(c + 1) * H],
                                        ((abh[:, 1, c, :], abh[:, 0, c, :]), (abl[:, 1, c, :], abh[:, 0, c, :]),
                                         (abh[:, 1, c, :], abl[:, 0, c, :])))
                    last.then_inc(z_summed, 1)
                    zf = zc[:, :, :].rearrange("j i c -> j (i c)")
                    for q in range(4):
                        pe.wait_ge(zn_done, b * 4 + (q + 1))
                        for u in range(4):
                            at = (4 * q + u) * P
                            last = nc.tensor.transpose(zps[:, at:at + P], zf[:, at:at + P], ident[:, :])
                        last.then_inc(z_turned, 1)

                def batch(b, first=False):
                    rows(b, 0, first, True)
                    with pe.Fori(1, NB) as i:
                        rows(b, i, first, False)
                    with pe.Fori(0, NB // 2) as i:
                        columns(b, i)
                    triangle(b, first)

                batch(0, True)
                with pe.Fori(1, B) as b:
                    batch(b)
                for tt in range(2 * PT):
                    outer(B - 1, 0, tt, True)
                with pe.Fori(1, NB) as i:
                    for tt in range(2 * PT):
                        outer(B - 1, i, tt, False)

            @block.scalar
            def _(act):
                def hi(b, i, k, start=False):
                    act.wait_ge(x_in[0], 16)
                    if not start:
                        act.wait_ge(lo_done, b * TILES + (i * (2 * PT) + (k - 1) * PT))
                    act.wait_ge(x_in[k], b * (16 * NB) + i * 16 + 16)
                    for u in range(PT):
                        scale = coef[:, bass.ds(b, 1), 0:1].rearrange("c a s -> c (a s)")
                        shift = coef[:, bass.ds(b, 1), 1:2].rearrange("c a s -> c (a s)")
                        nc.scalar.activation(plane_tile(xh, i, k * PT + u), slot_tile(xin, k, u), ACT.Identity,
                                             bias=shift, scale=scale).then_inc(hi_done, 1)
                        nc.scalar.activation(halves_of(xn[:, k * PT + u, :]), slot_tile(xin, k, u), ACT.Identity,
                                             bias=shift, scale=scale).then_inc(xn_done, 1)

                def sig(b, i, k, first):
                    for u in range(PT):
                        tt = k * PT + u
                        T = b * TILES + (i * (2 * PT) + tt)
                        act.wait_ge(g_summed, T + 1)
                        if not first:
                            act.wait_ge(o_done, T - (TILES - 1))
                        act.wait_ge(g_summed, 1)
                        nc.scalar.activation(plane_tile(gate, i, tt), halves_of(gps[tt % 2][:, :]),
                                             ACT.Sigmoid, bias=bgc[:, 0:1], scale=DESCALE).then_inc(g_done, 1)

                def halve(n_, bank):
                    act.wait_ge(p_summed, n_ + 1)
                    act.wait_ge(ab_done, n_ + 1)
                    v = pps[bank][:, :].rearrange("p (r s c) -> p r s c", s=2, c=CI)
                    nc.scalar.activation(half[:, bank, :, :], v[:, :, 0, :], ACT.Copy).then_inc(half_done, 1)

                def group(n_, bank, halved=False):
                    if not halved:
                        halve(n_, bank)
                    act.wait_ge(prod_done, n_ + 1)
                    nc.scalar.activation(ab[:, bank, :, :], half[:, bank, :, :], ACT.Sigmoid, scale=DESCALE * DESCALE
                                         ).then_inc(ab_done, 1)

                def batch(b, first=False, last=False):
                    hi(b, 0, 1, start=first)
                    sig(b, 0, 0, first)
                    with act.Fori(1, NB) as i:
                        hi(b, i, 0)
                        sig(b, i - 1, 1, first)
                        hi(b, i, 1)
                        halve(b * (2 * NGR) + i - 1, 0)
                        sig(b, i, 0, first)
                        group(b * (2 * NGR) + i - 1, 0, True)
                    sig(b, NB - 1, 1, first)
                    group(b * (2 * NGR) + (NGR - 1), 0)
                    with act.Fori(0, NB // 2) as i:
                        group(b * (2 * NGR) + NGR + i * 2, 1)
                        group(b * (2 * NGR) + NGR + i * 2 + 1, 0)
                    if not last:
                        hi(b + 1, 0, 0)
                    if not first:
                        act.wait_ge(o_summed, b * TILES)
                    for u in range(2):
                        rows = slice(u * (H // 2), (u + 1) * (H // 2))
                        act.wait_ge(zc_done, b * 2 + (u + 1))
                        nc.scalar.activation(zq[:, u * (ZN // 2):(u + 1) * (ZN // 2)],
                                             zc[:, rows, :].rearrange("j i c -> j (i c)"), ACT.Square
                                             ).then_inc(sq_done, 1)
                    act.wait_ge(var_ready, b + 1)
                    nc.scalar.activation(zs[:, 2, :], zs[:, 1, :], ACT.Sqrt).then_inc(root_ready, 1)
                    act.preload_act_table_set("sigmoid_and_others")
                    for q in range(4):
                        cols = slice(q * TILE, (q + 1) * TILE)
                        act.wait_ge(z_turned, b * 4 + (q + 1))
                        nc.scalar.activation(znh[:, cols], zps[:, cols], ACT.Copy, scale=SA).then_inc(znh_done, 1)

                act.sem_inc(ab_done, 1)
                hi(0, 0, 0, start=True)
                batch(0, first=True)
                with act.Fori(1, B - 1) as b:
                    batch(b)
                batch(B - 1, last=True)

                def lift(i, tt, start):
                    T = (B - 1) * TILES + (i * (2 * PT) + tt)
                    act.wait_ge(o_summed, T + 1)
                    if not start:
                        act.wait_ge(o_done, T - 3)
                    nc.scalar.activation(xn[:, tt, :], ops[tt], ACT.Identity, bias=bzc[:, 0:1]).then_inc(lifted, 1)

                for tt in range(2 * PT):
                    lift(0, tt, True)
                with act.Fori(1, NB) as i:
                    for tt in range(2 * PT):
                        lift(i, tt, False)

            @block.vector
            def _(dve):
                def outer(b, i, tt):
                    T = b * TILES + (i * (2 * PT) + tt)
                    k, u = divmod(tt, PT)
                    if u == 0:
                        dve.wait_ge(stored[k], b * (16 * NB) + i * 16 + 16)
                    dve.wait_ge(o_summed, T + 1)
                    nc.vector.scalar_tensor_tensor(slot_tile(xo, k, u), halves_of(ops[tt]), bzc[:, 0:1],
                                                   plane_tile(gate, i, tt),
                                                   ALU.add, ALU.mult).then_inc(o_done, 1)

                def add(b, i, tt):
                    T = b * TILES + (i * (2 * PT) + tt)
                    k, u = divmod(tt, PT)
                    if u == 0:
                        dve.wait_ge(r_in[k], b * (16 * NB) + i * 16 + 16)
                    dve.wait_ge(o_done, T + 1)
                    nc.vector.scalar_tensor_tensor(slot_tile(xo, k, u), slot_tile(xo, k, u), DESCALE, slot_tile(xr, k, u),
                                                   ALU.mult, ALU.add).then_inc(x2_done, 1)

                def stat(b, i, tt):
                    T = b * TILES + (i * (2 * PT) + tt)
                    k, u = divmod((tt - 1) % (2 * PT), PT)
                    dve.wait_ge(x2_done, T)
                    nc.vector.bn_stats(st[:, bass.ds(T - 1, 1), :].rearrange("c a s -> c (a s)"),
                                       slot_tile(xo, k, u)).then_inc(st_done, 1)

                def leave(b, i, tt, start):
                    outer(b, i, tt)
                    if not (start and tt == 0):
                        stat(b, i, tt)
                    add(b, i, tt)

                def multiply(n_, bank):
                    dve.wait_ge(half_done, n_ + 1)
                    v = pps[bank][:, :].rearrange("p (r s c) -> p r s c", s=2, c=CI)
                    nc.vector.tensor_tensor(half[:, bank, :, :], v[:, :, 1, :], half[:, bank, :, :], ALU.mult
                                            ).then_inc(prod_done, 1)

                def group(n_, k, r0, bank, multiplied=False):
                    if not multiplied:
                        multiply(n_, bank)
                    dve.wait_ge(ab_done, n_ + 2)
                    src = ab[:, bank, :, :].rearrange("p r c -> p c r")
                    nc.vector.tensor_scalar(abh[:, k, :, bass.ds(r0, GR)], src, SA, None, ALU.mult).then_inc(abh_done, 1)
                    dve.wait_ge(abh_done, n_ + 1)
                    nc.vector.scalar_tensor_tensor(abl[:, k, :, bass.ds(r0, GR)], src, SA, abh[:, k, :, bass.ds(r0, GR)],
                                                   ALU.mult, ALU.subtract).then_inc(abl_done, 1)

                def normalise(b):
                    LINKS = 7
                    count = [0]

                    def link(ins):
                        count[0] += 1
                        ins.then_inc(zstep, 1)
                        dve.wait_ge(zstep, b * LINKS + count[0])

                    dve.wait_ge(z_summed, b + 1)
                    halves = [slice(u * (H // 2), (u + 1) * (H // 2)) for u in range(2)]
                    zv = zps[:, :].rearrange("j (c i) -> j i c", i=H)
                    for rows in halves:
                        link(nc.vector.reduce_sum(zs[:, 0, rows], zv[:, rows, :], AX.X))
                        nc.vector.scalar_tensor_tensor(
                            zc[:, rows, :], zs[:, 0, rows].unsqueeze(2).broadcast_to([P, H // 2, CI]), -1.0 / CI,
                            zv[:, rows, :], ALU.mult, ALU.add).then_inc(zc_done, 1)
                    for u, rows in enumerate(halves):
                        dve.wait_ge(sq_done, b * 2 + (u + 1))
                        last = nc.vector.reduce_sum(
                            zs[:, 2, rows], zq[:, u * (ZN // 2):(u + 1) * (ZN // 2)].rearrange("j (i c) -> j i c", c=CI), AX.X)
                    link(last)
                    nc.vector.tensor_scalar(zs[:, 1, :], zs[:, 2, :], 1.0 / CI, LN_EPS * (SA * SA) ** 2,
                                            ALU.mult, ALU.add).then_inc(var_ready, 1)
                    dve.wait_ge(root_ready, b + 1)
                    link(nc.vector.reciprocal(zs[:, 3, :], zs[:, 2, :]))
                    link(nc.vector.scalar_tensor_tensor(zs[:, 0, :], zs[:, 3, :], -0.5, zs[:, 3, :], ALU.mult, ALU.mult))
                    link(nc.vector.tensor_tensor(zs[:, 0, :], zs[:, 0, :], zs[:, 1, :], ALU.mult))
                    link(nc.vector.scalar_tensor_tensor(zs[:, 3, :], zs[:, 0, :], 1.5, zs[:, 3, :], ALU.add, ALU.mult))
                    assert count[0] == LINKS, count[0]
                    for q in range(4):
                        rows = slice(q * (H // 4), (q + 1) * (H // 4))
                        nc.vector.tensor_tensor(zc[:, rows, :], zc[:, rows, :],
                                                zs[:, 3, rows].unsqueeze(2).broadcast_to([P, H // 4, CI]),
                                                ALU.mult).then_inc(zn_done, 1)
                    dve.wait_ge(g_done, b * TILES + TILES)
                    for q in range(4):
                        cols = slice(q * TILE, (q + 1) * TILE)
                        dve.wait_ge(znh_done, b * 4 + (q + 1))
                        nc.vector.scalar_tensor_tensor(znl[:, cols], zps[:, cols], SA, znh[:, cols],
                                                       ALU.mult, ALU.subtract).then_inc(znl_done, 1)

                def batch(b, first=False):
                    def tiles(i, start):
                        for tt in range(2 * PT):
                            if not first:
                                leave(b - 1, i, tt, start)
                            if tt == 0 and not start:
                                multiply(b * (2 * NGR) + i - 1, 0)
                            if tt == 1 and not start:
                                group(b * (2 * NGR) + i - 1, 0, i * GR - GR, 0, True)
                    tiles(0, True)
                    with dve.Fori(1, NB) as i:
                        tiles(i, False)
                    group(b * (2 * NGR) + (NGR - 1), 0, (NGR - 1) * GR, 0)
                    if not first:
                        stat(b - 1, NB, 0)
                    with dve.Fori(0, NB // 2) as i:
                        group(b * (2 * NGR) + NGR + i * 2, 1, i * (2 * GR), 1)
                        group(b * (2 * NGR) + NGR + i * 2 + 1, 1, i * (2 * GR) + GR, 0)
                    normalise(b)

                batch(0, True)
                with dve.Fori(1, B) as b:
                    batch(b)
                for tt in range(2 * PT):
                    add(B - 1, 0, tt)
                    if tt:
                        stat(B - 1, 0, tt)
                with dve.Fori(1, NB) as i:
                    for tt in range(2 * PT):
                        add(B - 1, i, tt)
                        stat(B - 1, i, tt)
                stat(B - 1, NB, 0)


def stage_lstm(nc, x2, stats2, wx, wm, bias, x3, stats3):
    n = Names(nc, "lstm")
    HALF = B // 2
    N = HALF * W
    GATES = 4
    FORGET, IN, CELL, OUT = range(GATES)
    NT = H // ROWS
    SPAN = ROWS * TILE
    SPAN2 = 2 * SPAN
    with n.stack:
        coef = n.sb("coef", [C, B, 2])
        w32 = n.sb("w32", [C, 2 * GATES, C])
        wh = n.sb("wh", [C, 2 * GATES, C], F16)
        wl = n.sb("wl", [C, 2 * GATES, C], F16)
        bc = n.sb("bias", [C, GATES])
        xin = n.sb("xin", [C, 2, B, TILE])
        xn = n.sb("xn", [C, B, TILE])
        xh = n.sb("xh", [C, 2, B, TILE], F16)
        xl = n.sb("xl", [C, 2, B, TILE], F16)
        hh = n.sb("hh", [C, 2, N], F16)
        hl = n.sb("hl", [C, 2, N], F16)
        cell = n.sb("cell", [C, 2, N])
        gate = n.sb("gate", [C, 2, GATES, N])
        ig = n.sb("ig", [C, 2, N])
        tc = n.sb("tanh_c", [C, 2, N])
        h = n.sb("h", [C, 2, 2, N])
        xres = n.sb("xres", [C, 2, ROWS, TILE])
        xout = n.sb("xout", [C, 2, ROWS, TILE])
        st = n.sb("st", [C, B * TILES, 6])
        w_in, w_hi, setup = (n.sem(x) for x in ("w_in", "w_hi", "setup"))
        x_in = [n.sem(f"x_in{k}") for k in range(2)]
        res_in = [n.sem(f"res_in{k}") for k in range(2)]
        x2_t = x2.rearrange("c (b t) -> c b t", b=B)

        def first_loads(sp):
            for g in range(GATES):
                sp.dma_start(w32[:, g, :], wx[g]).then_inc(w_in, 16)
                sp.dma_start(w32[:, GATES + g, :], wm[g]).then_inc(w_in, 16)
                sp.dma_start(bc[:, g:g + 1], bias[g].rearrange("a h -> h a")).then_inc(w_in, 16)
            for k in range(2):
                sp.dma_start(xin[:, k, :, :], x2_t[:, :, k * TILE:(k + 1) * TILE]).then_inc(x_in[k], 16)
                sp.dma_start(xres[:, k, :, :], x2[:, k * SPAN:(k + 1) * SPAN]).then_inc(res_in[k], 16)

        group_norm_coefficients(nc, n, stats2, coef, SA, first_loads)
        with nc.Block() as block:
            @block.vector
            def _(dve):
                nc.vector.memset(hh[:, :, :], 0.0)
                nc.vector.memset(hl[:, :, :], 0.0)
                nc.vector.memset(cell[:, :, :], 0.0)
                dve.wait_ge(w_in, 16 * 3 * GATES)
                split_weights(nc, dve, w_hi, 1, w32[:, :, :], wh[:, :, :], wl[:, :, :]).then_inc(setup, 1)

        z = [[n.ps(f"z{q}{s}", [C, GATES * N]) for s in range(2)] for q in range(2)]
        hi_done = n.sem("x_hi_done")
        xn_done = n.sem("xn_done")
        xl_done = n.sem("xl_done")
        z_first = [n.sem(f"z_first{q}") for q in range(2)]
        z_second = [n.sem(f"z_second{q}") for q in range(2)]
        g_cell = [n.sem(f"g_cell{q}") for q in range(2)]
        g_forget = [n.sem(f"g_forget{q}") for q in range(2)]
        g_out = [n.sem(f"g_out{q}") for q in range(2)]
        ig_done = [n.sem(f"ig_done{q}") for q in range(2)]
        fc_done = [n.sem(f"fc_done{q}") for q in range(2)]
        c_ready = [n.sem(f"c_ready{q}") for q in range(2)]
        tc_ready = [n.sem(f"tc_ready{q}") for q in range(2)]
        h_done = [n.sem(f"h_done{q}") for q in range(2)]
        hh_done = [n.sem(f"hh_done{q}") for q in range(2)]
        h_ready = [n.sem(f"h_ready{q}") for q in range(2)]
        x3_rows = n.sem("x3_rows")
        st_done = n.sem("st_done")
        stored = [n.sem(f"stored{k}") for k in range(2)]
        st_stored = n.sem("st_stored")
        GATE_W = {IN: 0, FORGET: 1, OUT: 2, CELL: 3}

        with nc.Block() as block:
            @block.sync
            def _(sp):
                def load_x(i, k):
                    sp.wait_ge(xn_done, (i * 2 + (k - 1)) * B)
                    sp.wait_ge(hi_done, (i * 2 + (k - 1)) * B)
                    sp.dma_start(xin[:, k, :, :], x2_t[:, :, bass.ds(i * (2 * TILE) + k * TILE, TILE)]
                                 ).then_inc(x_in[k], 16)

                def load_res(i, k):
                    sp.dma_start(xres[:, k, :, :], x2[:, bass.ds(i * SPAN2 + k * SPAN, SPAN)]).then_inc(res_in[k], 16)

                def store(i, k):
                    sp.wait_ge(x3_rows, i * (4 * ROWS) + (k + 1) * 2 * ROWS)
                    sp.dma_start(x3[:, bass.ds(i * SPAN2 + k * SPAN, SPAN)], xout[:, k, :, :]
                                 ).then_inc(stored[k], 16)

                with sp.Fori(0, NT // 2 - 1) as i:
                    for k in range(2):
                        load_x(i + 1, k)
                        store(i, k)
                        load_res(i + 1, k)
                store(NT // 2 - 1, 0)
                store(NT // 2 - 1, 1)
                sp.wait_ge(st_done, B * NT)
                sp.dma_start(stats3, st[:, :, :].rearrange("c (b t) s -> c b (t s)", b=B)).then_inc(st_stored, 16)
                sp.wait_ge(st_stored, 16)
                for k in range(2):
                    sp.wait_ge(stored[k], 16 * NT // 2)

            @block.tensor
            def _(pe):
                def x_part(k, r, q):
                    hi = xh[:, k, q * HALF:(q + 1) * HALF, r * W:(r + 1) * W]
                    lo = xl[:, k, q * HALF:(q + 1) * HALF, r * W:(r + 1) * W]
                    for g in range(GATES):
                        w = GATE_W[g]
                        for p, (a, b) in enumerate(((wh, hi), (wh, lo), (wl, hi))):
                            nc.tensor.matmul(z[q][r % 2][:, g * N:(g + 1) * N], a[:, w, :], b,
                                             start=(g % 2 == 0 and p == 0), stop=False, skip_group_check=True)

                def h_part(t, r, q, wait=True):
                    def product(g, a, b):
                        return nc.tensor.matmul(z[q][r % 2][:, g * N:(g + 1) * N], a[:, GATES + GATE_W[g], :], b[:, q, :],
                                                start=False, stop=True, skip_group_check=True)

                    if wait:
                        pe.wait_ge(hh_done[q], t)
                    for g in (FORGET, IN, CELL, OUT):
                        product(g, wh, hh)
                        product(g, wl, hh)
                    if wait:
                        pe.wait_ge(h_ready[q], t)
                    product(FORGET, wh, hl)
                    product(IN, wh, hl).then_inc(z_first[q], 1)
                    product(CELL, wh, hl)
                    last = product(OUT, wh, hl)
                    last.then_inc(z_second[q], 1)

                def tile(i, k, first=False, last=False):
                    for r in range(ROWS):
                        t = i * (2 * ROWS) + (k * ROWS + r)
                        for q in range(2):
                            h_part(t, r, q, not (first and r == 0))
                            if r < ROWS - 1:
                                x_part(k, r + 1, q)
                            elif not last:
                                if q == 0:
                                    pe.wait_ge(xl_done, i * (2 * B) + (k + 2) * B)
                                x_part(1 - k, 0, q)

                pe.wait_ge(xl_done, B)
                x_part(0, 0, 0)
                x_part(0, 0, 1)
                tile(0, 0, first=True)
                tile(0, 1)
                with pe.Fori(1, NT // 2 - 1) as i:
                    tile(i, 0)
                    tile(i, 1)
                tile(NT // 2 - 1, 0)
                tile(NT // 2 - 1, 1, last=True)

            @block.scalar
            def _(act):
                def gate_fn(q, s, g, fn):
                    return nc.scalar.activation(gate[:, q, g, :], z[q][s][:, g * N:(g + 1) * N], fn,
                                                bias=bc[:, GATE_W[g]:GATE_W[g] + 1], scale=DESCALE)

                def norm(i, k, b):
                    if b == 0:
                        act.wait_ge(x_in[k], i * 16 + 16)
                    nc.scalar.activation(xh[:, k, b, :], xin[:, k, b, :], ACT.Identity, bias=coef[:, b, 1:2],
                                         scale=coef[:, b, 0:1]).then_inc(hi_done, 1)

                def tile(i, k, last=False):
                    for r in range(ROWS):
                        t, s = i * (2 * ROWS) + (k * ROWS + r), r % 2
                        for q in range(2):
                            act.wait_ge(z_first[q], t + 1)
                            gate_fn(q, s, FORGET, ACT.Sigmoid).then_inc(g_forget[q], 1)
                            gate_fn(q, s, IN, ACT.Sigmoid)
                            act.wait_ge(z_second[q], t + 1)
                            gate_fn(q, s, CELL, ACT.Tanh).then_inc(g_cell[q], 1)
                            gate_fn(q, s, OUT, ACT.Sigmoid).then_inc(g_out[q], 1)
                            if r < 2 and not last:
                                norm(i + (k == 1), 1 - k, 2 * r + q)
                            act.wait_ge(c_ready[q], t + 1)
                            nc.scalar.activation(tc[:, q, :], cell[:, q, :], ACT.Tanh).then_inc(tc_ready[q], 1)

                act.preload_act_table_set("sigmoid_and_others")
                for b in range(B):
                    norm(0, 0, b)
                with act.Fori(0, NT // 2 - 1) as i:
                    tile(i, 0)
                    tile(i, 1)
                tile(NT // 2 - 1, 0)
                tile(NT // 2 - 1, 1, last=True)

            @block.vector
            def _(dve):
                def norm(i, k, b, used=True):
                    if b == 0:
                        dve.wait_ge(x_in[k], i * 16 + 16)
                    if used:
                        dve.wait_ge(xl_done, (i * 2 + (k - 1)) * B + (b + 1))
                    nc.vector.tensor_scalar(xn[:, b, :], xin[:, k, b, :], coef[:, b, 0:1], coef[:, b, 1:2],
                                            ALU.mult, ALU.add).then_inc(xn_done, 1)

                def stat(i, k, r):
                    dve.wait_ge(x3_rows, i * (4 * ROWS) + (k * ROWS + r + 1) * 2)
                    nc.vector.bn_stats(st[:, bass.ds(i * (2 * ROWS) + (k * ROWS + r), 1), :].rearrange("c a s -> c (a s)"),
                                       xout[:, k, r, :]).then_inc(st_done, 1)

                def gated_input(t, q):
                    dve.wait_ge(g_cell[q], t + 1)
                    nc.vector.tensor_tensor(ig[:, q, :], gate[:, q, IN, :], gate[:, q, CELL, :],
                                            ALU.mult).then_inc(ig_done[q], 1)

                def new_cell(t, q):
                    dve.wait_ge(ig_done[q], t + 1)
                    dve.wait_ge(fc_done[q], t + 1)
                    nc.vector.tensor_tensor(cell[:, q, :], cell[:, q, :], ig[:, q, :],
                                            ALU.add).then_inc(c_ready[q], 1)

                def between(i, k, r, q, first, last):
                    if r < 2 and not last:
                        norm(i + (k == 1), 1 - k, 2 * r + q)
                    if r >= 2 and not first:
                        stat(i - (k == 0), 1 - k, 2 * (r - 2) + q)

                def tile(i, k, first=False, last=False, next_last=False):
                    for r in range(ROWS):
                        t = i * (2 * ROWS) + (k * ROWS + r)
                        s = r % 2
                        for q in range(2):
                            dve.wait_ge(tc_ready[q], t + 1)
                            dve.wait_ge(g_out[q], t + 1)
                            if not (first and r < 2):
                                dve.wait_ge(x3_rows, (t - 2) * 2 + (q + 1))
                            nc.vector.scalar_tensor_tensor(hh[:, q, :], gate[:, q, OUT, :], SA, tc[:, q, :],
                                                           ALU.mult, ALU.mult).then_inc(hh_done[q], 1)
                            nc.vector.tensor_tensor(h[:, q, s, :], gate[:, q, OUT, :], tc[:, q, :],
                                                    ALU.mult).then_inc(h_done[q], 1)
                            goes_on = not (last and r == ROWS - 1 and q == 1)
                            if goes_on:
                                gated_input(t + q, 1 - q)
                            dve.wait_ge(hh_done[q], t + 1)
                            dve.wait_ge(h_done[q], t + 1)
                            nc.vector.scalar_tensor_tensor(hl[:, q, :], h[:, q, s, :], SA, hh[:, q, :],
                                                           ALU.mult, ALU.subtract).then_inc(h_ready[q], 1)
                            if goes_on:
                                new_cell(t + q, 1 - q)
                                if r + q < ROWS:
                                    between(i, k, r + q, 1 - q, first, last)
                                else:
                                    between(i + (k == 1), 1 - k, 0, 0, False, next_last)

                for b in range(B):
                    norm(0, 0, b, used=False)
                gated_input(0, 0)
                new_cell(0, 0)
                between(0, 0, 0, 0, True, False)
                tile(0, 0, first=True)
                tile(0, 1)
                with dve.Fori(1, NT // 2 - 1) as i:
                    tile(i, 0)
                    tile(i, 1)
                tile(NT // 2 - 1, 0, next_last=True)
                tile(NT // 2 - 1, 1, last=True)
                for r in range(ROWS):
                    stat(NT // 2 - 1, 1, r)

            @block.gpsimd
            def _(pool):
                def split(i, k, b):
                    pool.wait_ge(hi_done, (i * 2 + k) * B + (b + 1))
                    pool.wait_ge(xn_done, (i * 2 + k) * B + (b + 1))
                    nc.gpsimd.tensor_tensor(xl[:, k, b, :], xn[:, b, :], xh[:, k, b, :],
                                            ALU.subtract).then_inc(xl_done, 1)

                def forget(t, q):
                    pool.wait_ge(g_forget[q], t + 1)
                    nc.gpsimd.tensor_tensor(cell[:, q, :], gate[:, q, FORGET, :], cell[:, q, :],
                                            ALU.mult).then_inc(fc_done[q], 1)

                def residual(i, k, r, q, reused=True):
                    pool.wait_ge(h_done[q], i * (2 * ROWS) + (k * ROWS + r + 1))
                    if r == 0 and q == 0:
                        if reused:
                            pool.wait_ge(stored[k], i * 16)
                            pool.wait_ge(st_done, (i * 2 + (k - 1)) * B)
                        pool.wait_ge(res_in[k], i * 16 + 16)
                    cols = slice(q * N, (q + 1) * N)
                    nc.gpsimd.tensor_tensor(xout[:, k, r, cols], h[:, q, r % 2, :], xres[:, k, r, cols],
                                            ALU.add).then_inc(x3_rows, 1)

                def tile(i, k, first=False, last=False, reused=True):
                    for r in range(ROWS):
                        for q in range(2):
                            forget(i * (2 * ROWS) + (k * ROWS + r), q)
                            if r > 0 or q > 0:
                                residual(i, k, r - (q == 0), 1 - q, reused)
                            elif not first:
                                residual(i - (k == 0), 1 - k, ROWS - 1, 1)
                            if 1 <= 2 * r + q <= B and not last:
                                split(i + (k == 1), 1 - k, 2 * r + q - 1)

                for b in range(B):
                    split(0, 0, b)
                tile(0, 0, first=True, reused=False)
                tile(0, 1, reused=False)
                with pool.Fori(1, NT // 2 - 1) as i:
                    tile(i, 0)
                    tile(i, 1)
                tile(NT // 2 - 1, 0)
                tile(NT // 2 - 1, 1, last=True)
                residual(NT // 2 - 1, 1, ROWS - 1, 1)


TAPS = 9
PAD = TAPS // 2


def stage_rowconv(nc, x3, stats3, w_conv, out):
    n = Names(nc, "rc")
    PADW = W + 2 * PAD
    HALF = B // 2
    NEW_SCALE = SA * SW
    with n.stack:
        coef = n.sb("coef", [C, B, 2])
        ident = n.sb("ident", [P, P])
        w32 = n.sb("w32", [C, TAPS, C])
        wh = n.sb("wh", [C, TAPS, C], F16)
        wl = n.sb("wl", [C, TAPS, C], F16)
        xin = n.sb("xin", [C, 2, B, TILE])
        rowx = n.sb("rowx", [C, 2, B, TILE])
        ch = n.sb("carry_hi", [C, 2, HALF, PADW], F16)
        cl = n.sb("carry_lo", [C, 2, HALF, PADW], F16)
        new = n.sb("new", [C, 2, 2, HALF, W])
        fin = n.sb("fin", [C, 2, B, W])
        ot = n.sb("ot", [P, 4, B, C])
        (w_in, w_hi, setup, ident_ready) = (n.sem(x) for x in ("w_in", "w_hi", "setup", "ident_ready"))
        x_in = [n.sem(f"x_in{k}") for k in range(2)]
        x3_t = x3.rearrange("c (b t) -> c b t", b=B)

        def first_loads(sp):
            sp.dma_start(w32[:, :, :], w_conv.rearrange("k i o -> i k o")).then_inc(w_in, 16)
            for k in range(2):
                sp.dma_start(xin[:, k, :, :], x3_t[:, :, k * TILE:(k + 1) * TILE]).then_inc(x_in[k], 16)

        group_norm_coefficients(nc, n, stats3, coef, NEW_SCALE, first_loads)
        with nc.Block() as block:
            @block.gpsimd
            def _(pool):
                nc.gpsimd.memset(ident[:, :], 0.0).then_inc(ident_ready, 1)
                pool.wait_ge(ident_ready, 1)
                nc.gpsimd.affine_select(out=ident[:, :], in_=ident[:, :], compare_op=ALU.not_equal, fill=1.0,
                                        base=0, pattern=[[-1, P]], channel_multiplier=1).then_inc(ident_ready, 1)

            @block.vector
            def _(dve):
                nc.vector.memset(ch[:, :, :, :], 0.0)
                nc.vector.memset(cl[:, :, :, :], 0.0)
                dve.wait_ge(w_in, 16)
                nc.vector.tensor_scalar(wh[:, :, :], w32[:, :, :], SW, None, ALU.mult).then_inc(w_hi, 1)
                dve.wait_ge(w_hi, 1)
                nc.vector.scalar_tensor_tensor(wl[:, :, :], w32[:, :, :], SW, wh[:, :, :],
                                               ALU.mult, ALU.subtract).then_inc(setup, 1)

        conv_ps = [n.ps(f"conv{k}", [C, 512]) for k in range(2)]
        tr_ps = [n.ps(f"tr{k}", [P, 512]) for k in range(2)]
        x_used = n.sem("x_used")
        row_ready = n.sem("row_ready")
        conv_done = [n.sem(f"conv_done{k}") for k in range(2)]
        new_ready = [n.sem(f"new_ready{k}") for k in range(2)]
        hi_ready = [n.sem(f"hi_ready{k}") for k in range(2)]
        carry_ready = [n.sem(f"carry_ready{k}") for k in range(2)]
        fin_ready = n.sem("fin_ready")
        turned = n.sem("turned")
        turned_copied = n.sem("turned_copied")
        stored = [n.sem(f"stored{k}") for k in range(4)]
        NT = H // ROWS
        out_t = out.rearrange("b h w c -> w b h c")

        with nc.Block() as block:
            @block.sync
            def _(sp):
                with sp.Fori(1, NT // 2) as i:
                    for k in range(2):
                        sp.wait_ge(x_used, i * 2 + (k - 1))
                        sp.dma_start(xin[:, k, :, :], x3_t[:, :, bass.ds(i * (2 * TILE) + k * TILE, TILE)]).then_inc(x_in[k], 16)

            @block.tensor
            def _(pe):
                def conv(t, k):
                    if t is not None:
                        pe.wait_ge(carry_ready[k], t)
                    for tap in range(TAPS):
                        for part, (w, c) in enumerate(((wh, ch), (wh, cl), (wl, ch))):
                            last = nc.tensor.matmul(conv_ps[k][:, 0:HALF * W], w[:, tap, :],
                                                    c[:, k, :, tap:tap + W],
                                                    start=(tap == 0 and part == 0),
                                                    stop=(tap == TAPS - 1 and part == 2))
                    last.then_inc(conv_done[k], 1)

                def turn(t, slot, reused=True):
                    pe.wait_ge(fin_ready, t + 1)
                    if reused:
                        pe.wait_ge(turned_copied, t - 1)
                    for b in range(B):
                        last = nc.tensor.transpose(tr_ps[slot][:, b * C:(b + 1) * C], fin[:, slot, b, :], ident[:, :])
                    last.then_inc(turned, 1)

                for t in range(4):
                    conv(t or None, 0)
                    conv(t or None, 1)
                    if t:
                        turn(t - 1, (t - 1) % 2, t > 2)
                with pe.Fori(2, H // 2) as i:
                    for r in range(2):
                        conv(i * 2 + r, 0)
                        conv(i * 2 + r, 1)
                        turn(i * 2 + (r - 1), 1 - r)
                turn(H - 1, 1)

            @block.vector
            def _(dve):
                def tile(i, k, first):
                    dve.wait_ge(x_in[k], i * 16 + 16)
                    for b in range(B):
                        last = nc.vector.tensor_scalar(rowx[:, k, b, :], xin[:, k, b, :], coef[:, b, 0:1],
                                                       coef[:, b, 1:2], ALU.mult, ALU.add)
                    last.then_inc(row_ready, 1)
                    dve.wait_ge(row_ready, i * 2 + (k + 1))
                    for r in range(ROWS):
                        t = i * (2 * ROWS) + (k * ROWS + r)
                        s = r % 2
                        cols = slice(r * W, (r + 1) * W)
                        for q in range(2):
                            bs = slice(q * HALF, (q + 1) * HALF)
                            dve.wait_ge(conv_done[q], t + 1)
                            nc.vector.scalar_tensor_tensor(
                                new[:, s, q, :, :], conv_ps[q][:, 0:HALF * W].rearrange("c (b w) -> c b w", b=HALF),
                                0.0, rowx[:, k, bs, cols], ALU.max, ALU.add).then_inc(new_ready[q], 1)
                            dve.wait_ge(new_ready[q], t + 1)
                            nc.vector.tensor_scalar(ch[:, q, :, PAD:PAD + W], new[:, s, q, :, :], SA / NEW_SCALE,
                                                    None, ALU.mult).then_inc(hi_ready[q], 1)
                            dve.wait_ge(hi_ready[q], t + 1)
                            nc.vector.scalar_tensor_tensor(
                                cl[:, q, :, PAD:PAD + W], new[:, s, q, :, :], SA / NEW_SCALE,
                                ch[:, q, :, PAD:PAD + W], ALU.mult, ALU.subtract).then_inc(carry_ready[q], 1)
                        if not (first and r < 2):
                            dve.wait_ge(turned, t - 1)
                        last = nc.vector.scalar_tensor_tensor(
                            fin[:, s, :, :], new[:, s, :, :, :].rearrange("c q b w -> c (q b) w"), 1.0 / NEW_SCALE,
                            xin[:, k, :, cols], ALU.mult, ALU.add)
                        last.then_inc(fin_ready, 1)
                    dve.wait_ge(fin_ready, i * (2 * ROWS) + (k + 1) * ROWS)
                    dve.sem_inc(x_used, 1)

                tile(0, 0, True)
                tile(0, 1, False)
                with dve.Fori(1, NT // 2) as i:
                    tile(i, 0, False)
                    tile(i, 1, False)

            @block.scalar
            def _(act):
                def rows4(i, first):
                    for r in range(4):
                        t = i * 4 + r
                        act.wait_ge(turned, t + 1)
                        if not first:
                            act.wait_ge(stored[r], i * 16)
                        nc.scalar.activation(ot[:, r, :, :].rearrange("w b c -> w (b c)"), tr_ps[r % 2][:, :],
                                             ACT.Copy).then_inc(turned_copied, 1)
                        act.wait_ge(turned_copied, t + 1)
                        act.dma_start(out_t[:, :, bass.ds(t, 1), :].rearrange("w b h c -> w (b h) c"), ot[:, r, :, :]).then_inc(stored[r], 16)

                rows4(0, True)
                with act.Fori(1, H // 4) as i:
                    rows4(i, False)
                for r in range(4):
                    act.wait_ge(stored[r], 16 * (H // 4))


def conv_preact_stack(nc, a, out):
    scratch = lambda name, shape, dt=F32: nc.dram_tensor(name, shape, dt, kind="Internal").ap()
    taps = scratch("taps", (PER, C, 2 * SUMS * PER), F16)
    coef0 = scratch("coef0", (NCG, QG * B * 2))
    hf = scratch("hf", (C, B * PLANE))
    x1, x2, x3 = (scratch(f"x{k}", (C, B * PLANE)) for k in (1, 2, 3))
    stats1, stats2, stats3 = (scratch(f"stats{k}", (C, B, TILES * 6)) for k in (1, 2, 3))
    l0, l1, l2 = (lambda s, p=p: a[f"{p}_conv_{s}"] for p in ("L0", "L1", "L2"))
    kept = Names(nc, "kept")
    with kept.stack:
        raw = kept.sb("raw", [C, KS * B, KS])
        gsum = kept.sb("gsum", [C, 1])
        ahead = Names(nc, "ahead")
        with ahead.stack:
            xg = ahead.sb("xg", [H, 2 * B, W, CG])
            x_in = [ahead.sem(f"x_in{b}") for b in range(B)]
            taps_stored = ahead.sem("taps_stored")
            stage_ahead(nc, a["x"], l0("B_kernel"), l0("gate_B_kernel"), l0("gate_A_kernel"), taps, xg, x_in,
                        taps_stored, raw, gsum)
            stage_depthwise(nc, a["x"], xg, x_in, taps, taps_stored, coef0, hf)
        stage_origin(nc, raw, gsum, l0("A_kernel"), coef0.rearrange("n (g b s) -> (n g) b s", g=QG, b=B), hf)
    stage_mix(nc, a["x"], hf, l0("W_out"), l0("b_out"), x1, stats1)
    stage_triangle(nc, x1, stats1, (l1("Wa1"), l1("Wa2")), (l1("ba1"), l1("ba2")), (l1("Wb1"), l1("Wb2")),
                   (l1("bb1"), l1("bb2")), l1("ln2_g"), l1("ln2_b"), l1("Wg"), l1("bg"), l1("Wz"), l1("bz"), x2, stats2)
    stage_lstm(nc, x2, stats2, [l2(f"W{g}x") for g in "ifoc"], [l2(f"W{g}m") for g in "ifoc"],
               [l2(f"b{g}") for g in "ifoc"], x3, stats3)
    stage_rowconv(nc, x3, stats3, a["L3_conv_W"], out)


def kernel(**inputs):
    import numpy as _np
    import concourse.bacc as _bacc
    from concourse import mybir as _mybir
    from concourse.bass_utils import run_bass_kernel_spmd as _run

    nc = _bacc.Bacc("TRN2", target_bir_lowering=False, num_devices=1)
    arrays, aps = {}, {}
    for name, value in inputs.items():
        array = _np.ascontiguousarray(value)
        arrays[f"in_{name}_dram"] = array
        aps[name] = nc.dram_tensor(f"in_{name}_dram", array.shape, _mybir.dt.from_np(array.dtype),
                                   kind="ExternalInput").ap()
    out = nc.dram_tensor("out_dram", (B, H, W, C), F32, kind="ExternalOutput").ap()
    conv_preact_stack(nc, aps, out)
    r = _run(nc, [arrays], core_ids=[0])
    return r.results[0]["out_dram"]
```
